# Optimizing a Trainium2 kernel written in Bass

```python
import numpy as np
import jax
import jax.numpy as jnp

def _softmax(x, axis=-1):
    return jax.nn.softmax(x, axis=axis)

def _gelu(x):
    return jax.nn.gelu(x, approximate=True)

def _silu(x):
    return jax.nn.silu(x)

def _sigmoid(x):
    return jax.nn.sigmoid(x)

def _layernorm(x, axis=-1, eps=1e-05):
    m = jnp.mean(x, axis=axis, keepdims=True)
    v = jnp.var(x, axis=axis, keepdims=True)
    return (x - m) / jnp.sqrt(v + eps)

def _scatter_add(tgt, idx, src, axis=0):
    return tgt.at[idx].add(src)

def _segment_sum(src, seg, n):
    return jax.ops.segment_sum(src, seg, n)
kernel_name = 'mk_decoder_preln_d4_seqx_r8_62ccdd'

def setup_inputs(seed: int=0):
    np.random.seed(seed)
    _w = jnp.asarray

    def _rec_inputs():
        import jax
        import jax.numpy as jnp
        _rk = jax.random.key(seed)
        x = -0.0002928 + 1 * jax.random.normal(jax.random.fold_in(_rk, 1), (32, 128, 128), jnp.float32)
        _lenS = 128 - jax.random.randint(jax.random.fold_in(_rk, 7), (32,), 0, max(1, 128 // 4) + 1, jnp.int32)
        _lenS2 = 77 - jax.random.randint(jax.random.fold_in(_rk, 8), (32,), 0, max(1, 77 // 4) + 1, jnp.int32)
        _ctx_1024P = jax.random.normal(jax.random.fold_in(_rk, 11), (32, 16, 128), jnp.float32)
        _ctx_1024c = jax.random.dirichlet(jax.random.fold_in(_rk, 511), 0.3 * jnp.ones((16,), jnp.float32), (32, 77))
        _ctx_1024t = jnp.einsum('bsk,bkd->bsd', _ctx_1024c, _ctx_1024P)
        _ctx_1024t = _ctx_1024t * jax.lax.rsqrt(jnp.mean(jnp.square(_ctx_1024t)) + 1e-12) * 0.953939
        ctx_1024 = 2.81802e-05 + 1.00001 * (_ctx_1024t + 0.3 * jax.random.normal(jax.random.fold_in(_rk, 611), (32, 77, 128), jnp.float32))
        _validS = jnp.arange(128)[None, :] < _lenS[:, None]
        _validS2 = jnp.arange(77)[None, :] < _lenS2[:, None]
        _causal = jnp.tril(jnp.ones((128, 128), dtype=bool))
        mask_BxS2_bk0 = jnp.logical_not(jnp.broadcast_to(_validS2[:, :], (32, 77)))
        return (x, ctx_1024, mask_BxS2_bk0)
    x, ctx_1024, mask_BxS2_bk0 = _rec_inputs()

    def _L0_attn_setup():
        import jax, jax.numpy as jnp
        import numpy as np
        B, S, D, H = (2, 256, 128, 16)
        HD = D // H
        key = jax.random.key(seed)
        ks = jax.random.split(key, 5)
        return {'x': jax.random.normal(ks[0], (B, S, D), dtype=jnp.float32), 'qkv_w': jax.random.normal(ks[1], (3 * D, D), dtype=jnp.float32) * (1.0 / np.sqrt(D)), 'qkv_b': jax.random.normal(ks[2], (3 * D,), dtype=jnp.float32) * 0.02, 'proj_w': jax.random.normal(ks[3], (D, D), dtype=jnp.float32) * (1.0 / np.sqrt(D)), 'proj_b': jax.random.normal(ks[4], (D,), dtype=jnp.float32) * 0.02}
    _L0_attn_all = _L0_attn_setup()
    _L0_attn_in = {k: v for k, v in _L0_attn_all.items() if k in ('qkv_w', 'qkv_b', 'proj_w', 'proj_b')}
    del _L0_attn_all

    def _L0_xattn_setup():
        import jax, jax.numpy as jnp
        import numpy as np
        NUM_HEADS, NUM_KV, HEAD_DIM, WIDTH = (4, 1, 32, 128)
        MASK_FILL = -2.3819763e+38

        def _apply_rope(x, positions, max_wavelength=10000.0):
            d = x.shape[-1]
            freq_exp = 2.0 / d * jnp.arange(d // 2, dtype=jnp.float32)
            timescale = max_wavelength ** freq_exp
            radians = positions[..., None].astype(jnp.float32) / timescale
            radians = radians[..., None, :]
            sin, cos = (jnp.sin(radians), jnp.cos(radians))
            x1, x2 = jnp.split(x, 2, axis=-1)
            out = jnp.concatenate([x1 * cos - x2 * sin, x2 * cos + x1 * sin], axis=-1)
            return out.astype(x.dtype)

        def _rmsnorm(x, scale):
            var = jnp.mean(jnp.square(x.astype(jnp.float32)), axis=-1, keepdims=True)
            normed = x * jax.lax.rsqrt(var + 1e-06)
            return (normed * (1 + scale)).astype(x.dtype)
        key = jax.random.key(seed)
        ks = jax.random.split(key, 7)
        B, T, S = (8, 64, 256)
        return {'x': jax.random.normal(ks[0], (B, T, WIDTH), jnp.float32), 'mem_seq': jax.random.normal(ks[1], (B, S, WIDTH), jnp.float32), 'mem_mask': jax.random.randint(ks[2], (B, S), 0, 2).astype(bool), 'rms_scale': jax.random.normal(ks[3], (WIDTH,), jnp.float32) * 0.02, 'q_w': jax.random.normal(ks[4], (NUM_HEADS, WIDTH, HEAD_DIM), jnp.float32) / np.sqrt(WIDTH), 'kv_w': jax.random.normal(ks[5], (2, NUM_KV, WIDTH, HEAD_DIM), jnp.float32) / np.sqrt(WIDTH), 'out_w': jax.random.normal(ks[6], (NUM_HEADS, HEAD_DIM, WIDTH), jnp.float32) / np.sqrt(NUM_HEADS * HEAD_DIM)}
    _L0_xattn_all = _L0_xattn_setup()
    _L0_xattn_in = {k: v for k, v in _L0_xattn_all.items() if k in ('rms_scale', 'q_w', 'kv_w', 'out_w')}
    del _L0_xattn_all

    def _L0_ffn_setup():
        import jax, jax.numpy as jnp
        import numpy as np
        QMAX = 127.0

        def _ste_round(v):
            return v + jax.lax.stop_gradient(jnp.round(v) - v)

        def _act_fake_quant(x, clip_factor):
            scale = jax.nn.sigmoid(clip_factor) * jnp.max(jnp.abs(x)) / QMAX
            return jnp.clip(_ste_round(x / scale), -QMAX - 1.0, QMAX) * scale

        def _weight_fake_quant(w):
            scale = jnp.max(jnp.abs(w), axis=1, keepdims=True) / QMAX
            return jnp.clip(_ste_round(w / scale), -QMAX - 1.0, QMAX) * scale
        key = jax.random.key(seed)
        k1, k2, k3, k4 = jax.random.split(key, 4)
        B, S, H, I = (8, 1024, 128, 352)
        return {'x': jax.random.normal(k1, (B, S, H), dtype=jnp.float32), 'clip_x': jnp.full((1,), 4.0, dtype=jnp.float32), 'clip_down': jnp.full((1,), 4.0, dtype=jnp.float32), 'w_gate': jax.random.normal(k2, (I, H), dtype=jnp.float32) * 0.02, 'w_up': jax.random.normal(k3, (I, H), dtype=jnp.float32) * 0.02, 'w_down': jax.random.normal(k4, (H, I), dtype=jnp.float32) * 0.02}
    _L0_ffn_all = _L0_ffn_setup()
    _L0_ffn_in = {k: v for k, v in _L0_ffn_all.items() if k in ('clip_x', 'clip_down', 'w_gate', 'w_up', 'w_down')}
    del _L0_ffn_all

    def _L1_attn_setup():
        import jax, jax.numpy as jnp
        import numpy as np
        import math
        E = 128
        B, T = (8, 256)
        key = jax.random.key(seed)
        ks = jax.random.split(key, 7)
        s = 1.0 / math.sqrt(E)
        return {'X': jax.random.normal(ks[0], (B, T, E), dtype=jnp.float32), 'Wq': jax.random.uniform(ks[1], (E, E), jnp.float32, -s, s), 'bq': jax.random.uniform(ks[2], (E,), jnp.float32, -s, s), 'Wk': jax.random.uniform(ks[3], (E, E), jnp.float32, -s, s), 'bk': jax.random.uniform(ks[4], (E,), jnp.float32, -s, s), 'Wv': jax.random.uniform(ks[5], (E, E), jnp.float32, -s, s), 'bv': jax.random.uniform(ks[6], (E,), jnp.float32, -s, s)}
    _L1_attn_all = _L1_attn_setup()
    _L1_attn_in = {k: v for k, v in _L1_attn_all.items() if k in ('Wq', 'bq', 'Wk', 'bk', 'Wv', 'bv')}
    del _L1_attn_all

    def _L1_xattn_setup():
        import jax, jax.numpy as jnp
        import numpy as np
        DIM = 128
        HEADS = 16
        DIM_HEAD = 64
        INNER = HEADS * DIM_HEAD
        EPS = 1e-05

        def _layernorm(t, w, b):
            mu = jnp.mean(t, axis=-1, keepdims=True)
            var = jnp.mean(jnp.square(t - mu), axis=-1, keepdims=True)
            return (t - mu) * jax.lax.rsqrt(var + EPS) * w + b
        key = jax.random.key(seed)
        ks = jax.random.split(key, 8)
        b, n, l = (8, 512, 64)
        x = jax.random.normal(ks[0], (b, n, DIM), dtype=jnp.float32)
        latents = jax.random.normal(ks[1], (b, l, DIM), dtype=jnp.float32)
        ln1_w = jnp.ones((DIM,), jnp.float32)
        ln1_b = jnp.zeros((DIM,), jnp.float32)
        ln2_w = jnp.ones((DIM,), jnp.float32)
        ln2_b = jnp.zeros((DIM,), jnp.float32)
        Wq = jax.random.normal(ks[2], (DIM, INNER), dtype=jnp.float32) / np.sqrt(DIM)
        Wkv = jax.random.normal(ks[3], (DIM, 2 * INNER), dtype=jnp.float32) / np.sqrt(DIM)
        Wo = jax.random.normal(ks[4], (INNER, DIM), dtype=jnp.float32) / np.sqrt(INNER)
        return {'x': x, 'latents': latents, 'ln1_w': ln1_w, 'ln1_b': ln1_b, 'ln2_w': ln2_w, 'ln2_b': ln2_b, 'Wq': Wq, 'Wkv': Wkv, 'Wo': Wo}
    _L1_xattn_all = _L1_xattn_setup()
    _L1_xattn_in = {k: v for k, v in _L1_xattn_all.items() if k in ('ln1_w', 'ln1_b', 'ln2_w', 'ln2_b', 'Wq', 'Wkv', 'Wo')}
    del _L1_xattn_all

    def _L1_ffn_setup():
        import jax, jax.numpy as jnp
        import numpy as np
        S, B, D, H, DH = (512, 8, 128, 16, 64)

        def _forward(x, Wg, Wq, bq, Wkv, bkv, Wo, bo, ln_g, ln_b):
            s_len, bsz, d_model = x.shape
            n_head, _, d_head = Wq.shape
            cap = s_len // n_head
            scale = 1.0 / d_head ** 0.5
            h = jnp.transpose(x, (1, 0, 2))
            t = h
            probs = jax.nn.softmax(h @ Wg, axis=-1)
            scores = jnp.transpose(probs, (0, 2, 1))
            _, idx = jax.lax.top_k(scores, cap)
            idx = jnp.sort(idx, axis=-1)
            hg = jnp.take_along_axis(h[:, None, :, :], idx[..., None], axis=2)
            hg = jnp.transpose(hg, (1, 0, 2, 3))
            q = jnp.einsum('hbcd,hde->hbce', hg, Wq) + bq[:, None, None, :]
            kv = jnp.einsum('hbcd,hde->hbce', hg, Wkv) + bkv[:, None, None, :]
            k, v = jnp.split(kv, 2, axis=-1)
            att = jnp.einsum('hbid,hbjd->hbij', q, k) * scale
            p = jax.nn.softmax(att, axis=1)
            av = jnp.einsum('hbij,hbjd->hbid', p, v)
            ao = jnp.einsum('hbid,hde->hbie', av, Wo) + bo
            tok = jnp.transpose(idx, (1, 0, 2))
            b_ids = jnp.arange(bsz)[None, :, None]
            outs = jnp.zeros_like(t).at[b_ids, tok].add(ao)
            y = t + outs
            mu = jnp.mean(y, axis=-1, keepdims=True)
            var = jnp.var(y, axis=-1, keepdims=True)
            yn = (y - mu) * jax.lax.rsqrt(var + 1e-05) * ln_g + ln_b
            return jnp.transpose(yn, (1, 0, 2))
        key = jax.random.key(seed)
        ks = jax.random.split(key, 6)
        s = 0.02
        return {'x': jax.random.normal(ks[0], (S, B, D), jnp.float32), 'attn_mask': jnp.zeros((S, S), jnp.bool_), 'Wg': jax.random.normal(ks[1], (D, H), jnp.float32) * s, 'Wq': jax.random.normal(ks[2], (H, D, DH), jnp.float32) * s, 'bq': jnp.zeros((H, DH), jnp.float32), 'Wkv': jax.random.normal(ks[3], (H, D, 2 * DH), jnp.float32) * s, 'bkv': jnp.zeros((H, 2 * DH), jnp.float32), 'Wo': jax.random.normal(ks[4], (H, DH, D), jnp.float32) * s, 'bo': jnp.zeros((D,), jnp.float32), 'ln_g': jnp.ones((D,), jnp.float32), 'ln_b': jnp.zeros((D,), jnp.float32)}
    _L1_ffn_all = _L1_ffn_setup()
    _L1_ffn_in = {k: v for k, v in _L1_ffn_all.items() if k in ('attn_mask', 'Wg', 'Wq', 'bq', 'Wkv', 'bkv', 'Wo', 'bo', 'ln_g', 'ln_b')}
    del _L1_ffn_all

    def _L2_attn_setup():
        import jax, jax.numpy as jnp
        import numpy as np
        B, N, D_IN, D_OUT, HEADS = (4, 512, 128, 128, 16)
        D_HEAD = D_OUT // HEADS
        key = jax.random.key(seed)
        ks = jax.random.split(key, 5)
        x = jax.random.normal(ks[0], (B, N, D_IN), dtype=jnp.float32)
        s_in = 1.0 / np.sqrt(D_IN)
        s_out = 1.0 / np.sqrt(D_OUT)
        Wq = jax.random.normal(ks[1], (D_IN, D_OUT), dtype=jnp.float32) * s_in
        Wk = jax.random.normal(ks[2], (D_IN, D_OUT), dtype=jnp.float32) * s_in
        Wv = jax.random.normal(ks[3], (D_IN, D_OUT), dtype=jnp.float32) * s_in
        Wo = jax.random.normal(ks[4], (D_OUT, D_OUT), dtype=jnp.float32) * s_out
        bo = jnp.zeros((D_OUT,), dtype=jnp.float32)
        return {'x': x, 'Wq': Wq, 'Wk': Wk, 'Wv': Wv, 'Wo': Wo, 'bo': bo}
    _L2_attn_all = _L2_attn_setup()
    _L2_attn_in = {k: v for k, v in _L2_attn_all.items() if k in ('Wq', 'Wk', 'Wv', 'Wo', 'bo')}
    del _L2_attn_all

    def _L2_xattn_setup():
        import jax, jax.numpy as jnp
        import numpy as np
        HEADS = 8
        DIM_HEAD = 64
        SCALE = 8.0
        EPS = 1e-05

        def layer_norm(x, g, b):
            mu = jnp.mean(x, axis=-1, keepdims=True)
            var = jnp.mean((x - mu) ** 2, axis=-1, keepdims=True)
            return (x - mu) * jax.lax.rsqrt(var + EPS) * g + b
        key = jax.random.key(seed)
        ks = jax.random.split(key, 6)
        b, n, dim = (4, 512, 128)
        inner = HEADS * DIM_HEAD
        return {'x': jax.random.normal(ks[0], (b, n, dim), jnp.float32), 'context': jax.random.normal(ks[1], (b, n, dim), jnp.float32), 'Wq': jax.random.normal(ks[2], (dim, inner), jnp.float32) * 0.03, 'Wkv': jax.random.normal(ks[3], (dim, 2 * inner), jnp.float32) * 0.03, 'null_kv': jax.random.normal(ks[4], (2, DIM_HEAD), jnp.float32), 'ln_q_g': jnp.ones((inner,), jnp.float32), 'ln_q_b': jnp.zeros((inner,), jnp.float32), 'ln_out_g': jnp.ones((inner,), jnp.float32), 'ln_out_b': jnp.zeros((inner,), jnp.float32), 'Wout': jax.random.normal(ks[5], (inner, dim), jnp.float32) * 0.03}
    _L2_xattn_all = _L2_xattn_setup()
    _L2_xattn_in = {k: v for k, v in _L2_xattn_all.items() if k in ('Wq', 'Wkv', 'null_kv', 'ln_q_g', 'ln_q_b', 'ln_out_g', 'ln_out_b', 'Wout')}
    del _L2_xattn_all

    def _L2_ffn_setup():
        import jax, jax.numpy as jnp
        import numpy as np
        B, S, H = (2, 256, 128)
        E_ROUTED = 8
        TOP_K = 2
        I = 256
        key = jax.random.key(seed)
        ks = jax.random.split(key, 9)
        s = 0.02
        return {'x': jax.random.normal(ks[0], (B, S, H), dtype=jnp.float32), 'shared_gate': jax.random.normal(ks[1], (I, H), dtype=jnp.float32) * s, 'shared_up': jax.random.normal(ks[2], (I, H), dtype=jnp.float32) * s, 'shared_down': jax.random.normal(ks[3], (H, I), dtype=jnp.float32) * s, 'gate_w': jax.random.normal(ks[4], (E_ROUTED, H, I), dtype=jnp.float32) * s, 'up_w': jax.random.normal(ks[5], (E_ROUTED, H, I), dtype=jnp.float32) * s, 'down_w': jax.random.normal(ks[6], (E_ROUTED, I, H), dtype=jnp.float32) * s, 'router_w': jax.random.normal(ks[7], (E_ROUTED, H), dtype=jnp.float32) * s, 'routing_bias': jnp.zeros((E_ROUTED,), dtype=jnp.float32)}
    _L2_ffn_all = _L2_ffn_setup()
    _L2_ffn_in = {k: v for k, v in _L2_ffn_all.items() if k in ('shared_gate', 'shared_up', 'shared_down', 'gate_w', 'up_w', 'down_w', 'router_w', 'routing_bias')}
    del _L2_ffn_all

    def _L3_attn_setup():
        import jax, jax.numpy as jnp
        import numpy as np
        import math
        D_MODEL, N_HEADS, D_K, D_C, D_HR = (128, 8, 128, 32, 32)
        B, S = (4, 256)
        key = jax.random.key(seed)
        ks = jax.random.split(key, 17)

        def lin(k, fan_in, fan_out):
            lim = 1.0 / math.sqrt(fan_in)
            kw, kb = jax.random.split(k)
            W = jax.random.uniform(kw, (fan_in, fan_out), jnp.float32, -lim, lim)
            b = jax.random.uniform(kb, (fan_out,), jnp.float32, -lim, lim)
            return (W, b)
        W_DQ, b_DQ = lin(ks[0], D_MODEL, D_C)
        W_UQ, b_UQ = lin(ks[1], D_C, N_HEADS * D_K)
        W_DKV, b_DKV = lin(ks[2], D_MODEL, D_C)
        W_UK, b_UK = lin(ks[3], D_C, N_HEADS * D_K)
        W_UV, b_UV = lin(ks[4], D_C, N_HEADS * D_K)
        W_QR, b_QR = lin(ks[5], D_C, N_HEADS * D_HR)
        W_KR, b_KR = lin(ks[6], D_MODEL, D_HR)
        W_O, b_O = lin(ks[7], N_HEADS * D_K, D_MODEL)
        h_t = jax.random.normal(ks[8], (B, S, D_MODEL), jnp.float32)
        return {'h_t': h_t, 'W_DQ': W_DQ, 'b_DQ': b_DQ, 'W_UQ': W_UQ, 'b_UQ': b_UQ, 'W_DKV': W_DKV, 'b_DKV': b_DKV, 'W_UK': W_UK, 'b_UK': b_UK, 'W_UV': W_UV, 'b_UV': b_UV, 'W_QR': W_QR, 'b_QR': b_QR, 'W_KR': W_KR, 'b_KR': b_KR, 'W_O': W_O, 'b_O': b_O}
    _L3_attn_all = _L3_attn_setup()
    _L3_attn_in = {k: v for k, v in _L3_attn_all.items() if k in ('W_DQ', 'b_DQ', 'W_UQ', 'b_UQ', 'W_DKV', 'b_DKV', 'W_UK', 'b_UK', 'W_UV', 'b_UV', 'W_QR', 'b_QR', 'W_KR', 'b_KR', 'W_O', 'b_O')}
    del _L3_attn_all

    def _L3_xattn_setup():
        import jax, jax.numpy as jnp
        import numpy as np
        EMBED = 128
        HEADS = 16
        HEAD_DIM = EMBED // HEADS
        key = jax.random.key(seed)
        kv, kk, kq, kwv, kwk, kwq, kwo, kbo = jax.random.split(key, 8)
        B, Lq, Lk = (4, 256, 256)
        inp = {'values': jax.random.normal(kv, (B, Lk, EMBED), dtype=jnp.float32), 'keys': jax.random.normal(kk, (B, Lk, EMBED), dtype=jnp.float32), 'queries': jax.random.normal(kq, (B, Lq, EMBED), dtype=jnp.float32), 'Wv': jax.random.normal(kwv, (HEAD_DIM, HEAD_DIM), dtype=jnp.float32) / np.sqrt(HEAD_DIM), 'Wk': jax.random.normal(kwk, (HEAD_DIM, HEAD_DIM), dtype=jnp.float32) / np.sqrt(HEAD_DIM), 'Wq': jax.random.normal(kwq, (HEAD_DIM, HEAD_DIM), dtype=jnp.float32) / np.sqrt(HEAD_DIM), 'Wo': jax.random.normal(kwo, (EMBED, EMBED), dtype=jnp.float32) / np.sqrt(EMBED), 'bo': jax.random.normal(kbo, (EMBED,), dtype=jnp.float32) * 0.01}
        return inp
    _L3_xattn_all = _L3_xattn_setup()
    _L3_xattn_in = {k: v for k, v in _L3_xattn_all.items() if k in ('Wv', 'Wk', 'Wq', 'Wo', 'bo')}
    del _L3_xattn_all

    def _L3_ffn_setup():
        import jax, jax.numpy as jnp
        import numpy as np
        TOP_K = 2
        key = jax.random.key(seed)
        k0, k1, k2, k3, k4 = jax.random.split(key, 5)
        B, S, D, H, E = (4, 256, 128, 256, 8)
        x = jax.random.normal(k0, (B, S, D), dtype=jnp.float32)
        router_w = jax.random.normal(k1, (E, D), dtype=jnp.float32) * D ** (-0.5)
        w_gate = jax.random.normal(k2, (E, D, H), dtype=jnp.float32) * D ** (-0.5)
        w_up = jax.random.normal(k3, (E, D, H), dtype=jnp.float32) * D ** (-0.5)
        w_down = jax.random.normal(k4, (E, H, D), dtype=jnp.float32) * H ** (-0.5)
        return {'x': x, 'router_w': router_w, 'w_gate': w_gate, 'w_up': w_up, 'w_down': w_down}
    _L3_ffn_all = _L3_ffn_setup()
    _L3_ffn_in = {k: v for k, v in _L3_ffn_all.items() if k in ('router_w', 'w_gate', 'w_up', 'w_down')}
    del _L3_ffn_all
    return {'x': x, 'ctx_1024': ctx_1024, 'mask_BxS2_bk0': mask_BxS2_bk0, 'L0_attn_qkv_w': _L0_attn_in['qkv_w'], 'L0_attn_qkv_b': _L0_attn_in['qkv_b'], 'L0_attn_proj_w': _L0_attn_in['proj_w'], 'L0_attn_proj_b': _L0_attn_in['proj_b'], 'L0_xattn_rms_scale': _L0_xattn_in['rms_scale'], 'L0_xattn_q_w': _L0_xattn_in['q_w'], 'L0_xattn_kv_w': _L0_xattn_in['kv_w'], 'L0_xattn_out_w': _L0_xattn_in['out_w'], 'L0_ffn_clip_x': _L0_ffn_in['clip_x'], 'L0_ffn_clip_down': _L0_ffn_in['clip_down'], 'L0_ffn_w_gate': _L0_ffn_in['w_gate'], 'L0_ffn_w_up': _L0_ffn_in['w_up'], 'L0_ffn_w_down': _L0_ffn_in['w_down'], 'L1_attn_Wq': _L1_attn_in['Wq'], 'L1_attn_bq': _L1_attn_in['bq'], 'L1_attn_Wk': _L1_attn_in['Wk'], 'L1_attn_bk': _L1_attn_in['bk'], 'L1_attn_Wv': _L1_attn_in['Wv'], 'L1_attn_bv': _L1_attn_in['bv'], 'L1_xattn_ln1_w': _L1_xattn_in['ln1_w'], 'L1_xattn_ln1_b': _L1_xattn_in['ln1_b'], 'L1_xattn_ln2_w': _L1_xattn_in['ln2_w'], 'L1_xattn_ln2_b': _L1_xattn_in['ln2_b'], 'L1_xattn_Wq': _L1_xattn_in['Wq'], 'L1_xattn_Wkv': _L1_xattn_in['Wkv'], 'L1_xattn_Wo': _L1_xattn_in['Wo'], 'L1_ffn_attn_mask': _L1_ffn_in['attn_mask'], 'L1_ffn_Wg': _L1_ffn_in['Wg'], 'L1_ffn_Wq': _L1_ffn_in['Wq'], 'L1_ffn_bq': _L1_ffn_in['bq'], 'L1_ffn_Wkv': _L1_ffn_in['Wkv'], 'L1_ffn_bkv': _L1_ffn_in['bkv'], 'L1_ffn_Wo': _L1_ffn_in['Wo'], 'L1_ffn_bo': _L1_ffn_in['bo'], 'L1_ffn_ln_g': _L1_ffn_in['ln_g'], 'L1_ffn_ln_b': _L1_ffn_in['ln_b'], 'L2_attn_Wq': _L2_attn_in['Wq'], 'L2_attn_Wk': _L2_attn_in['Wk'], 'L2_attn_Wv': _L2_attn_in['Wv'], 'L2_attn_Wo': _L2_attn_in['Wo'], 'L2_attn_bo': _L2_attn_in['bo'], 'L2_xattn_Wq': _L2_xattn_in['Wq'], 'L2_xattn_Wkv': _L2_xattn_in['Wkv'], 'L2_xattn_null_kv': _L2_xattn_in['null_kv'], 'L2_xattn_ln_q_g': _L2_xattn_in['ln_q_g'], 'L2_xattn_ln_q_b': _L2_xattn_in['ln_q_b'], 'L2_xattn_ln_out_g': _L2_xattn_in['ln_out_g'], 'L2_xattn_ln_out_b': _L2_xattn_in['ln_out_b'], 'L2_xattn_Wout': _L2_xattn_in['Wout'], 'L2_ffn_shared_gate': _L2_ffn_in['shared_gate'], 'L2_ffn_shared_up': _L2_ffn_in['shared_up'], 'L2_ffn_shared_down': _L2_ffn_in['shared_down'], 'L2_ffn_gate_w': _L2_ffn_in['gate_w'], 'L2_ffn_up_w': _L2_ffn_in['up_w'], 'L2_ffn_down_w': _L2_ffn_in['down_w'], 'L2_ffn_router_w': _L2_ffn_in['router_w'], 'L2_ffn_routing_bias': _L2_ffn_in['routing_bias'], 'L3_attn_W_DQ': _L3_attn_in['W_DQ'], 'L3_attn_b_DQ': _L3_attn_in['b_DQ'], 'L3_attn_W_UQ': _L3_attn_in['W_UQ'], 'L3_attn_b_UQ': _L3_attn_in['b_UQ'], 'L3_attn_W_DKV': _L3_attn_in['W_DKV'], 'L3_attn_b_DKV': _L3_attn_in['b_DKV'], 'L3_attn_W_UK': _L3_attn_in['W_UK'], 'L3_attn_b_UK': _L3_attn_in['b_UK'], 'L3_attn_W_UV': _L3_attn_in['W_UV'], 'L3_attn_b_UV': _L3_attn_in['b_UV'], 'L3_attn_W_QR': _L3_attn_in['W_QR'], 'L3_attn_b_QR': _L3_attn_in['b_QR'], 'L3_attn_W_KR': _L3_attn_in['W_KR'], 'L3_attn_b_KR': _L3_attn_in['b_KR'], 'L3_attn_W_O': _L3_attn_in['W_O'], 'L3_attn_b_O': _L3_attn_in['b_O'], 'L3_xattn_Wv': _L3_xattn_in['Wv'], 'L3_xattn_Wk': _L3_xattn_in['Wk'], 'L3_xattn_Wq': _L3_xattn_in['Wq'], 'L3_xattn_Wo': _L3_xattn_in['Wo'], 'L3_xattn_bo': _L3_xattn_in['bo'], 'L3_ffn_router_w': _L3_ffn_in['router_w'], 'L3_ffn_w_gate': _L3_ffn_in['w_gate'], 'L3_ffn_w_up': _L3_ffn_in['w_up'], 'L3_ffn_w_down': _L3_ffn_in['w_down']}

def reference(x, ctx_1024, mask_BxS2_bk0, L0_attn_qkv_w, L0_attn_qkv_b, L0_attn_proj_w, L0_attn_proj_b, L0_xattn_rms_scale, L0_xattn_q_w, L0_xattn_kv_w, L0_xattn_out_w, L0_ffn_clip_x, L0_ffn_clip_down, L0_ffn_w_gate, L0_ffn_w_up, L0_ffn_w_down, L1_attn_Wq, L1_attn_bq, L1_attn_Wk, L1_attn_bk, L1_attn_Wv, L1_attn_bv, L1_xattn_ln1_w, L1_xattn_ln1_b, L1_xattn_ln2_w, L1_xattn_ln2_b, L1_xattn_Wq, L1_xattn_Wkv, L1_xattn_Wo, L1_ffn_attn_mask, L1_ffn_Wg, L1_ffn_Wq, L1_ffn_bq, L1_ffn_Wkv, L1_ffn_bkv, L1_ffn_Wo, L1_ffn_bo, L1_ffn_ln_g, L1_ffn_ln_b, L2_attn_Wq, L2_attn_Wk, L2_attn_Wv, L2_attn_Wo, L2_attn_bo, L2_xattn_Wq, L2_xattn_Wkv, L2_xattn_null_kv, L2_xattn_ln_q_g, L2_xattn_ln_q_b, L2_xattn_ln_out_g, L2_xattn_ln_out_b, L2_xattn_Wout, L2_ffn_shared_gate, L2_ffn_shared_up, L2_ffn_shared_down, L2_ffn_gate_w, L2_ffn_up_w, L2_ffn_down_w, L2_ffn_router_w, L2_ffn_routing_bias, L3_attn_W_DQ, L3_attn_b_DQ, L3_attn_W_UQ, L3_attn_b_UQ, L3_attn_W_DKV, L3_attn_b_DKV, L3_attn_W_UK, L3_attn_b_UK, L3_attn_W_UV, L3_attn_b_UV, L3_attn_W_QR, L3_attn_b_QR, L3_attn_W_KR, L3_attn_b_KR, L3_attn_W_O, L3_attn_b_O, L3_xattn_Wv, L3_xattn_Wk, L3_xattn_Wq, L3_xattn_Wo, L3_xattn_bo, L3_ffn_router_w, L3_ffn_w_gate, L3_ffn_w_up, L3_ffn_w_down):
    import jax
    import jax.numpy as jnp

    def _L0_attn_ref(x, qkv_w, qkv_b, proj_w, proj_b):
        import jax, jax.numpy as jnp
        import numpy as np
        B, S, D, H = (2, 256, 128, 16)
        HD = D // H
        b, s, d = x.shape
        qkv = jnp.einsum('bsd,ed->bse', x, qkv_w) + qkv_b
        qkv = qkv.reshape(b, s, 3, H, HD)
        q = jnp.transpose(qkv[:, :, 0], (0, 2, 1, 3))
        k = jnp.transpose(qkv[:, :, 1], (0, 2, 1, 3))
        v = jnp.transpose(qkv[:, :, 2], (0, 2, 1, 3))
        scale = 1.0 / jnp.sqrt(jnp.asarray(HD, dtype=x.dtype))
        scores = jnp.einsum('bhqe,bhke->bhqk', q, k) * scale
        attn = jax.nn.softmax(scores, axis=-1)
        out = jnp.einsum('bhqk,bhke->bhqe', attn, v)
        out = jnp.transpose(out, (0, 2, 1, 3)).reshape(b, s, d)
        out = jnp.einsum('bsd,ed->bse', out, proj_w) + proj_b
        return out

    def _L0_xattn_ref(x, mem_seq, mem_mask, rms_scale, q_w, kv_w, out_w):
        import jax, jax.numpy as jnp
        import numpy as np
        NUM_HEADS, NUM_KV, HEAD_DIM, WIDTH = (4, 1, 32, 128)
        MASK_FILL = -2.3819763e+38

        def _apply_rope(x, positions, max_wavelength=10000.0):
            d = x.shape[-1]
            freq_exp = 2.0 / d * jnp.arange(d // 2, dtype=jnp.float32)
            timescale = max_wavelength ** freq_exp
            radians = positions[..., None].astype(jnp.float32) / timescale
            radians = radians[..., None, :]
            sin, cos = (jnp.sin(radians), jnp.cos(radians))
            x1, x2 = jnp.split(x, 2, axis=-1)
            out = jnp.concatenate([x1 * cos - x2 * sin, x2 * cos + x1 * sin], axis=-1)
            return out.astype(x.dtype)

        def _rmsnorm(x, scale):
            var = jnp.mean(jnp.square(x.astype(jnp.float32)), axis=-1, keepdims=True)
            normed = x * jax.lax.rsqrt(var + 1e-06)
            return (normed * (1 + scale)).astype(x.dtype)
        B, S, _ = mem_seq.shape
        T = x.shape[1]
        G = NUM_HEADS // NUM_KV
        xn = _rmsnorm(x, rms_scale)
        mn = _rmsnorm(mem_seq, rms_scale)
        q = jnp.einsum('BTD,NDH->BTNH', xn, q_w)
        kv = jnp.einsum('BSD,cKDH->cBSKH', mn, kv_w)
        k, v = (kv[0], kv[1])
        q_pos = jnp.broadcast_to(jnp.arange(S, T + S), (B, T))
        k_pos = jnp.broadcast_to(jnp.arange(S), (B, S))
        q = _apply_rope(q, q_pos) * HEAD_DIM ** (-0.5)
        k = _apply_rope(k, k_pos)
        q = q.reshape(B, T, NUM_KV, G, HEAD_DIM)
        logits = jnp.einsum('BTKGH,BSKH->BKGTS', q, k, preferred_element_type=jnp.float32)
        masked = jnp.where(mem_mask[:, None, None, None, :], logits, MASK_FILL)
        probs = jax.nn.softmax(masked, axis=-1).astype(x.dtype)
        enc = jnp.einsum('BKGTS,BSKH->BTKGH', probs, v).reshape(B, T, NUM_HEADS, HEAD_DIM)
        return jnp.einsum('BTNH,NHD->BTD', enc, out_w)

    def _L0_ffn_ref(x, clip_x, clip_down, w_gate, w_up, w_down):
        import jax, jax.numpy as jnp
        import numpy as np
        QMAX = 127.0

        def _ste_round(v):
            return v + jax.lax.stop_gradient(jnp.round(v) - v)

        def _act_fake_quant(x, clip_factor):
            scale = jax.nn.sigmoid(clip_factor) * jnp.max(jnp.abs(x)) / QMAX
            return jnp.clip(_ste_round(x / scale), -QMAX - 1.0, QMAX) * scale

        def _weight_fake_quant(w):
            scale = jnp.max(jnp.abs(w), axis=1, keepdims=True) / QMAX
            return jnp.clip(_ste_round(w / scale), -QMAX - 1.0, QMAX) * scale
        xq = _act_fake_quant(x, clip_x[0])
        gate = jnp.einsum('bsh,ih->bsi', xq, _weight_fake_quant(w_gate))
        up = jnp.einsum('bsh,ih->bsi', xq, _weight_fake_quant(w_up))
        h = _act_fake_quant(jax.nn.silu(gate) * up, clip_down[0])
        return jnp.einsum('bsi,hi->bsh', h, _weight_fake_quant(w_down))

    def _L1_attn_ref(X, Wq, bq, Wk, bk, Wv, bv):
        import jax, jax.numpy as jnp
        import numpy as np
        import math
        E = 128
        B, T = (8, 256)
        q = jnp.einsum('bte,fe->btf', X, Wq) + bq
        k = jnp.einsum('bte,fe->btf', X, Wk) + bk
        v = jnp.einsum('bte,fe->btf', X, Wv) + bv
        scores = jnp.einsum('bie,bje->bij', q, k) / math.sqrt(E)
        i = jnp.arange(scores.shape[-2])[:, None]
        j = jnp.arange(scores.shape[-1])[None, :]
        scores = jnp.where(j > i, -jnp.inf, scores)
        attn = jax.nn.softmax(scores, axis=-2)
        return jnp.einsum('bij,bje->bie', attn, v)

    def _L1_xattn_ref(x, latents, ln1_w, ln1_b, ln2_w, ln2_b, Wq, Wkv, Wo):
        import jax, jax.numpy as jnp
        import numpy as np
        DIM = 128
        HEADS = 16
        DIM_HEAD = 64
        INNER = HEADS * DIM_HEAD
        EPS = 1e-05

        def _layernorm(t, w, b):
            mu = jnp.mean(t, axis=-1, keepdims=True)
            var = jnp.mean(jnp.square(t - mu), axis=-1, keepdims=True)
            return (t - mu) * jax.lax.rsqrt(var + EPS) * w + b
        xn = _layernorm(x, ln1_w, ln1_b)
        latn = _layernorm(latents, ln2_w, ln2_b)
        b, l, _ = latn.shape
        q = latn @ Wq
        kv_input = jnp.concatenate([xn, latn], axis=1)
        kv = kv_input @ Wkv
        k, v = jnp.split(kv, 2, axis=-1)

        def heads(t):
            return t.reshape(t.shape[0], t.shape[1], HEADS, DIM_HEAD).transpose(0, 2, 1, 3)
        q, k, v = (heads(q), heads(k), heads(v))
        scale = 1.0 / np.sqrt(np.sqrt(DIM_HEAD))
        weight = jnp.einsum('bhld,bhnd->bhln', q * scale, k * scale)
        weight = jax.nn.softmax(weight.astype(jnp.float32), axis=-1).astype(weight.dtype)
        out = jnp.einsum('bhln,bhnd->bhld', weight, v)
        out = out.transpose(0, 2, 1, 3).reshape(b, l, INNER)
        return out @ Wo

    def _L1_ffn_ref(x, attn_mask, Wg, Wq, bq, Wkv, bkv, Wo, bo, ln_g, ln_b):
        import jax, jax.numpy as jnp
        import numpy as np
        S, B, D, H, DH = (512, 8, 128, 16, 64)

        def _forward(x, Wg, Wq, bq, Wkv, bkv, Wo, bo, ln_g, ln_b):
            s_len, bsz, d_model = x.shape
            n_head, _, d_head = Wq.shape
            cap = s_len // n_head
            scale = 1.0 / d_head ** 0.5
            h = jnp.transpose(x, (1, 0, 2))
            t = h
            probs = jax.nn.softmax(h @ Wg, axis=-1)
            scores = jnp.transpose(probs, (0, 2, 1))
            _, idx = jax.lax.top_k(scores, cap)
            idx = jnp.sort(idx, axis=-1)
            hg = jnp.take_along_axis(h[:, None, :, :], idx[..., None], axis=2)
            hg = jnp.transpose(hg, (1, 0, 2, 3))
            q = jnp.einsum('hbcd,hde->hbce', hg, Wq) + bq[:, None, None, :]
            kv = jnp.einsum('hbcd,hde->hbce', hg, Wkv) + bkv[:, None, None, :]
            k, v = jnp.split(kv, 2, axis=-1)
            att = jnp.einsum('hbid,hbjd->hbij', q, k) * scale
            p = jax.nn.softmax(att, axis=1)
            av = jnp.einsum('hbij,hbjd->hbid', p, v)
            ao = jnp.einsum('hbid,hde->hbie', av, Wo) + bo
            tok = jnp.transpose(idx, (1, 0, 2))
            b_ids = jnp.arange(bsz)[None, :, None]
            outs = jnp.zeros_like(t).at[b_ids, tok].add(ao)
            y = t + outs
            mu = jnp.mean(y, axis=-1, keepdims=True)
            var = jnp.var(y, axis=-1, keepdims=True)
            yn = (y - mu) * jax.lax.rsqrt(var + 1e-05) * ln_g + ln_b
            return jnp.transpose(yn, (1, 0, 2))
        return _forward(x, Wg, Wq, bq, Wkv, bkv, Wo, bo, ln_g, ln_b)

    def _L2_attn_ref(x, Wq, Wk, Wv, Wo, bo):
        import jax, jax.numpy as jnp
        import numpy as np
        B, N, D_IN, D_OUT, HEADS = (4, 512, 128, 128, 16)
        D_HEAD = D_OUT // HEADS
        q = jax.nn.softmax(jnp.einsum('bni,io->bno', x, Wq), axis=-1)
        k = jax.nn.softmax(jnp.einsum('bni,io->bno', x, Wk), axis=-2)
        v = jnp.einsum('bni,io->bno', x, Wv)
        scale = 1.0 / np.sqrt(D_HEAD).astype(np.float32)
        ctx = jnp.einsum('bnd,bne->bde', k, v) * scale
        y = jnp.einsum('bnd,bde->bne', q, ctx) / jnp.float32(D_OUT)
        return jnp.einsum('bnd,de->bne', y, Wo) + bo

    def _L2_xattn_ref(x, context, Wq, Wkv, null_kv, ln_q_g, ln_q_b, ln_out_g, ln_out_b, Wout):
        import jax, jax.numpy as jnp
        import numpy as np
        HEADS = 8
        DIM_HEAD = 64
        SCALE = 8.0
        EPS = 1e-05

        def layer_norm(x, g, b):
            mu = jnp.mean(x, axis=-1, keepdims=True)
            var = jnp.mean((x - mu) ** 2, axis=-1, keepdims=True)
            return (x - mu) * jax.lax.rsqrt(var + EPS) * g + b
        b, n, _ = x.shape
        m = context.shape[1]
        h, d = (HEADS, DIM_HEAD)
        q = x @ Wq
        kv = context @ Wkv
        k, v = jnp.split(kv, 2, axis=-1)
        q = layer_norm(q, ln_q_g, ln_q_b)
        split = lambda t: t.reshape(t.shape[0], t.shape[1], h, d).transpose(0, 2, 1, 3)
        q, k, v = (split(q), split(k), split(v))
        nk = jnp.broadcast_to(null_kv[0], (b, h, 1, d))
        nv = jnp.broadcast_to(null_kv[1], (b, h, 1, d))
        k = jnp.concatenate([nk, k], axis=2)
        v = jnp.concatenate([nv, v], axis=2)
        q = jax.nn.softmax(q, axis=-1) * SCALE
        k = jax.nn.softmax(k, axis=2)
        ctx = jnp.einsum('bhnd,bhne->bhde', k, v)
        out = jnp.einsum('bhnd,bhde->bhne', q, ctx)
        out = out.transpose(0, 2, 1, 3).reshape(b, n, h * d)
        out = layer_norm(out, ln_out_g, ln_out_b)
        return out @ Wout

    def _L2_ffn_ref(x, shared_gate, shared_up, shared_down, gate_w, up_w, down_w, router_w, routing_bias):
        import jax, jax.numpy as jnp
        import numpy as np
        B, S, H = (2, 256, 128)
        E_ROUTED = 8
        TOP_K = 2
        I = 256
        b, s, h = x.shape
        shared = jnp.einsum('bsi,hi->bsh', jax.nn.silu(jnp.einsum('bsh,ih->bsi', x, shared_gate)) * jnp.einsum('bsh,ih->bsi', x, shared_up), shared_down)
        logits = jnp.einsum('bsh,eh->bse', x, router_w) + routing_bias
        probs = jax.nn.sigmoid(logits)
        scores, indices = jax.lax.top_k(probs, TOP_K)
        scores = scores / jnp.sum(scores, axis=-1, keepdims=True)
        t = b * s
        xf = x.reshape(t, h)
        idx = indices.reshape(t, TOP_K)
        sc = scores.reshape(t, TOP_K)
        w = jnp.zeros((t, E_ROUTED), dtype=x.dtype)
        w = w.at[jnp.arange(t)[:, None], idx].add(sc)
        g = jax.nn.silu(jnp.einsum('th,ehi->tei', xf, gate_w))
        u = jnp.einsum('th,ehi->tei', xf, up_w)
        combined = jnp.einsum('tei,eih,te->th', g * u, down_w, w)
        return shared + combined.reshape(b, s, h)

    def _L3_attn_ref(h_t, W_DQ, b_DQ, W_UQ, b_UQ, W_DKV, b_DKV, W_UK, b_UK, W_UV, b_UV, W_QR, b_QR, W_KR, b_KR, W_O, b_O):
        import jax, jax.numpy as jnp
        import numpy as np
        import math
        D_MODEL, N_HEADS, D_K, D_C, D_HR = (128, 8, 128, 32, 32)
        B, S = (4, 256)
        b, s, _ = h_t.shape
        c_q = h_t @ W_DQ + b_DQ
        c_kv = h_t @ W_DKV + b_DKV
        q_c = (c_q @ W_UQ + b_UQ).reshape(b, s, N_HEADS, D_K).transpose(0, 2, 1, 3)
        k_c = (c_kv @ W_UK + b_UK).reshape(b, s, N_HEADS, D_K).transpose(0, 2, 1, 3)
        v_c = (c_kv @ W_UV + b_UV).reshape(b, s, N_HEADS, D_K).transpose(0, 2, 1, 3)
        q_r = (c_q @ W_QR + b_QR).reshape(b, s, N_HEADS, D_HR).transpose(0, 2, 1, 3)
        k_r = (h_t @ W_KR + b_KR)[:, None, :, :]
        k_r = jnp.broadcast_to(k_r, (b, N_HEADS, s, D_HR))
        q = jnp.concatenate([q_c, q_r], axis=-1)
        k = jnp.concatenate([k_c, k_r], axis=-1)
        scale = 1.0 / math.sqrt(D_K + D_HR)
        scores = jnp.einsum('bhsd,bhtd->bhst', q, k) * scale
        attn = jax.nn.softmax(scores, axis=-1)
        o = jnp.einsum('bhst,bhtd->bhsd', attn, v_c)
        o = o.transpose(0, 2, 1, 3).reshape(b, s, N_HEADS * D_K)
        return o @ W_O + b_O

    def _L3_xattn_ref(values, keys, queries, Wv, Wk, Wq, Wo, bo):
        import jax, jax.numpy as jnp
        import numpy as np
        EMBED = 128
        HEADS = 16
        HEAD_DIM = EMBED // HEADS
        N, Lq, _ = queries.shape
        Lk = keys.shape[1]
        v = values.reshape(N, Lk, HEADS, HEAD_DIM)
        k = keys.reshape(N, Lk, HEADS, HEAD_DIM)
        q = queries.reshape(N, Lq, HEADS, HEAD_DIM)
        v = jnp.einsum('nlhd,ed->nlhe', v, Wv)
        k = jnp.einsum('nlhd,ed->nlhe', k, Wk)
        q = jnp.einsum('nqhd,ed->nqhe', q, Wq)
        energy = jnp.einsum('nqhd,nkhd->nhqk', q, k)
        attn = jax.nn.softmax(energy / jnp.sqrt(jnp.float32(EMBED)), axis=-1)
        out = jnp.einsum('nhqk,nkhd->nqhd', attn, v).reshape(N, Lq, EMBED)
        return out @ Wo.T + bo

    def _L3_ffn_ref(x, router_w, w_gate, w_up, w_down):
        import jax, jax.numpy as jnp
        import numpy as np
        TOP_K = 2
        B, S, D = x.shape
        E = router_w.shape[0]
        xt = x.reshape(-1, D)
        logits = xt @ router_w.T
        topk_vals, topk_idx = jax.lax.top_k(logits, TOP_K)
        g = jax.nn.sigmoid(topk_vals)
        g = g / (g.sum(axis=-1, keepdims=True) + 1e-10)
        out = jnp.zeros_like(xt)
        for e in range(E):
            ge = jnp.sum(jnp.where(topk_idx == e, g, jnp.zeros_like(g)), axis=-1)
            h = jax.nn.silu(xt @ w_gate[e]) * (xt @ w_up[e])
            out = out + ge[:, None] * (h @ w_down[e])
        return out.reshape(B, S, D)
    x = x + _L0_attn_ref(_layernorm(x, axis=-1), L0_attn_qkv_w, L0_attn_qkv_b, L0_attn_proj_w, L0_attn_proj_b)
    x = x + _L0_xattn_ref(_layernorm(x, axis=-1), ctx_1024, mask_BxS2_bk0, L0_xattn_rms_scale, L0_xattn_q_w, L0_xattn_kv_w, L0_xattn_out_w)
    x = x + _L0_ffn_ref(_layernorm(x, axis=-1), L0_ffn_clip_x, L0_ffn_clip_down, L0_ffn_w_gate, L0_ffn_w_up, L0_ffn_w_down)
    x = x + _L1_attn_ref(_layernorm(x, axis=-1), L1_attn_Wq, L1_attn_bq, L1_attn_Wk, L1_attn_bk, L1_attn_Wv, L1_attn_bv)
    x = x + _L1_xattn_ref(ctx_1024, _layernorm(x, axis=-1), L1_xattn_ln1_w, L1_xattn_ln1_b, L1_xattn_ln2_w, L1_xattn_ln2_b, L1_xattn_Wq, L1_xattn_Wkv, L1_xattn_Wo)
    x = x + _L1_ffn_ref(_layernorm(x, axis=-1), L1_ffn_attn_mask, L1_ffn_Wg, L1_ffn_Wq, L1_ffn_bq, L1_ffn_Wkv, L1_ffn_bkv, L1_ffn_Wo, L1_ffn_bo, L1_ffn_ln_g, L1_ffn_ln_b)
    x = x + _L2_attn_ref(_layernorm(x, axis=-1), L2_attn_Wq, L2_attn_Wk, L2_attn_Wv, L2_attn_Wo, L2_attn_bo)
    x = x + _L2_xattn_ref(_layernorm(x, axis=-1), ctx_1024, L2_xattn_Wq, L2_xattn_Wkv, L2_xattn_null_kv, L2_xattn_ln_q_g, L2_xattn_ln_q_b, L2_xattn_ln_out_g, L2_xattn_ln_out_b, L2_xattn_Wout)
    x = x + _L2_ffn_ref(_layernorm(x, axis=-1), L2_ffn_shared_gate, L2_ffn_shared_up, L2_ffn_shared_down, L2_ffn_gate_w, L2_ffn_up_w, L2_ffn_down_w, L2_ffn_router_w, L2_ffn_routing_bias)
    x = x + _L3_attn_ref(_layernorm(x, axis=-1), L3_attn_W_DQ, L3_attn_b_DQ, L3_attn_W_UQ, L3_attn_b_UQ, L3_attn_W_DKV, L3_attn_b_DKV, L3_attn_W_UK, L3_attn_b_UK, L3_attn_W_UV, L3_attn_b_UV, L3_attn_W_QR, L3_attn_b_QR, L3_attn_W_KR, L3_attn_b_KR, L3_attn_W_O, L3_attn_b_O)
    x = x + _L3_xattn_ref(ctx_1024, ctx_1024, _layernorm(x, axis=-1), L3_xattn_Wv, L3_xattn_Wk, L3_xattn_Wq, L3_xattn_Wo, L3_xattn_bo)
    x = x + _L3_ffn_ref(_layernorm(x, axis=-1), L3_ffn_router_w, L3_ffn_w_gate, L3_ffn_w_up, L3_ffn_w_down)
    return x

_drawn_inputs = setup_inputs


def setup_inputs(seed=0):
    import zlib

    import numpy as np

    out = dict(_drawn_inputs(seed))
    spreads = {'L1_xattn_ln1_w': (1.0, 0.2),
     'L1_xattn_ln1_b': (0.0, 0.1),
     'L1_xattn_ln2_w': (1.0, 0.2),
     'L1_xattn_ln2_b': (0.0, 0.1),
     'L1_ffn_bq': (0.0, 0.8),
     'L1_ffn_bkv': (0.0, 0.8),
     'L1_ffn_bo': (0.0, 0.1),
     'L1_ffn_ln_g': (1.0, 0.2),
     'L1_ffn_ln_b': (0.0, 0.1),
     'L2_attn_bo': (0.0, 0.1),
     'L2_xattn_ln_q_g': (1.0, 0.6),
     'L2_xattn_ln_q_b': (0.0, 0.8),
     'L2_xattn_ln_out_g': (1.0, 0.2),
     'L2_xattn_ln_out_b': (0.0, 0.1),
     'L2_ffn_routing_bias': (0.0, 0.8)}
    factors = {'L0_ffn_w_gate': 3.633,
     'L0_ffn_w_up': 3.736,
     'L0_ffn_w_down': 3.822,
     'L1_attn_bq': 64.0,
     'L1_attn_bk': 4.564,
     'L1_ffn_Wq': 8.0,
     'L1_ffn_Wkv': 8.0,
     'L1_ffn_Wo': 8.0,
     'L2_attn_Wq': 8.0,
     'L2_attn_Wk': 8.0,
     'L2_attn_Wv': 8.0,
     'L2_attn_Wo': 8.0,
     'L2_xattn_Wq': 3.743,
     'L2_ffn_shared_gate': 5.821,
     'L2_ffn_shared_up': 6.325,
     'L2_ffn_shared_down': 5.732,
     'L2_ffn_gate_w': 7.474,
     'L2_ffn_up_w': 6.99,
     'L2_ffn_down_w': 8.0,
     'L2_ffn_router_w': 8.0,
     'L3_attn_W_DQ': 8.0,
     'L3_attn_b_DQ': 32.029,
     'L3_attn_W_UQ': 8.0,
     'L3_attn_b_UQ': 53.303,
     'L3_attn_b_DKV': 17.515,
     'L3_attn_W_UK': 8.0,
     'L3_attn_b_UK': 64.0,
     'L3_attn_W_QR': 8.0,
     'L3_attn_b_QR': 62.495,
     'L3_attn_W_KR': 8.0,
     'L3_attn_b_KR': 64.0,
     'L3_attn_b_O': 12.14,
     'L3_xattn_bo': 21.511,
     'L3_attn_b_UV': 3.628}
    for name, (base, spread) in spreads.items():
        noise = np.random.default_rng([zlib.crc32(name.encode()), seed]).standard_normal(out[name].shape)
        drawn = base * np.exp(spread * noise) if base else spread * noise
        out[name] = jnp.asarray(drawn.astype(out[name].dtype))
    for name, factor in factors.items():
        out[name] = (out[name] * factor).astype(out[name].dtype)
    return out
```

```python
import numpy as np
from contextlib import ExitStack

import concourse.bass as bass
import concourse.mybir as mybir

F32 = mybir.dt.float32
BF16 = mybir.dt.bfloat16
U8 = mybir.dt.uint8
U32 = mybir.dt.uint32
I32 = mybir.dt.int32
ALU = mybir.AluOpType
ACT = mybir.ActivationFunctionType
AX = mybir.AxisListType
REDUCE_MAX = bass.bass_isa.ReduceOp.max

B, S, D = 32, 128, 128
SC = 77
LN_EPS = 1e-5
RMS_EPS = 1e-6


class Signal:

    def __init__(self, scope, name, per_step=1):
        self.sem, self.n = scope.semaphore(name), per_step
        scope.signals.append(self)

    def wait(self, eng, t, k):
        eng.wait_ge(self.sem, t * self.n + (k + 1))

    def wait_steps(self, eng, t):
        eng.wait_ge(self.sem, t * self.n + 1)


class Scope:

    def __init__(self, nc, name):
        self.nc, self.name, self.stack, self.sems, self.signals = nc, name, ExitStack(), [], []

    def __enter__(self):
        self.passed = self.semaphore("waits_passed")
        return self

    def sb(self, name, shape, dt=F32):
        return self.stack.enter_context(self.nc.sbuf_tensor(f"{self.name}_{name}", shape, dt))

    def ps(self, name, shape, dt=F32):
        return self.stack.enter_context(self.nc.psum_tensor(f"{self.name}_{name}", shape, dt))

    def semaphore(self, name):
        sem = self.nc.alloc_semaphore(f"{self.name}_{name}")
        self.sems.append(sem)
        return sem

    def counter(self, name, per_step=1):
        return Signal(self, name, per_step)

    def begin(self):
        for s in self.signals:
            self.nc.gpsimd.sem_inc(s.sem, 1)
        self.nc.all_engine_barrier()

    def __exit__(self, failure, *_):
        if failure:
            return
        self.stack.close()
        self.nc.clear_and_free_semaphores(self.sems)


def settle(eng, passed):
    eng.sem_inc(passed, 1)


def make_consts(nc, c):
    made = nc.alloc_semaphore("consts_made")
    with nc.Block() as block:
        @block.gpsimd
        def _(pool):
            nc.gpsimd.memset(c["ident"][:, :], 1.0)
            nc.gpsimd.memset(c["ones"][:, :], 1.0)
            nc.gpsimd.memset(c["neg_half"][:, :], -0.5)
            nc.gpsimd.memset(c["head_mask"][:, :, :], 1.0).then_inc(made, 1)
            pool.wait_ge(made, 1)
            nc.gpsimd.affine_select(out=c["ident"][:, :], in_=c["ident"][:, :], compare_op=ALU.is_equal, fill=0.0,
                                    base=0, pattern=[[-1, 128]], channel_multiplier=1).then_inc(made, 1)
            m = c["head_mask"]
            nc.gpsimd.affine_select(out=m[:, :, :], in_=m[:, :, :], compare_op=ALU.is_ge, fill=0.0,
                                    base=0, pattern=[[-8, 4], [-32, 4]], channel_multiplier=1).then_inc(made, 1)
            pool.wait_ge(made, 3)
            nc.gpsimd.affine_select(out=m[:, :, :], in_=m[:, :, :], compare_op=ALU.is_ge, fill=0.0,
                                    base=7, pattern=[[8, 4], [32, 4]], channel_multiplier=-1).then_inc(made, 1)

        @block.vector
        def _(dve):
            dve.wait_ge(made, 4)
            nc.vector.reduce_sum(c["mask8"][:, :], c["head_mask"][:, :, :], axis=AX.X)
    nc.clear_and_free_semaphores([made])
    nc.all_engine_barrier()


def normalize(nc, c, name, src, P, dstT, stages, dstT_step=None, scale=None, shift=None, token_out=None):
    G = 4
    N = B // G
    step = dstT_step or P
    k = len(stages)
    with Scope(nc, name) as sc:
        m = max(k, 1)
        st = sc.sb("stats", [P, m, G, 6])
        mv = sc.sb("mean_var", [P, m, G, 2])
        ve = sc.sb("var_eps", [P, m, G])
        rs = sc.sb("rstd", [P, m, G])
        xn = sc.sb("xn", [P, 2, k + 1, G, 128])
        before = [sum(2 if kind == "ln" else 3 for kind in stages[:i]) for i in range(k + 1)]
        ps = [sc.ps(f"tp{i}", [128, 512]) for i in range(2)]
        var_ready = sc.counter("var_ready", k)
        rstd_ready = sc.counter("rstd_ready", k)
        stats_done = sc.counter("stats_done", before[k])
        stage_done = sc.counter("stage_done", k)
        copied_in = sc.counter("tiles_copied")
        transposed = sc.counter("transposed")
        evacuated = sc.counter("evacuated")
        sc.begin()
        with nc.Block() as block:
            @block.gpsimd
            def _(pool):
                if k:
                    with pool.Fori(0, N) as t:
                        for i in range(k):
                            var_ready.wait(pool, t, i + 1)
                            settle(pool, sc.passed)
                            nc.gpsimd.tensor_tensor(rs[:, i, :], ve[:, i, :], c["neg_half"][0:P, 0:G],
                                                    ALU.pow).then_inc(rstd_ready.sem, 1)

            @block.tensor
            def _(pe):
                with pe.Fori(0, N // 2) as it:
                    for s in range(2):
                        t = it * 2 + s
                        evacuated.wait_steps(pe, it * 2)
                        if k:
                            stage_done.wait(pe, t, k)
                        else:
                            copied_in.wait(pe, t, 1)
                        settle(pe, sc.passed)
                        for j in range(G):
                            last = nc.tensor.transpose(ps[s][:, j * P:(j + 1) * P], xn[:, s, k, j, :],
                                                       c["ident"][0:P, 0:P])
                        last.then_inc(transposed.sem, 1)

            @block.vector
            def _(dve):
                def norm(t, s):
                    transposed.wait_steps(dve, t - s)
                    for i, kind in enumerate(stages):
                        def tile(j):
                            return src[:, t * G + j, :] if i == 0 else xn[:, s, i, j, :]
                        for j in range(G):
                            settle(dve, sc.passed)
                            last = nc.vector.bn_stats(st[:, i, j, :], tile(j))
                        last.then_inc(stats_done.sem, 1)
                        stats_done.wait(dve, t, before[i] + 1)
                        settle(dve, sc.passed)
                        for j in range(G):
                            last = nc.vector.bn_aggr(mv[:, i, j, :], st[:, i, j, :])
                        last.then_inc(stats_done.sem, 1)
                        stats_done.wait(dve, t, before[i] + 2)
                        if kind == "ln":
                            nc.vector.tensor_scalar(ve[:, i, :], mv[:, i, :, 1], LN_EPS, None, ALU.add) \
                                .then_inc(var_ready.sem, 1)
                        else:
                            nc.vector.tensor_tensor(ve[:, i, :], mv[:, i, :, 0], mv[:, i, :, 0], ALU.mult) \
                                .then_inc(stats_done.sem, 1)
                            stats_done.wait(dve, t, before[i] + 3)
                            nc.vector.scalar_tensor_tensor(out=ve[:, i, :], in0=ve[:, i, :], scalar=RMS_EPS,
                                                           in1=mv[:, i, :, 1], op0=ALU.add,
                                                           op1=ALU.add).then_inc(var_ready.sem, 1)
                        rstd_ready.wait(dve, t, i + 1)
                        for j in range(G):
                            if kind == "ln":
                                last = nc.vector.tensor_scalar(xn[:, s, i + 1, j, :], tile(j), mv[:, i, j, 0:1],
                                                               rs[:, i, j:j + 1], ALU.subtract, ALU.mult)
                            else:
                                last = nc.vector.tensor_scalar(xn[:, s, i + 1, j, :], tile(j), rs[:, i, j:j + 1],
                                                               None, ALU.mult)
                        last.then_inc(stage_done.sem, 1)
                        if i + 1 < k:
                            stage_done.wait(dve, t, i + 1)

                def evac(t, s):
                    transposed.wait(dve, t, 1)
                    dst = dstT[:, bass.ds(t * (G * step), G * step)]
                    if step != P:
                        dst = dst.rearrange("p (g n) -> p g n", n=step)[:, :, 0:P]
                        src_ps = ps[s][:, 0:G * P].rearrange("p (g n) -> p g n", n=P)
                    else:
                        src_ps = ps[s][:, 0:G * P]
                    if scale is not None:
                        i = nc.vector.tensor_scalar(dst, src_ps, scale[:, 0:1], shift[:, 0:1], ALU.mult, ALU.add)
                    else:
                        i = nc.vector.tensor_scalar(dst, src_ps, 1.0, None, ALU.mult)
                    i.then_inc(evacuated.sem, 1)

                with dve.Fori(0, N // 2) as it:
                    for s in range(2):
                        t = it * 2 + s
                        if k:
                            norm(t, s)
                            if token_out is not None:
                                stage_done.wait(dve, t, k)
                                for j in range(G):
                                    settle(dve, sc.passed)
                                    nc.vector.tensor_copy(token_out[:, t * G + j, :], xn[:, s, k, j, :])
                        else:
                            transposed.wait_steps(dve, it * 2)
                            for j in range(G):
                                settle(dve, sc.passed)
                                last = nc.vector.tensor_copy(xn[:, s, 0, j, :], src[:, t * G + j, :])
                            last.then_inc(copied_in.sem, 1)
                        evac(t, s)


def attention(nc, c, name, cfg, load):
    with Scope(nc, name) as sc:
        b = load(sc)
        H, U, TK = cfg["heads"], cfg["units"], cfg["keys"]
        NB, R = 2, min(4, U)
        LAG = 3
        HU = H // U
        DV = cfg["dv"]
        GP = cfg["proj_groups"]
        kchunks = cfg["key_chunks"]
        KC = len(kchunks)
        WO = H * DV
        NP = (WO + 511) // 512
        PW = min(512, WO)
        post, masked = cfg.get("post"), cfg.get("masked")
        nmax = sc.sb("neg_max", [128, H])
        sums = sc.sb("sums", [128, 2, H])
        rsum = sc.sb("rsum", [128, 2, HU])
        P_sb = sc.sb("probs", [128, R, HU, TK])
        PT_sb = sc.sb("probs_t", [128, 2, HU, KC, 128])
        OT_sb = sc.sb("heads_out_t", [128, 2, WO // 128, 128])
        Sm = sc.sb("masked_scores", [128, NB, HU, TK]) if masked else None
        S_ps = [sc.ps(f"scores{i}", [128, 512]) for i in range(NB)]
        PT_ps = sc.ps("pt", [128, 512])
        O_ps = [sc.ps(f"o{i}", [128, 512]) for i in range(2)]
        pr_ps = [sc.ps(f"proj{i}", [128, 512]) for i in range(2)]
        out_ps = sc.ps("out", [128, 512])

        tile_ready = sc.counter("tile_ready")
        projected = sc.counter("projected", GP)
        proj_copied = sc.counter("proj_copied", GP)
        posted = sc.counter("posted")
        post_part = sc.counter("post_part", 2)
        scored = sc.counter("scored", U)
        mask_part = sc.counter("mask_part", 2 * U)
        maxed = sc.counter("maxed", U)
        exped = sc.counter("exped", U)
        turned = sc.counter("turned", U)
        turned_copied = sc.counter("turned_copied", U)
        weighted = sc.counter("weighted", U)
        inverted = sc.counter("inverted", U)
        divided = sc.counter("divided", U)
        piece_copied = sc.counter("piece_copied", NP)
        out_filled = sc.counter("out_filled")
        added = sc.counter("added")
        loaded, nloads = b["loaded"], b["loads"]

        def back(sig, eng, t, k, lag):
            v = k - lag + 1
            if not isinstance(t, int) or t * sig.n + v > 0:
                sig.wait(eng, t, v)

        def lagging(t, u, first):
            if u >= LAG:
                return t, u - LAG
            return None if first else (t - 1, u - LAG + U)

        def steps(eng, before, slot, after):
            before()
            for u in range(U):
                slot(0, 0, u, True, False)
            with eng.Fori(0, (B - 2) // 2) as it:
                for s in range(2):
                    for u in range(U):
                        slot(it * 2 + 1 + s, (1 + s) % 2, u, False, False)
            for u in range(U):
                slot(B - 1, (B - 1) % 2, u, False, True)
            after()

        drain = [(B - 1, u) for u in range(U - LAG, U)]
        sched = cfg["schedule"]

        sc.begin()
        with nc.Block() as block:
            @block.sync
            def _(sp):
                b["dma"](sp)

            @block.gpsimd
            def _(pool):
                if "prepare_pool" in b:
                    b["prepare_pool"](pool)

                def tile_copy(t, s):
                    if not isinstance(t, int) or t >= 2:
                        projected.wait_steps(pool, t - 1)
                    settle(pool, sc.passed)
                    for dst, src in b["tiles"](t, s):
                        last = nc.gpsimd.tensor_copy(dst, src)
                    last.then_inc(tile_ready.sem, 1)

                def slot(t, s, u, first, last):
                    if u == 0 and not last:
                        tile_copy(t + 1, 1 - s)
                steps(pool, lambda: tile_copy(0, 0), slot, lambda: None)

            @block.tensor
            def _(pe):
                pe.wait_ge(loaded, 16 * nloads)
                if "prepared" in b:
                    pe.wait_ge(b["prepared"][0], b["prepared"][1])

                def proj(t, s, g):
                    if g == 0:
                        tile_ready.wait(pe, t, 1)
                    if g >= 2:
                        proj_copied.wait(pe, t, g - 1)
                    elif g == 0 and not (isinstance(t, int) and t == 0):
                        proj_copied.wait_steps(pe, t)
                    elif g == 1 and cfg.get("first_feeds"):
                        proj_copied.wait(pe, t, 1)
                    settle(pe, sc.passed)
                    cfg["proj"](b, g, s, pr_ps[g % 2]).then_inc(projected.sem, 1)

                def scores(t, s, u):
                    if u == 0:
                        if post:
                            posted.wait(pe, t, 1)
                        proj_copied.wait(pe, t, GP)
                    back(exped, pe, t, u, NB)
                    settle(pe, sc.passed)
                    cfg["scores"](b, u, s, S_ps[u % NB]).then_inc(scored.sem, 1)

                def turn(t, u):
                    divided.wait(pe, t, u + 1)
                    back(turned_copied, pe, t, u, 1)
                    settle(pe, sc.passed)
                    for j in range(HU):
                        for kc, (k0, kn) in enumerate(kchunks):
                            o = (j * KC + kc) * 128
                            last = nc.tensor.transpose(PT_ps[0:kn, o:o + 128], P_sb[:, u % R, j, k0:k0 + kn],
                                                       c["ident"][:, :])
                    last.then_inc(turned.sem, 1)

                def weigh(t, s, u):
                    turned_copied.wait(pe, t, u + 1)
                    if u * NP % U == 0:
                        back(piece_copied, pe, t, u * NP // U, 2)
                    settle(pe, sc.passed)
                    for j in range(HU):
                        h = cfg["unit_heads"](u)[j]
                        last = cfg["weigh"](b, h, s, O_ps[s if NP == 1 else h * NP // H],
                                            [PT_sb[0:kn, u % 2, j, kc, :] for kc, (k0, kn) in enumerate(kchunks)])
                    last.then_inc(weighted.sem, 1)

                def output(t, s):
                    piece_copied.wait(pe, t, NP)
                    back(added, pe, t, 0, 1)
                    settle(pe, sc.passed)
                    n = WO // 128
                    for m in range(n):
                        last = nc.tensor.matmul(out_ps[:, 0:128], OT_sb[:, s, m, :], b["wo"](m),
                                                start=(m == 0), stop=(m == n - 1 and "bo" not in b))
                    if "bo" in b:
                        last = nc.tensor.matmul(out_ps[:, 0:128], c["ones"][0:1, :], b["bo"], start=False, stop=True)
                    last.then_inc(out_filled.sem, 1)

                def slot(t, s, u, first, last):
                    old = lagging(t, u, first)
                    if old:
                        turn(*old)
                    scores(t, s, u)
                    for kind, g in sched[u]:
                        if kind == "p" and not last:
                            proj(t + 1, 1 - s, g)
                        if kind == "o" and not first:
                            output(t - 1, 1 - s)
                    if old:
                        weigh(old[0], s if u >= LAG else 1 - s, old[1])

                def before():
                    for g in range(GP):
                        proj(0, 0, g)

                def after():
                    for t, u in drain:
                        turn(t, u)
                        weigh(t, t % 2, u)
                    output(B - 1, (B - 1) % 2)
                steps(pe, before, slot, after)

            @block.scalar
            def _(act):
                act.wait_ge(loaded, 16 * nloads)
                if "prepare_act" in b:
                    b["prepare_act"](act)

                def copy_proj(t, s, g):
                    projected.wait(act, t, g + 1)
                    if not (isinstance(t, int) and t < 2):
                        if g in cfg["v_groups"]:
                            weighted.wait_steps(act, t - 1)
                        else:
                            scored.wait_steps(act, t - 1)
                    if g == 0 and post and not (isinstance(t, int) and t == 0):
                        posted.wait_steps(act, t)
                    settle(act, sc.passed)
                    cfg["copy"](b, g, s, pr_ps[g % 2]).then_inc(proj_copied.sem, 1)

                def exps(t, s, u):
                    maxed.wait(act, t, u + 1)
                    back(turned, act, t, u, R)
                    for j in range(HU):
                        h = cfg["unit_heads"](u)[j]
                        src = Sm[:, u % NB, j, :] if masked else S_ps[u % NB][:, j * TK:(j + 1) * TK]
                        last = nc.scalar.activation(P_sb[:, u % R, j, :], src, ACT.Exp, bias=nmax[:, h:h + 1],
                                                    accum_out=sums[:, s, h:h + 1])
                    last.then_inc(exped.sem, 1)

                def copy_piece(t, s, p):
                    weighted.wait(act, t, (p + 1) * U // NP)
                    back(out_filled, act, t, 0, 2)
                    n = PW // 128
                    nc.scalar.activation(OT_sb[:, s, p * n:p * n + n, :], O_ps[s if NP == 1 else p][:, 0:PW],
                                         ACT.Copy).then_inc(piece_copied.sem, 1)

                def finish(t, s, u):
                    if (u + 1) * NP % U == 0:
                        copy_piece(t, s, (u + 1) * NP // U - 1)

                def slot(t, s, u, first, last):
                    groups = [] if last else [g for kind, g in sched[u] if kind == "p"]
                    for g in groups[:2]:
                        copy_proj(t + 1, 1 - s, g)
                    exps(t, s, u)
                    for g in groups[2:]:
                        copy_proj(t + 1, 1 - s, g)
                    old = lagging(t, u, first)
                    if old:
                        finish(old[0], s if u >= LAG else 1 - s, old[1])

                def before():
                    for g in range(GP):
                        copy_proj(0, 0, g)

                def after():
                    for t, u in drain:
                        finish(t, t % 2, u)
                steps(act, before, slot, after)

            @block.vector
            def _(dve):
                if "prepare_dve" in b:
                    b["prepare_dve"](dve)

                def maxima(t, s, u):
                    scored.wait(dve, t, u + 1)
                    if masked:
                        back(exped, dve, t, u, NB)
                        settle(dve, sc.passed)
                        keep, fill = b["mask"](t)
                        nc.vector.tensor_tensor(Sm[:, u % NB, 0, :], S_ps[u % NB][:, 0:TK], keep, ALU.mult) \
                            .then_inc(mask_part.sem, 1)
                        mask_part.wait(dve, t, 2 * u + 1)
                        nc.vector.tensor_tensor(Sm[:, u % NB, 0, :], Sm[:, u % NB, 0, :], fill, ALU.add) \
                            .then_inc(mask_part.sem, 1)
                        mask_part.wait(dve, t, 2 * u + 2)
                        src = Sm[:, u % NB, :, :]
                    else:
                        src = S_ps[u % NB][:, 0:HU * TK].rearrange("p (h k) -> p h k", h=HU)
                    nm = b["columns"](nmax, u) if "columns" in b else nmax[:, u * HU:(u + 1) * HU]
                    nc.vector.tensor_reduce(nm, src, AX.X, ALU.max, negate=True).then_inc(maxed.sem, 1)

                def copy_turned(t, u):
                    turned.wait(dve, t, u + 1)
                    back(weighted, dve, t, u, 2)
                    if KC == 1:
                        kn = kchunks[0][1]
                        last = nc.vector.tensor_copy(PT_sb[0:kn, u % 2, :, 0, :], PT_ps[0:kn, 0:HU * 128]
                                                     .rearrange("p (h q) -> p h q", h=HU))
                    else:
                        src = PT_ps[:, :].rearrange("p (h k q) -> p h k q", h=HU, k=KC)
                        for kc, (k0, kn) in enumerate(kchunks):
                            last = nc.vector.tensor_copy(PT_sb[0:kn, u % 2, :, kc, :], src[0:kn, :, kc, :])
                    last.then_inc(turned_copied.sem, 1)

                def divide(t, s, u):
                    exped.wait(dve, t, u + 1)
                    sm = b["columns"](sums[:, s, :], u) if "columns" in b else sums[:, s, u * HU:(u + 1) * HU]
                    nc.vector.reciprocal(rsum[:, u % 2, :], sm).then_inc(inverted.sem, 1)
                    inverted.wait(dve, t, u + 1)
                    nc.vector.tensor_tensor(P_sb[:, u % R, :, :], P_sb[:, u % R, :, :],
                                            rsum[:, u % 2, :].unsqueeze(2).to_broadcast([128, HU, TK]), ALU.mult) \
                        .then_inc(divided.sem, 1)

                def add(t):
                    out_filled.wait(dve, t, 1)
                    settle(dve, sc.passed)
                    xs = c["x"][:, t, :]
                    nc.vector.tensor_tensor(xs, out_ps[:, 0:128], xs, ALU.add).then_inc(added.sem, 1)

                def do_post(t, s):
                    proj_copied.wait(dve, t, 1)
                    cfg["post"](dve, b, t, s, post_part, posted)

                def slot(t, s, u, first, last):
                    old = lagging(t, u, first)
                    if u >= 2:
                        divide(t, s, u - 2)
                    elif not first:
                        divide(t - 1, 1 - s, u - 2 + U)
                    if old:
                        copy_turned(*old)
                    maxima(t, s, u)
                    if post and u == cfg["post_slot"] and not last:
                        do_post(t + 1, 1 - s)
                    if u == U - 1 and not first:
                        add(t - 1)

                def after():
                    for u in (U - 2, U - 1):
                        divide(B - 1, (B - 1) % 2, u)
                    for t, u in drain:
                        copy_turned(t, u)
                    add(B - 1)
                steps(dve, (lambda: do_post(0, 0)) if post else (lambda: None), slot, after)


def loader(nc, sc, items):
    loaded = sc.semaphore("loaded")

    def dma(sp):
        for dst, src in items:
            sp.dma_start(dst, src, allow_slow_non_contiguous=True).then_inc(loaded, 16)
    return dict(loaded=loaded, loads=len(items), dma=dma)


def spread_values(nc, v, s, src, keys):
    for j in range(4):
        last = nc.scalar.activation(v[0:keys, s, :, j, 8 * j:8 * j + 8],
                                    src.rearrange("p (u j d) -> p u j d", j=4, d=8)[:, :, j, :], ACT.Copy)
    return last


def weigh_small(nc, b, h, s, bank, pts):
    u, j = h // 4, h % 4
    return nc.tensor.matmul(bank[32 * u:32 * u + 32, 0:128], b["vb"][:, s, u, j, :], pts[0],
                            start=(j == 0), stop=(j == 3))


def l0_attention(nc, c, T):
    H, HD = 16, 8
    scale = float(HD) ** -0.5

    def load(sc):
        w = sc.sb("wqkv", [128, 384])
        wo = sc.sb("wo", [128, 128])
        bqk = sc.sb("bqk", [128, 2])
        bv = sc.sb("bv", [1, 128])
        bo = sc.sb("bo", [1, 128])
        bq_s = sc.sb("bq_scaled", [128, 1])
        bk_m = sc.sb("bk_masked", [128, 4])
        cur = sc.sb("tile", [128, 2, 128])
        q = sc.sb("q_t", [128, 2, 128])
        km = sc.sb("k_t", [128, 2, 4, 128])
        v = sc.sb("v", [128, 2, 4, 4, 32])
        zeroed = sc.semaphore("zeroed")
        biases = sc.semaphore("biases_ready")
        qb = T["L0_attn_qkv_b"]
        b = loader(nc, sc, [(w[:, :], T["L0_attn_qkv_w"]), (wo[:, :], T["L0_attn_proj_w"]),
                            (bqk[:, :], qb[0:256].rearrange("(a p) -> p a", p=128)),
                            (bv[:, :], qb[256:384].rearrange("(a p) -> a p", a=1)),
                            (bo[:, :], T["L0_attn_proj_b"].rearrange("(a p) -> a p", a=1))])

        def prepare_act(act):
            nc.scalar.activation(bq_s[:, :], bqk[:, 0:1], ACT.Copy, scale=scale)
            nc.scalar.activation(bk_m[:, :], c["mask8"][:, :], ACT.Copy, scale=bqk[:, 1:2]).then_inc(biases, 1)
            act.wait_ge(biases, 1)
            act.wait_ge(zeroed, 1)

        b.update(w=w, bq=bq_s, bk=bk_m, bv=bv, cur=cur, q=q, km=km, vb=v, prepare_act=prepare_act,
                 tiles=lambda t, s: [(cur[:, s, :], c["nT"][:, bass.ds(t * 128, 128)])],
                 prepare_pool=lambda pool: nc.gpsimd.memset(v[:, :, :, :, :], 0.0).then_inc(zeroed, 1),
                 wo=lambda m: wo[:, :], bo=bo[:, :])
        return b

    def proj(b, g, s, bank):
        t = b["cur"][:, s, :]
        if g == 0:
            for i in range(2):
                last = nc.tensor.matmul(bank[:, i * 128:(i + 1) * 128], b["w"][:, i * 128:(i + 1) * 128], t,
                                        start=True, stop=True)
            return last
        nc.tensor.matmul(bank[:, 0:128], t, b["w"][:, 256:384], start=True, stop=False)
        return nc.tensor.matmul(bank[:, 0:128], c["ones"][0:1, :], b["bv"][:, :], start=False, stop=True)

    def copy(b, g, s, bank):
        if g == 0:
            nc.scalar.activation(b["q"][:, s, :], bank[:, 0:128], ACT.Identity, bias=b["bq"][:, 0:1], scale=scale)
            for j in range(4):
                last = nc.scalar.activation(b["km"][:, s, j, :], bank[:, 128:256], ACT.Identity,
                                            bias=b["bk"][:, j:j + 1], scale=c["mask8"][:, j:j + 1])
            return last
        return spread_values(nc, b["vb"], s, bank[:, 0:128], 128)

    def scores(b, u, s, bank):
        r = slice(32 * u, 32 * u + 32)
        for j in range(4):
            last = nc.tensor.matmul(bank[:, j * 128:(j + 1) * 128], b["q"][r, s, :], b["km"][r, s, j, :],
                                    start=True, stop=True)
        return last

    attention(nc, c, "l0_attn", dict(heads=H, units=4, v_groups=(1,), schedule=[[("p", 0)], [], [], [("p", 1), ("o", 0)]], keys=128, dv=HD, proj_groups=2, weigh=lambda *a: weigh_small(nc, *a),
                                     key_chunks=[(0, 128)], proj=proj, copy=copy, scores=scores,
                                     unit_heads=lambda u: [4 * u + j for j in range(4)]), load)


def row(ap):
    return ap.rearrange("(a p) -> a p", a=1)


def column(ap):
    return ap.rearrange("(p a) -> p a", a=1)


def l0_cross_attention(nc, c, T):
    H, HD = 4, 32
    MASK_FILL = -2.3819763e+38
    NQK = 128 + SC

    def load(sc):
        wq = sc.sb("wq", [128, 2, 4, 32])
        wk = sc.sb("wk", [128, 2, 4, 32])
        wv = sc.sb("wv", [128, 32])
        wo = sc.sb("wo", [128, 128])
        rms = sc.sb("rms", [128, 2])
        table = sc.sb("rope", [128, 2, NQK])
        cur = sc.sb("tile", [128, 2, NQK])
        raw = sc.sb("raw", [128, 2, NQK])
        turned = sc.sb("rotated", [128, 2, NQK])
        qk = sc.sb("qk_t", [128, 2, NQK])
        v = sc.sb("v", [SC, 2, 32])
        bits = sc.sb("mask_bytes", [128, B * SC], U8)
        keep = sc.sb("keep", [128, B * SC])
        fill = sc.sb("fill", [128, B * SC])
        scaled = sc.semaphore("weights_scaled")
        masks = sc.semaphore("masks_ready")
        qw, kw = T["L0_xattn_q_w"], T["L0_xattn_kv_w"]
        items = [(wv[:, :], kw[1, 0]), (wo[:, :], T["L0_xattn_out_w"].rearrange("n h d -> (n h) d")),
                 (rms[:, 0:1], column(T["L0_xattn_rms_scale"])), (table[:, :, :], T["rope"]),
                 (bits[:, :], T["mask_BxS2_bk0"].rearrange("(a b) k -> a (b k)", a=1).to_broadcast([128, B * SC])),
                 (wq[:, 0, :, :], qw.rearrange("n d h -> d n h"))]
        for half in range(2):
            o, i = slice(16 * half, 16 * half + 16), slice(16 - 16 * half, 32 - 16 * half)
            items.append((wq[:, 1, :, o], qw[:, :, i].rearrange("n d h -> d n h")))
            for n in range(4):
                items.append((wk[:, 1, n, o], kw[0, 0, :, i]))
        for n in range(4):
            items.append((wk[:, 0, n, :], kw[0, 0]))
        b = loader(nc, sc, items)

        def prepare_act(act):
            nc.scalar.activation(rms[:, 1:2], rms[:, 0:1], ACT.Copy, bias=1.0).then_inc(scaled, 1)
            act.wait_ge(scaled, 1)
            for w in (wq[:, :, :, :], wk[:, :, :, :], wv[:, :]):
                last = nc.scalar.activation(w, w, ACT.Copy, scale=rms[:, 1:2])
            last.then_inc(scaled, 1)

        def prepare_dve(dve):
            dve.wait_ge(b["loaded"], 16 * b["loads"])
            nc.vector.tensor_copy(keep[:, :], bits[:, :]).then_inc(masks, 1)
            dve.wait_ge(masks, 1)
            nc.vector.tensor_scalar(fill[:, :], keep[:, :], -MASK_FILL, MASK_FILL, ALU.mult, ALU.add) \
                .then_inc(masks, 1)
            dve.wait_ge(masks, 2)

        b.update(wq=wq, wk=wk, wv=wv, cur=cur, raw=raw, turned=turned, qk=qk, vb=v, table=table,
                 prepare_act=prepare_act, prepare_dve=prepare_dve, prepared=(scaled, 2),
                 tiles=lambda t, s: [(cur[:, s, 0:128], c["nT"][:, bass.ds(t * 128, 128)]),
                                     (cur[:, s, 128:NQK], c["cT"][:, bass.ds(t * SC, SC)])],
                 mask=lambda t: (keep[:, bass.ds(t * SC, SC)], fill[:, bass.ds(t * SC, SC)]),
                 wo=lambda m: wo[:, :])
        return b

    def proj(b, g, s, bank):
        if g == 0:
            for i in range(2):
                o = i * NQK
                nc.tensor.matmul(bank[:, o:o + 128], b["wq"][:, i, :, :].rearrange("p n h -> p (n h)"),
                                 b["cur"][:, s, 0:128], start=True, stop=True)
                last = nc.tensor.matmul(bank[:, o + 128:o + NQK], b["wk"][:, i, :, :].rearrange("p n h -> p (n h)"),
                                        b["cur"][:, s, 128:NQK], start=True, stop=True)
            return last
        return nc.tensor.matmul(bank[0:SC, 0:32], b["cur"][:, s, 128:NQK], b["wv"][:, :], start=True, stop=True)

    def copy(b, g, s, bank):
        if g == 0:
            return nc.scalar.activation(b["raw"][:, :, :], bank[:, 0:2 * NQK], ACT.Copy)
        return nc.scalar.activation(b["vb"][:, s, :], bank[0:SC, 0:32], ACT.Copy)

    def post(dve, b, t, s, part, posted):
        for i in range(2):
            last = nc.vector.tensor_tensor(b["turned"][:, i, :], b["raw"][:, i, :], b["table"][:, i, :], ALU.mult)
        last.then_inc(part.sem, 1)
        part.wait(dve, t, 1)
        nc.vector.tensor_tensor(b["qk"][:, s, :], b["turned"][:, 0, :], b["turned"][:, 1, :], ALU.add) \
            .then_inc(part.sem, 1)
        part.wait(dve, t, 2)
        nc.vector.tensor_scalar(b["qk"][:, s, 0:128], b["qk"][:, s, 0:128], float(HD) ** -0.5, None, ALU.mult) \
            .then_inc(posted.sem, 1)

    def scores(b, u, s, bank):
        r = slice(32 * u, 32 * u + 32)
        return nc.tensor.matmul(bank[:, 0:SC], b["qk"][r, s, 0:128], b["qk"][r, s, 128:NQK], start=True, stop=True)

    def weigh(b, h, s, bank, pts):
        return nc.tensor.matmul(bank[32 * h:32 * h + 32, 0:128], b["vb"][:, s, :], pts[0], start=True, stop=True)

    attention(nc, c, "l0_xattn", dict(heads=H, units=4, keys=SC, dv=HD, proj_groups=2, weigh=weigh,
                                      v_groups=(1,), post_slot=1, schedule=[[("p", 0)], [], [], [("p", 1), ("o", 0)]],
                                      key_chunks=[(0, SC)], proj=proj, copy=copy, scores=scores, post=post,
                                      masked=True, unit_heads=lambda u: [u]), load)


def l1_cross_attention(nc, c, T):
    H, HD = 16, 64
    NK = SC + 128

    def load(sc):
        wq = sc.sb("wq", [128, 1024])
        wkv = sc.sb("wkv", [128, 2048])
        wo = sc.sb("wo", [128, 8, 128])
        cur = sc.sb("tile", [128, 2, NK])
        q = sc.sb("q_t", [128, 2, 8, 128])
        k = sc.sb("k_t", [128, 2, 8, NK])
        v = sc.sb("v", [128, 2, 2, 1024])
        b = loader(nc, sc, [(wq[:, :], T["L1_xattn_Wq"]), (wkv[:, :], T["L1_xattn_Wkv"]),
                            (wo[:, :, :], T["L1_xattn_Wo"].rearrange("(m p) d -> p m d", p=128))])

        def columns(nmax, u):
            o = 4 * (u // 2) + u % 2
            return nmax[:, o:o + 3:2]

        b.update(wq=wq, wkv=wkv, cur=cur, q=q, k=k, vb=v, columns=columns,
                 tiles=lambda t, s: [(cur[:, s, SC:NK], c["nT"][:, bass.ds(t * 128, 128)]),
                                     (cur[:, s, 0:SC], c["cT"][:, bass.ds(t * SC, SC)])],
                 wo=lambda m: wo[:, m, :])
        return b

    def proj(b, g, s, bank):
        if g < 2:
            for m in range(4):
                n = 4 * g + m
                last = nc.tensor.matmul(bank[:, m * 128:(m + 1) * 128], b["wq"][:, n * 128:(n + 1) * 128],
                                        b["cur"][:, s, SC:NK], start=True, stop=True)
        elif g < 6:
            for m in range(2):
                n = 2 * (g - 2) + m
                last = nc.tensor.matmul(bank[:, m * NK:(m + 1) * NK], b["wkv"][:, n * 128:(n + 1) * 128],
                                        b["cur"][:, s, :], start=True, stop=True)
        else:
            part, half = (g - 6) // 2, (g - 6) % 2
            t = b["cur"][:, s, SC:NK] if part else b["cur"][:, s, 0:SC]
            last = nc.tensor.matmul(bank[0:(SC, 128)[part], :], t,
                                    b["wkv"][:, 1024 + half * 512:1536 + half * 512], start=True, stop=True)
        return last

    def copy(b, g, s, bank):
        if g < 2:
            return nc.scalar.activation(b["q"][:, s, 4 * g:4 * g + 4, :], bank[:, :], ACT.Copy,
                                        scale=float(HD) ** -0.5)
        if g < 6:
            n = 2 * (g - 2)
            return nc.scalar.activation(b["k"][:, s, n:n + 2, :], bank[:, 0:2 * NK], ACT.Copy)
        part, half = (g - 6) // 2, (g - 6) % 2
        p = (SC, 128)[part]
        return nc.scalar.activation(b["vb"][0:p, s, part, half * 512:half * 512 + 512], bank[0:p, :], ACT.Copy)

    def scores(b, u, s, bank):
        r = slice(64 * (u % 2), 64 * (u % 2) + 64)
        for j in range(2):
            m = 2 * (u // 2) + j
            last = nc.tensor.matmul(bank[:, j * NK:(j + 1) * NK], b["q"][r, s, m, :], b["k"][r, s, m, :],
                                    start=True, stop=True)
        return last

    def weigh(b, h, s, bank, pts):
        r, m = 64 * (h % 2), h // 2 % 4
        for kc in range(2):
            last = nc.tensor.matmul(bank[r:r + 64, m * 128:(m + 1) * 128],
                                    b["vb"][0:(SC, 128)[kc], s, kc, h * HD:(h + 1) * HD], pts[kc],
                                    start=(kc == 0), stop=(kc == 1))
        return last

    attention(nc, c, "l1_xattn", dict(heads=H, units=8, v_groups=(6, 7, 8, 9),
                                      schedule=[[("p", 0), ("p", 1)], [("p", 2), ("p", 3)], [("p", 4)],
                                                [("o", 0), ("p", 5)], [("p", 6)], [("p", 7)], [("p", 8)], [("p", 9)]],
                                       keys=NK, dv=HD, proj_groups=10, weigh=weigh,
                                      key_chunks=[(0, SC), (SC, 128)], proj=proj, copy=copy, scores=scores,
                                      unit_heads=lambda u: [4 * (u // 2) + u % 2 + 2 * j for j in range(2)]), load)


def l3_attention(nc, c, T):
    H, DK, DC = 8, 128, 32
    scale = float(DK + DC) ** -0.5

    def load(sc):
        wd = sc.sb("w_down", [128, 192])
        bd = sc.sb("b_down", [128, 3])
        wuq = sc.sb("w_uq", [33, 1024])
        wuk = sc.sb("w_uk", [33, 1024])
        wuv = sc.sb("w_uv", [33, 1024])
        wqr = sc.sb("w_qr", [33, 256])
        wo = sc.sb("wo", [128, 8, 128])
        bo = sc.sb("bo", [1, 128])
        cur = sc.sb("tile", [128, 2, 128])
        cc = sc.sb("compressed", [33, 2, 128])
        kr = sc.sb("k_r", [128, 2, 128])
        qc = sc.sb("q_c", [128, 2, 8, 128])
        kc_ = sc.sb("k_c", [128, 2, 8, 128])
        qr = sc.sb("q_r", [128, 2, 2, 128])
        v = sc.sb("v", [128, 2, 1024])
        ready = sc.semaphore("ones_ready")
        items = [(wo[:, :, :], T["L3_attn_W_O"].rearrange("(m p) d -> p m d", p=128)), (bo[:, :], row(T["L3_attn_b_O"]))]
        for i, n in enumerate(("DQ", "DKV", "KR", "KR", "KR", "KR")):
            r = 32 * max(i - 2, 0)
            items += [(wd[:, 32 * i:32 * i + 32], T["L3_attn_W_" + n]),
                      (bd[r:r + 32, min(i, 2):min(i, 2) + 1], column(T["L3_attn_b_" + n]))]
        for m in range(2):
            for dst, src in ((wqr[0:32, m * 128:(m + 1) * 128], T["L3_attn_W_QR"]),
                             (wqr[32:33, m * 128:(m + 1) * 128], row(T["L3_attn_b_QR"]))):
                items.append((dst.rearrange("k (j d) -> k j d", j=4),
                              src.rearrange("k (j m d) -> k m j d", m=2, d=32)[:, m, :, :]))
        for w, n in ((wuq, "UQ"), (wuk, "UK"), (wuv, "UV")):
            items += [(w[0:32, :], T["L3_attn_W_" + n]), (w[32:33, :], row(T["L3_attn_b_" + n]))]
        b = loader(nc, sc, items)

        def prepare_pool(pool):
            nc.gpsimd.memset(cc[:, :, :], 1.0).then_inc(ready, 1)

        b.update(wd=wd, bd=bd, wuq=wuq, wuk=wuk, wuv=wuv, wqr=wqr, cur=cur, cc=cc, kr=kr, qc=qc, kc=kc_, qr=qr,
                 vb=v, prepare_pool=prepare_pool, prepared=(ready, 1), prepare_act=lambda act: act.wait_ge(ready, 1),
                 tiles=lambda t, s: [(cur[:, s, :], c["nT"][:, bass.ds(t * 128, 128)])],
                 wo=lambda m: wo[:, m, :], bo=bo[:, :])
        return b

    def proj(b, g, s, bank):
        if g == 0:
            for i in range(3):
                p = 128 if i == 2 else 32
                last = nc.tensor.matmul(bank[0:p, i * 128:(i + 1) * 128], b["wd"][:, 32 * i:32 * i + p],
                                        b["cur"][:, s, :], start=True, stop=True)
        elif g < 5:
            w, i = (b["wuq"], 0) if g < 3 else (b["wuk"], 1)
            for m in range(4):
                h = 4 * ((g - 1) % 2) + m
                last = nc.tensor.matmul(bank[:, m * 128:(m + 1) * 128], w[:, h * 128:(h + 1) * 128],
                                        b["cc"][:, i, :], start=True, stop=True)
        elif g < 6:
            for m in range(2):
                last = nc.tensor.matmul(bank[:, m * 128:(m + 1) * 128], b["wqr"][:, m * 128:(m + 1) * 128],
                                        b["cc"][:, 0, :], start=True, stop=True)
        else:
            o = (g - 6) * 512
            last = nc.tensor.matmul(bank[:, :], b["cc"][:, 1, :], b["wuv"][:, o:o + 512], start=True, stop=True)
        return last

    def copy(b, g, s, bank):
        if g == 0:
            for i, dst in enumerate((b["cc"][0:32, 0, :], b["cc"][0:32, 1, :], b["kr"][:, s, :])):
                p = 128 if i == 2 else 32
                last = nc.scalar.activation(dst, bank[0:p, i * 128:(i + 1) * 128], ACT.Identity,
                                            bias=b["bd"][0:p, i:i + 1])
            return last
        if g < 5:
            dst = b["qc"] if g < 3 else b["kc"]
            h = 4 * ((g - 1) % 2)
            return nc.scalar.activation(dst[:, s, h:h + 4, :], bank[:, :], ACT.Copy, scale=scale if g < 3 else 1.0)
        if g < 6:
            return nc.scalar.activation(b["qr"][:, s, :, :], bank[:, 0:256], ACT.Copy, scale=scale)
        o = (g - 6) * 512
        return nc.scalar.activation(b["vb"][:, s, o:o + 512], bank[:, :], ACT.Copy)

    def scores(b, u, s, bank):
        for j in range(2):
            h = 2 * u + j
            o, r = bank[:, j * 128:(j + 1) * 128], slice(32 * u, 32 * u + 32)
            nc.tensor.matmul(o, b["qc"][:, s, h, :], b["kc"][:, s, h, :], start=True, stop=False)
            last = nc.tensor.matmul(o, b["qr"][r, s, j, :], b["kr"][r, s, :], start=False, stop=True)
        return last

    def weigh(b, h, s, bank, pts):
        return nc.tensor.matmul(bank[:, (h % 4) * 128:(h % 4) * 128 + 128], b["vb"][:, s, h * DK:(h + 1) * DK],
                                pts[0], start=True, stop=True)

    attention(nc, c, "l3_attn", dict(heads=H, units=4, v_groups=(6, 7),
                                     schedule=[[("p", 0)], [("p", 1), ("p", 2), ("p", 3)], [("p", 4), ("p", 5)],
                                               [("p", 6), ("o", 0), ("p", 7)]],
                                      keys=128, dv=DK, proj_groups=8, weigh=weigh,
                                     key_chunks=[(0, 128)], proj=proj, copy=copy, scores=scores, first_feeds=True,
                                     unit_heads=lambda u: [2 * u + j for j in range(2)]), load)


def l3_cross_attention(nc, c, T):
    H, HD = 16, 8

    def load(sc):
        w = sc.sb("w_heads", [128, 3, 128])
        wo = sc.sb("wo", [128, 128])
        bo = sc.sb("bo", [1, 128])
        cur = sc.sb("tile", [128, 2, 128 + SC])
        q = sc.sb("q_t", [128, 2, 128])
        km = sc.sb("k_t", [128, 2, 4, SC])
        v = sc.sb("v", [SC, 2, 4, 4, 32])
        zeroed = sc.semaphore("zeroed")
        items = [(wo[:, :], T["L3_xattn_Wo"]), (bo[:, :], row(T["L3_xattn_bo"]))]
        for i, n in enumerate(("Wq", "Wk", "Wv")):
            for h in range(H):
                items.append((w[8 * h:8 * h + 8, i, 8 * h:8 * h + 8], T["L3_xattn_" + n]))
        b = loader(nc, sc, items)
        start = b["dma"]

        def prepare_pool(pool):
            nc.gpsimd.memset(v[:, :, :, :, :], 0.0)
            nc.gpsimd.memset(w[:, :, :], 0.0).then_inc(zeroed, 1)

        def dma(sp):
            sp.wait_ge(zeroed, 1)
            start(sp)

        b.update(w=w, cur=cur, q=q, km=km, vb=v, dma=dma,
                 prepare_pool=prepare_pool,
                 tiles=lambda t, s: [(cur[:, s, 0:128], c["nT"][:, bass.ds(t * 128, 128)]),
                                     (cur[:, s, 128:128 + SC], c["cT"][:, bass.ds(t * SC, SC)])],
                 wo=lambda m: wo[:, :], bo=bo[:, :])
        return b

    def proj(b, g, s, bank):
        tq, tk = b["cur"][:, s, 0:128], b["cur"][:, s, 128:128 + SC]
        if g == 0:
            nc.tensor.matmul(bank[:, 0:128], b["w"][:, 0, :], tq, start=True, stop=True)
            return nc.tensor.matmul(bank[:, 128:128 + SC], b["w"][:, 1, :], tk, start=True, stop=True)
        return nc.tensor.matmul(bank[0:SC, 0:128], tk, b["w"][:, 2, :], start=True, stop=True)

    def copy(b, g, s, bank):
        if g == 0:
            nc.scalar.activation(b["q"][:, s, :], bank[:, 0:128], ACT.Copy, scale=float(D) ** -0.5)
            for j in range(4):
                last = nc.scalar.activation(b["km"][:, s, j, :], bank[:, 128:128 + SC], ACT.Copy,
                                            scale=c["mask8"][:, j:j + 1])
            return last
        return spread_values(nc, b["vb"], s, bank[0:SC, 0:128], SC)

    def scores(b, u, s, bank):
        r = slice(32 * u, 32 * u + 32)
        for j in range(4):
            last = nc.tensor.matmul(bank[:, j * SC:(j + 1) * SC], b["q"][r, s, :], b["km"][r, s, j, :],
                                    start=True, stop=True)
        return last

    attention(nc, c, "l3_xattn", dict(heads=H, units=4, v_groups=(1,), schedule=[[("p", 0)], [], [], [("p", 1), ("o", 0)]],
                                       keys=SC, dv=HD, proj_groups=2, weigh=lambda *a: weigh_small(nc, *a),
                                      key_chunks=[(0, SC)], proj=proj, copy=copy, scores=scores,
                                      unit_heads=lambda u: [4 * u + j for j in range(4)]), load)


def top_two(nc, dve, sc, w, val, n, m, first_of, part):
    count = [0]

    def then(ins):
        count[0] += 1
        ins.then_inc(part, 1)
        dve.wait_ge(part, count[0])

    def bc(ap):
        return ap.unsqueeze(2).to_broadcast([128, n, m])
    src = val
    for r in range(2):
        then(nc.vector.tensor_reduce(w["top"][:, r, 0:n], src, AX.X, ALU.max))
        then(nc.vector.tensor_tensor(w["eq"], src, bc(w["top"][:, r, 0:n]), ALU.is_equal))
        then(nc.vector.tensor_scalar(w["eq"], w["eq"], -float(m), float(m), ALU.mult, ALU.add))
        then(nc.vector.tensor_tensor(w["eq"], w["eq"], first_of, ALU.add))
        then(nc.vector.tensor_reduce(w["index"][:, r, 0:n], w["eq"], AX.X, ALU.min))
        then(nc.vector.tensor_tensor(w["hot"][r], first_of, bc(w["index"][:, r, 0:n]), ALU.is_equal))
        if r == 0:
            then(nc.vector.tensor_scalar(w["rest"], w["hot"][0], -1.0e38, None, ALU.mult))
            then(nc.vector.tensor_tensor(w["rest"], w["rest"], val, ALU.add))
            src = w["rest"]
    return then


def route_and_mix(nc, c, T, name, E, sigmoid_first, router, bias, experts, shared):
    NE = E + (1 if shared else 0)
    G, N = 4, B // 4
    with Scope(nc, name) as sc:
        wg = sc.sb("w_gate", [128, NE, 256])
        wu = sc.sb("w_up", [128, NE, 256])
        wd = sc.sb("w_down", [128, NE, 2, 128])
        weights = sc.sb("token_weights", [128, B, NE])
        cur = sc.sb("tiles", [128, 2, 512])
        items = []
        for e in range(NE):
            g, u, d = experts(e)
            items += [(wg[:, e, :], g), (wu[:, e, :], u), (wd[:, e, :, :], d.rearrange("(i p) d -> p i d", p=128))]
        b = loader(nc, sc, items)

        with Scope(nc, name + "_route") as rt:
            rw = rt.sb("router", [128, E])
            rb = rt.sb("router_bias", [1, E])
            iota_i = rt.sb("index_int", [128, B, E], I32)
            iota = rt.sb("index", [128, B, E])
            val = rt.sb("values", [128, B, E])
            w = dict(top=rt.sb("top", [128, 2, B]), index=rt.sb("top_index", [128, 2, B]),
                     eq=rt.sb("eq", [128, B, E])[:, :, :], rest=rt.sb("rest", [128, B, E])[:, :, :],
                     hot=[rt.sb(f"hot{i}", [128, B, E])[:, :, :] for i in range(2)])
            gates = rt.sb("gates", [128, 2, B])
            total = rt.sb("total", [128, B])
            R_ps = rt.ps("logits", [128, B * E])
            r_items = [(rw[:, :], router)] + ([(rb[:, :], bias)] if bias is not None else [])
            rl = loader(nc, rt, r_items)
            tile_ready = rt.counter("tile_ready")
            routed = rt.counter("routed")
            index_made, values_ready, top_part, gates_ready, sig_done = (
                rt.semaphore(n) for n in ("index_made", "values_ready", "top_part", "gates_ready", "sig_done"))
            rt.begin()
            with nc.Block() as block:
                @block.sync
                def _(sp):
                    rl["dma"](sp)
                    b["dma"](sp)

                @block.gpsimd
                def _(pool):
                    nc.gpsimd.iota(iota_i[:, :, :], pattern=[[0, B], [1, E]], base=0, channel_multiplier=0) \
                        .then_inc(index_made, 1)
                    with pool.Fori(0, N // 2) as it:
                        for s in range(2):
                            t = it * 2 + s
                            routed.wait_steps(pool, it * 2)
                            settle(pool, rt.passed)
                            nc.gpsimd.tensor_copy(cur[:, s, :], c["nT"][:, bass.ds(t * 512, 512)]) \
                                .then_inc(tile_ready.sem, 1)

                @block.tensor
                def _(pe):
                    pe.wait_ge(rl["loaded"], 16 * rl["loads"])
                    with pe.Fori(0, N // 2) as it:
                        for s in range(2):
                            t = it * 2 + s
                            tile_ready.wait(pe, t, 1)
                            settle(pe, rt.passed)
                            for j in range(G):
                                o = R_ps[:, bass.ds(t * (G * E) + j * E, E)]
                                last = nc.tensor.matmul(o, cur[:, s, j * 128:(j + 1) * 128], rw[:, :],
                                                        start=True, stop=bias is None)
                                if bias is not None:
                                    last = nc.tensor.matmul(o, c["ones"][0:1, :], rb[:, :], start=False, stop=True)
                            last.then_inc(routed.sem, 1)

                @block.scalar
                def _(act):
                    act.wait_ge(routed.sem, N + 1)
                    flat = val[:, :, :].rearrange("p b e -> p (b e)")
                    nc.scalar.activation(flat, R_ps[:, :], ACT.Sigmoid if sigmoid_first else ACT.Copy) \
                        .then_inc(values_ready, 1)
                    if not sigmoid_first:
                        act.wait_ge(gates_ready, 1)
                        nc.scalar.activation(gates[:, :, :], w["top"][:, :, :], ACT.Sigmoid).then_inc(sig_done, 1)

                @block.vector
                def _(dve):
                    dve.wait_ge(index_made, 1)
                    nc.vector.tensor_copy(iota[:, :, :], iota_i[:, :, :]).then_inc(index_made, 1)
                    dve.wait_ge(index_made, 2)
                    dve.wait_ge(values_ready, 1)
                    then = top_two(nc, dve, rt, w, val[:, :, :], B, E, iota[:, :, :], top_part)
                    g = w["top"]
                    if not sigmoid_first:
                        then(nc.vector.tensor_copy(total[:, :], g[:, 0, :]))
                        nc.vector.tensor_copy(total[:, :], g[:, 1, :]).then_inc(gates_ready, 1)
                        dve.wait_ge(gates_ready, 1)
                        dve.wait_ge(sig_done, 1)
                        g = gates
                    then(nc.vector.tensor_tensor(total[:, :], g[:, 0, :], g[:, 1, :], ALU.add))
                    if not sigmoid_first:
                        then(nc.vector.tensor_scalar(total[:, :], total[:, :], 1e-10, None, ALU.add))
                    then(nc.vector.reciprocal(total[:, :], total[:, :]))
                    for r in range(2):
                        then(nc.vector.tensor_tensor(g[:, r, :], g[:, r, :], total[:, :], ALU.mult))
                        then(nc.vector.tensor_tensor(w["hot"][r], w["hot"][r],
                                                     g[:, r, :].unsqueeze(2).to_broadcast([128, B, E]), ALU.mult))
                    if shared:
                        then(nc.vector.memset(weights[:, :, E:NE], 1.0))
                    then(nc.vector.tensor_tensor(weights[:, :, 0:E], w["hot"][0], w["hot"][1], ALU.add))

        SG = sc.sb("silu", [128, 2, 512])
        Hb = sc.sb("hidden", [128, 2, 2, 512])
        A = sc.sb("weighted_out", [128, 2, 512])
        gu = [[sc.ps(f"{n}{i}", [128, 512]) for n in ("gate", "up")] for i in range(2)]
        Yp = [sc.ps(f"down{i}", [128, 512]) for i in range(2)]
        tile_ready = sc.counter("tile_ready")
        hidden_done = sc.counter("gate_up_done", 2 * NE)
        silu_done = sc.counter("silu_done", 2 * NE)
        h_done = sc.counter("h_done", 2 * NE)
        down_done = sc.counter("down_done", NE)
        weighted = sc.counter("weighted", NE)
        added = sc.counter("added", NE)

        def two_back(sig, eng, t, n):
            if n >= 2:
                sig.wait(eng, t, n - 1)
            else:
                sig.wait_steps(eng, t)

        sc.begin()
        with nc.Block() as block:
            @block.gpsimd
            def _(pool):
                def tiles(t, s):
                    nc.gpsimd.tensor_copy(cur[:, s, :], c["nT"][:, bass.ds(t * 512, 512)]).then_inc(tile_ready.sem, 1)
                with pool.Fori(0, N // 2) as it:
                    for s in range(2):
                        t = it * 2 + s
                        hidden_done.wait_steps(pool, it * 2)
                        settle(pool, sc.passed)
                        tiles(t, s)
                        for e in range(NE):
                            weighted.wait(pool, t, e + 1)
                            added.wait(pool, t, e)
                            settle(pool, sc.passed)
                            xs = c["x"][:, bass.ds(t * G, G), :]
                            nc.gpsimd.tensor_tensor(xs, xs, A[:, e % 2, :].rearrange("p (g d) -> p g d", g=G),
                                                    ALU.add).then_inc(added.sem, 1)

            @block.tensor
            def _(pe):
                pe.wait_ge(b["loaded"], 16 * b["loads"])

                def up(t, s, n):
                    two_back(h_done, pe, t, n)
                    settle(pe, sc.passed)
                    e, i = n // 2, n % 2
                    for w_, o in ((wg, gu[n % 2][0]), (wu, gu[n % 2][1])):
                        last = nc.tensor.matmul(o[:, :], w_[:, e, i * 128:(i + 1) * 128], cur[:, s, :],
                                                start=True, stop=True)
                    last.then_inc(hidden_done.sem, 1)

                def down(t, e):
                    h_done.wait(pe, t, 2 * e + 2)
                    two_back(weighted, pe, t, e)
                    settle(pe, sc.passed)
                    for j in range(G):
                        for i in range(2):
                            last = nc.tensor.matmul(Yp[e % 2][:, j * 128:(j + 1) * 128],
                                                    Hb[:, e % 2, i, j * 128:(j + 1) * 128], wd[:, e, i, :],
                                                    start=(i == 0), stop=(i == 1))
                    last.then_inc(down_done.sem, 1)

                with pe.Fori(0, N // 2) as it:
                    for s in range(2):
                        t = it * 2 + s
                        tile_ready.wait(pe, t, 1)
                        for e in range(NE):
                            up(t, s, 2 * e)
                            up(t, s, 2 * e + 1)
                            if e:
                                down(t, e - 1)
                        down(t, NE - 1)

            @block.scalar
            def _(act):
                with act.Fori(0, N // 2) as it:
                    for s in range(2):
                        t = it * 2 + s
                        for n in range(2 * NE):
                            hidden_done.wait(act, t, n + 1)
                            two_back(h_done, act, t, n)
                            nc.scalar.activation(SG[:, n % 2, :], gu[n % 2][0][:, :], ACT.Silu) \
                                .then_inc(silu_done.sem, 1)

            @block.vector
            def _(dve):
                def weigh(t, e):
                    down_done.wait(dve, t, e + 1)
                    two_back(added, dve, t, e)
                    nc.vector.tensor_tensor(A[:, e % 2, :].rearrange("p (g d) -> p g d", g=G),
                                            Yp[e % 2][:, :].rearrange("p (g d) -> p g d", g=G),
                                            weights[:, bass.ds(t * G, G), e:e + 1].to_broadcast([128, G, 128]),
                                            ALU.mult).then_inc(weighted.sem, 1)
                with dve.Fori(0, N // 2) as it:
                    for s in range(2):
                        t = it * 2 + s
                        for n in range(2 * NE):
                            e, i = n // 2, n % 2
                            silu_done.wait(dve, t, n + 1)
                            two_back(down_done, dve, t, e)
                            nc.vector.tensor_tensor(Hb[:, e % 2, i, :], SG[:, n % 2, :], gu[n % 2][1][:, :], ALU.mult) \
                                .then_inc(h_done.sem, 1)
                            if i and e:
                                weigh(t, e - 1)
                        weigh(t, NE - 1)


def l2_ffn(nc, c, T):
    def experts(e):
        if e == 8:
            return T["L2_ffn_shared_gate"], T["L2_ffn_shared_up"], T["L2_ffn_shared_down"]
        return T["L2_ffn_gate_w"][e], T["L2_ffn_up_w"][e], T["L2_ffn_down_w"][e]
    route_and_mix(nc, c, T, "l2_ffn", 8, True, T["L2_ffn_router_w"], row(T["L2_ffn_routing_bias"]), experts, True)


def l3_ffn(nc, c, T):
    route_and_mix(nc, c, T, "l3_ffn", 8, False, T["L3_ffn_router_w"], None,
                  lambda e: (T["L3_ffn_w_gate"][e], T["L3_ffn_w_up"][e], T["L3_ffn_w_down"][e]), False)


def l1_attention(nc, c, T):
    G, N = 4, B // 4
    scale = float(D) ** -0.5
    with Scope(nc, "l1_attn") as sc:
        w = sc.sb("w", [128, 3, 128])
        bq = sc.sb("bq", [128, 1])
        bk = sc.sb("bk", [128, 1])
        bv = sc.sb("bv", [1, 128])
        bq_s = sc.sb("bq_scaled", [128, 1])
        causal = sc.sb("causal", [128, 128])
        cur = sc.sb("tiles", [128, 2, 512])
        q = sc.sb("q_t", [128, 2, 512])
        k = sc.sb("k_t", [128, 2, 512])
        v = sc.sb("v", [128, 2, G, 128])
        Sm = sc.sb("masked", [128, 2, G, 128])
        P = sc.sb("probs", [128, 2, G, 128])
        nmax = sc.sb("neg_max", [128, 2, G])
        sums = sc.sb("sums", [128, 2, G])
        rs = sc.sb("rsum", [128, 2, G])
        q_ps, k_ps, v_ps = (sc.ps(n, [128, 512]) for n in ("q_ps", "k_ps", "v_ps"))
        s_ps, o_ps = sc.ps("s_ps", [128, 512]), sc.ps("o_ps", [128, 512])
        items = [(w[:, i, :], T["L1_attn_W" + n]) for i, n in enumerate("qkv")]
        items += [(bq[:, :], column(T["L1_attn_bq"])), (bk[:, :], column(T["L1_attn_bk"])), (bv[:, :], row(T["L1_attn_bv"]))]
        b = loader(nc, sc, items)
        names = ("tile_ready", "qk_done", "v_done", "qk_copied", "scored", "masked", "maxed", "exped", "inverted",
                 "v_scaled", "out_done", "added")
        tile_ready, qk_done, v_done, qk_copied, scored, masked_, maxed, exped, inverted, v_scaled, out_done, added = (
            sc.counter(n) for n in names)
        causal_made, bias_ready = sc.semaphore("causal_made"), sc.semaphore("bias_ready")

        def pairs(eng, body):
            with eng.Fori(0, N // 2) as it:
                for s in range(2):
                    body(it * 2 + s, s)

        sc.begin()
        with nc.Block() as block:
            @block.sync
            def _(sp):
                b["dma"](sp)

            @block.gpsimd
            def _(pool):
                nc.gpsimd.memset(causal[:, :], 0.0).then_inc(causal_made, 1)
                pool.wait_ge(causal_made, 1)
                nc.gpsimd.affine_select(out=causal[:, :], in_=causal[:, :], compare_op=ALU.is_ge, fill=-3.0e38,
                                        base=0, pattern=[[1, 128]], channel_multiplier=-1).then_inc(causal_made, 1)

                def body(t, s):
                    v_done.wait_steps(pool, t - s)
                    settle(pool, sc.passed)
                    nc.gpsimd.tensor_copy(cur[:, s, :], c["nT"][:, bass.ds(t * 512, 512)]).then_inc(tile_ready.sem, 1)
                pairs(pool, body)

            @block.tensor
            def _(pe):
                pe.wait_ge(b["loaded"], 16 * b["loads"])

                def body(t, s):
                    tile_ready.wait(pe, t, 1)
                    qk_copied.wait_steps(pe, t)
                    settle(pe, sc.passed)
                    nc.tensor.matmul(q_ps[:, :], w[:, 0, :], cur[:, s, :], start=True, stop=True)
                    nc.tensor.matmul(k_ps[:, :], w[:, 1, :], cur[:, s, :], start=True, stop=True) \
                        .then_inc(qk_done.sem, 1)
                    v_scaled.wait_steps(pe, t)
                    settle(pe, sc.passed)
                    for j in range(G):
                        o = v_ps[:, j * 128:(j + 1) * 128]
                        nc.tensor.matmul(o, cur[:, s, j * 128:(j + 1) * 128], w[:, 2, :], start=True, stop=False)
                        last = nc.tensor.matmul(o, c["ones"][0:1, :], bv[:, :], start=False, stop=True)
                    last.then_inc(v_done.sem, 1)
                    qk_copied.wait(pe, t, 1)
                    masked_.wait_steps(pe, t)
                    settle(pe, sc.passed)
                    for j in range(G):
                        r = slice(j * 128, (j + 1) * 128)
                        last = nc.tensor.matmul(s_ps[:, r], k[:, s, r], q[:, s, r], start=True, stop=True)
                    last.then_inc(scored.sem, 1)
                    v_scaled.wait(pe, t, 1)
                    added.wait_steps(pe, t)
                    settle(pe, sc.passed)
                    for j in range(G):
                        last = nc.tensor.matmul(o_ps[:, j * 128:(j + 1) * 128], P[:, s, j, :], v[:, s, j, :],
                                                start=True, stop=True)
                    last.then_inc(out_done.sem, 1)
                pairs(pe, body)

            @block.scalar
            def _(act):
                act.wait_ge(b["loaded"], 16 * b["loads"])
                nc.scalar.activation(bq_s[:, :], bq[:, :], ACT.Copy, scale=scale).then_inc(bias_ready, 1)
                act.wait_ge(bias_ready, 1)

                def body(t, s):
                    qk_done.wait(act, t, 1)
                    scored.wait_steps(act, t)
                    settle(act, sc.passed)
                    nc.scalar.activation(q[:, s, :], q_ps[:, :], ACT.Identity, bias=bq_s[:, 0:1], scale=scale)
                    nc.scalar.activation(k[:, s, :], k_ps[:, :], ACT.Identity, bias=bk[:, 0:1]) \
                        .then_inc(qk_copied.sem, 1)
                    maxed.wait(act, t, 1)
                    out_done.wait_steps(act, t)
                    settle(act, sc.passed)
                    for j in range(G):
                        last = nc.scalar.activation(P[:, s, j, :], Sm[:, s, j, :], ACT.Exp, bias=nmax[:, s, j:j + 1],
                                                    accum_out=sums[:, s, j:j + 1])
                    last.then_inc(exped.sem, 1)
                pairs(act, body)

            @block.vector
            def _(dve):
                dve.wait_ge(causal_made, 2)

                def body(t, s):
                    scored.wait(dve, t, 1)
                    nc.vector.tensor_tensor(Sm[:, s, :, :], s_ps[:, :].rearrange("p (g i) -> p g i", g=G),
                                            causal[:, :].unsqueeze(1).to_broadcast([128, G, 128]), ALU.add) \
                        .then_inc(masked_.sem, 1)
                    masked_.wait(dve, t, 1)
                    nc.vector.tensor_reduce(nmax[:, s, :], Sm[:, s, :, :], AX.X, ALU.max, negate=True) \
                        .then_inc(maxed.sem, 1)
                    exped.wait(dve, t, 1)
                    nc.vector.reciprocal(rs[:, s, :], sums[:, s, :]).then_inc(inverted.sem, 1)
                    inverted.wait(dve, t, 1)
                    v_done.wait(dve, t, 1)
                    nc.vector.tensor_tensor(v[:, s, :, :], v_ps[:, :].rearrange("p (g i) -> p g i", g=G),
                                            rs[:, s, :].unsqueeze(2).to_broadcast([128, G, 128]), ALU.mult) \
                        .then_inc(v_scaled.sem, 1)
                    out_done.wait(dve, t, 1)
                    settle(dve, sc.passed)
                    xs = c["x"][:, bass.ds(t * G, G), :]
                    nc.vector.tensor_tensor(xs, o_ps[:, :].rearrange("p (g i) -> p g i", g=G), xs, ALU.add) \
                        .then_inc(added.sem, 1)
                pairs(dve, body)


def l2_attention(nc, c, T):
    G, N, H = 4, B // 4, 16
    const = 1.0 / float(np.sqrt(np.float32(D // H))) / D
    with Scope(nc, "l2_attn") as sc:
        w = sc.sb("w", [128, 4, 128])
        bo = sc.sb("bo", [128, 128])
        cur = sc.sb("tiles", [128, 2, 512])
        e_ = sc.sb("exps", [128, 2, 2, G, 128])
        et = sc.sb("exps_t", [128, 2, 2, G, 128])
        v = sc.sb("v", [128, 2, G, 128])
        kv = sc.sb("kv", [128, 2, G, 128])
        yt = sc.sb("y_t", [128, 2, 512])
        out = sc.sb("out", [128, 2, G, 128])
        nmax = sc.sb("neg_max", [128, 2, 2, G])
        sums = sc.sb("sums", [128, 2, 2, G])
        rs = sc.sb("rsum", [128, 2, 2, G])
        names = ("q_ps", "k_ps", "v_ps", "qt_ps", "kt_ps", "kv_ps", "y_ps", "o_ps")
        q_ps, k_ps, v_ps, qt_ps, kt_ps, kv_ps, y_ps, o_ps = (sc.ps(n, [128, 512]) for n in names)
        b = loader(nc, sc, [(w[:, i, :], T["L2_attn_W" + n]) for i, n in enumerate("qkvo")] +
                   [(bo[:, :], row(T["L2_attn_bo"]).to_broadcast([128, 128]))])
        names = ("tile_ready", "projected", "maxed", "exped", "v_copied", "turned", "turned_copied", "inverted",
                 "kv_done", "kv_copied", "y_done", "y_copied", "out_done", "out_scaled")
        (tile_ready, projected, maxed, exped, v_copied, turned, turned_copied, inverted, kv_done, kv_copied, y_done,
         y_copied, out_done, out_scaled) = (sc.counter(n) for n in names)
        added = sc.counter("added", 2)
        scaled = sc.counter("divisors_scaled")

        def pairs(eng, front, back):
            front(0, 0)
            with eng.Fori(0, (N - 2) // 2) as it:
                for s in range(2):
                    t = it * 2 + 1 + s
                    front(t, (1 + s) % 2)
                    back(it * 2 + s, s)
            front(N - 1, (N - 1) % 2)
            back(N - 2, (N - 2) % 2)
            back(N - 1, (N - 1) % 2)

        sc.begin()
        with nc.Block() as block:
            @block.sync
            def _(sp):
                b["dma"](sp)

            @block.gpsimd
            def _(pool):
                pool.wait_ge(b["loaded"], 16 * b["loads"])

                def front(t, s):
                    if not isinstance(t, int) or t >= 2:
                        projected.wait_steps(pool, t - 1)
                    settle(pool, sc.passed)
                    nc.gpsimd.tensor_copy(cur[:, s, :], c["nT"][:, bass.ds(t * 512, 512)]).then_inc(tile_ready.sem, 1)

                def back(t, s):
                    out_scaled.wait(pool, t, 1)
                    settle(pool, sc.passed)
                    nc.gpsimd.tensor_tensor(out[:, s, :, :], out[:, s, :, :],
                                            bo[:, :].unsqueeze(1).to_broadcast([128, G, 128]), ALU.add) \
                        .then_inc(added.sem, 1)
                    added.wait(pool, t, 1)
                    settle(pool, sc.passed)
                    xs = c["x"][:, bass.ds(t * G, G), :]
                    nc.gpsimd.tensor_tensor(xs, xs, out[:, s, :, :], ALU.add).then_inc(added.sem, 1)
                pairs(pool, front, back)

            @block.tensor
            def _(pe):
                pe.wait_ge(b["loaded"], 16 * b["loads"])

                def front(t, s):
                    tile_ready.wait(pe, t, 1)
                    exped.wait_steps(pe, t)
                    v_copied.wait_steps(pe, t)
                    settle(pe, sc.passed)
                    nc.tensor.matmul(k_ps[:, :], w[:, 1, :], cur[:, s, :], start=True, stop=True)
                    for i, o in ((0, q_ps), (2, v_ps)):
                        for j in range(G):
                            last = nc.tensor.matmul(o[:, j * 128:(j + 1) * 128], cur[:, s, j * 128:(j + 1) * 128],
                                                    w[:, i, :], start=True, stop=True)
                    last.then_inc(projected.sem, 1)

                def back(t, s):
                    exped.wait(pe, t, 1)
                    turned_copied.wait_steps(pe, t)
                    settle(pe, sc.passed)
                    for i, o in ((0, qt_ps), (1, kt_ps)):
                        for j in range(G):
                            last = nc.tensor.transpose(o[:, j * 128:(j + 1) * 128], e_[:, s, i, j, :], c["ident"][:, :])
                    last.then_inc(turned.sem, 1)
                    turned_copied.wait(pe, t, 1)
                    v_copied.wait(pe, t, 1)
                    kv_copied.wait_steps(pe, t)
                    settle(pe, sc.passed)
                    for j in range(G):
                        last = nc.tensor.matmul(kv_ps[:, j * 128:(j + 1) * 128], et[:, s, 1, j, :], v[:, s, j, :],
                                                start=True, stop=True)
                    last.then_inc(kv_done.sem, 1)
                    kv_copied.wait(pe, t, 1)
                    y_copied.wait_steps(pe, t)
                    settle(pe, sc.passed)
                    for j in range(G):
                        last = nc.tensor.matmul(y_ps[:, j * 128:(j + 1) * 128], kv[:, s, j, :], et[:, s, 0, j, :],
                                                start=True, stop=True)
                    last.then_inc(y_done.sem, 1)
                    y_copied.wait(pe, t, 1)
                    out_scaled.wait_steps(pe, t)
                    settle(pe, sc.passed)
                    for j in range(G):
                        last = nc.tensor.matmul(o_ps[:, j * 128:(j + 1) * 128], yt[:, s, j * 128:(j + 1) * 128],
                                                w[:, 3, :], start=True, stop=True)
                    last.then_inc(out_done.sem, 1)
                pairs(pe, front, back)

            @block.scalar
            def _(act):
                def front(t, s):
                    maxed.wait(act, t, 1)
                    if not isinstance(t, int) or t >= 2:
                        turned.wait_steps(act, t - 1)
                        inverted.wait_steps(act, t - 1)
                        kv_done.wait_steps(act, t - 1)
                    settle(act, sc.passed)
                    for i, o in ((0, q_ps), (1, k_ps)):
                        for j in range(G):
                            last = nc.scalar.activation(e_[:, s, i, j, :], o[:, j * 128:(j + 1) * 128], ACT.Exp,
                                                        bias=nmax[:, s, i, j:j + 1], accum_out=sums[:, s, i, j:j + 1])
                    last.then_inc(exped.sem, 1)
                    nc.scalar.activation(v[:, s, :, :], v_ps[:, :], ACT.Copy).then_inc(v_copied.sem, 1)

                def back(t, s):
                    y_done.wait(act, t, 1)
                    nc.scalar.activation(yt[:, s, :], y_ps[:, :], ACT.Copy).then_inc(y_copied.sem, 1)
                pairs(act, front, back)

            @block.vector
            def _(dve):
                def front(t, s):
                    projected.wait(dve, t, 1)
                    settle(dve, sc.passed)
                    for i, o in ((0, q_ps), (1, k_ps)):
                        last = nc.vector.tensor_reduce(nmax[:, s, i, :], o[:, :].rearrange("p (g f) -> p g f", g=G),
                                                       AX.X, ALU.max, negate=True)
                    last.then_inc(maxed.sem, 1)

                def back(t, s):
                    exped.wait(dve, t, 1)
                    nc.vector.reciprocal(rs[:, s, :, :], sums[:, s, :, :]).then_inc(inverted.sem, 1)
                    inverted.wait(dve, t, 1)
                    nc.vector.tensor_scalar(rs[:, s, 1, :], rs[:, s, 1, :], const, None, ALU.mult) \
                        .then_inc(scaled.sem, 1)
                    turned.wait(dve, t, 1)
                    for i, o in ((0, qt_ps), (1, kt_ps)):
                        last = nc.vector.tensor_copy(et[:, s, i, :, :], o[:, :].rearrange("p (g f) -> p g f", g=G))
                    last.then_inc(turned_copied.sem, 1)
                    kv_done.wait(dve, t, 1)
                    scaled.wait(dve, t, 1)
                    nc.vector.tensor_tensor(kv[:, s, :, :], kv_ps[:, :].rearrange("p (g f) -> p g f", g=G),
                                            rs[:, s, 1, :].unsqueeze(2).to_broadcast([128, G, 128]), ALU.mult) \
                        .then_inc(kv_copied.sem, 1)
                    out_done.wait(dve, t, 1)
                    if not isinstance(t, int) or t >= 2:
                        added.wait_steps(dve, t - s)
                    nc.vector.tensor_tensor(out[:, s, :, :], o_ps[:, :].rearrange("p (g f) -> p g f", g=G),
                                            rs[:, s, 0, :].unsqueeze(2).to_broadcast([128, G, 128]), ALU.mult) \
                        .then_inc(out_scaled.sem, 1)
                pairs(dve, front, back)


def l2_cross_attention(nc, c, T):
    H, HD, I = 8, 64, 512
    NK = SC + 1
    with Scope(nc, "l2_xattn") as sc:
        wq = sc.sb("wq", [128, I])
        wkv = sc.sb("wkv", [128, 2 * I])
        wo = sc.sb("wo", [128, 4, 128])
        gains = sc.sb("gains", [128, 4, I])
        null_k = sc.sb("null_k", [1, H, HD])
        null_v = sc.sb("null_v", [1, H, HD])
        at_null = sc.sb("at_null", [1, NK])
        cur = sc.sb("tile", [128, 2, 128])
        ctx = sc.sb("context_tile", [128, 2, NK])
        q = sc.sb("q", [128, 3, I])
        qm = sc.sb("q_shifted", [128, I])
        ek = sc.sb("k_exps", [128, 4, NK])
        v = sc.sb("v", [NK, I])
        qt = sc.sb("q_t", [128, 4, 128])
        kt = sc.sb("k_t", [NK, I])
        kv = sc.sb("kv", [128, 4, 128])
        o = sc.sb("o", [128, 4, I])
        ot = sc.sb("o_t", [128, 4, 128])
        st = sc.sb("stats", [128, 2, 6])
        mv = sc.sb("mean_var", [128, 2, 2])
        ve = sc.sb("var_eps", [128, 2])
        rstd = sc.sb("rstd", [128, 2])
        kmax, ksum, krs = sc.sb("k_neg_max", [128, 4]), sc.sb("k_sums", [128, 4]), sc.sb("k_rsum", [128, 4])
        qmax, qsum, qrs = sc.sb("q_neg_max", [128, H]), sc.sb("q_sums", [128, H]), sc.sb("q_rsum", [128, H])
        q_ps, k_ps, v_ps, t_ps, kt_ps, kv_ps, o_ps, y_ps = (
            sc.ps(n, [128, 512]) for n in ("q_ps", "k_ps", "v_ps", "t_ps", "kt_ps", "kv_ps", "o_ps", "y_ps"))

        def rep(v_):
            return v_.unsqueeze(1).to_broadcast([1, H, HD])
        items = [(wq[:, :], T["L2_xattn_Wq"]), (wkv[:, :], T["L2_xattn_Wkv"]),
                 (wo[:, :, :], T["L2_xattn_Wout"].rearrange("(m p) d -> p m d", p=128)),
                 (null_k[:, :, :], rep(T["L2_xattn_null_kv"][0:1, :])), (null_v[:, :, :], rep(T["L2_xattn_null_kv"][1:2, :]))]
        for i, n in enumerate(("ln_q_g", "ln_q_b", "ln_out_g", "ln_out_b")):
            items.append((gains[:, i, :], row(T["L2_xattn_" + n]).to_broadcast([128, I])))
        b = loader(nc, sc, items)
        names = ("tile_ready", "projected", "q_normed", "q_gained", "q_shifted", "q_exped", "k_maxed", "k_exped",
                 "v_copied", "q_turned", "k_turned", "qt_copied", "kt_copied", "kv_done", "kv_copied", "o_done",
                 "o_scaled", "o_normed", "o_gained", "o_turned", "ot_copied", "y_done", "added", "q_summed", "k_inverted")
        (tile_ready, projected, q_normed, q_gained, q_shifted, q_exped, k_maxed, k_exped, v_copied, q_turned,
         k_turned, qt_copied, kt_copied, kv_done, kv_copied, o_done, o_scaled, o_normed, o_gained, o_turned,
         ot_copied, y_done, added, q_summed, k_inverted) = (sc.counter(n) for n in names)
        stats = sc.counter("stats", 4)
        var_ready = sc.counter("var_ready", 2)
        rstd_ready = sc.counter("rstd_ready", 2)
        gain_part = sc.counter("gain_part", 2)
        q_maxed = sc.counter("q_maxed")
        q_inverted = sc.counter("q_inverted", 2)
        zeroed = sc.semaphore("zeroed")

        def split(eng, front, back):
            front(0, 0)
            with eng.Fori(0, (B - 2) // 2) as it:
                for s in range(2):
                    back(it * 2 + s, s, lambda: front(it * 2 + s + 1, 1 - s))
            back(B - 2, 0, lambda: front(B - 1, 1))
            back(B - 1, 1, lambda: None)

        sc.begin()
        with nc.Block() as block:
            @block.sync
            def _(sp):
                b["dma"](sp)

            @block.gpsimd
            def _(pool):
                nc.gpsimd.memset(ctx[:, :, :], 0.0)
                nc.gpsimd.memset(kv[:, :, :], 0.0)
                nc.gpsimd.memset(at_null[:, :], 0.0).then_inc(zeroed, 1)
                pool.wait_ge(zeroed, 1)
                nc.gpsimd.memset(at_null[:, SC:NK], 1.0).then_inc(zeroed, 1)
                pool.wait_ge(b["loaded"], 16 * b["loads"])

                def tiles(t, s):
                    if not isinstance(t, int) or t >= 2:
                        projected.wait_steps(pool, t - 1)
                    settle(pool, sc.passed)
                    nc.gpsimd.tensor_copy(cur[:, s, :], c["nT"][:, bass.ds(t * 128, 128)])
                    nc.gpsimd.tensor_copy(ctx[:, s, 0:SC], c["cT"][:, bass.ds(t * SC, SC)]) \
                        .then_inc(tile_ready.sem, 1)

                def power(t, i):
                    var_ready.wait(pool, t, i + 1)
                    settle(pool, sc.passed)
                    nc.gpsimd.tensor_tensor(rstd[:, i:i + 1], ve[:, i:i + 1], c["neg_half"][:, 0:1], ALU.pow) \
                        .then_inc(rstd_ready.sem, 1)

                def gain(t, i, src, tmp, dst, ready, done):
                    ready.wait(pool, t, 1)
                    settle(pool, sc.passed)
                    nc.gpsimd.tensor_tensor(tmp, src, gains[:, 2 * i, :], ALU.mult).then_inc(gain_part.sem, 1)
                    gain_part.wait(pool, t, i + 1)
                    settle(pool, sc.passed)
                    nc.gpsimd.tensor_tensor(dst, tmp, gains[:, 2 * i + 1, :], ALU.add).then_inc(done.sem, 1)

                def front(t, s):
                    tiles(t, s)

                def back(t, s, ahead):
                    power(t, 0)
                    gain(t, 0, q[:, 0, :], q[:, 1, :], q[:, 1, :], q_normed, q_gained)
                    ahead()
                    power(t, 1)
                    gain(t, 1, o[:, 1, :], o[:, 2, :], o[:, 3, :], o_normed, o_gained)
                split(pool, front, back)

            @block.tensor
            def _(pe):
                pe.wait_ge(zeroed, 2)
                pe.wait_ge(b["loaded"], 16 * b["loads"])

                def front(t, s):
                    tile_ready.wait(pe, t, 1)
                    if not (isinstance(t, int) and t == 0):
                        q_normed.wait_steps(pe, t)
                        k_exped.wait_steps(pe, t)
                        v_copied.wait_steps(pe, t)
                    settle(pe, sc.passed)
                    nc.tensor.matmul(q_ps[:, :], cur[:, s, :], wq[:, :], start=True, stop=True)
                    for m in range(4):
                        nc.tensor.matmul(k_ps[:, m * NK:(m + 1) * NK], wkv[:, m * 128:(m + 1) * 128], ctx[:, s, :],
                                         start=True, stop=False)
                        nc.tensor.matmul(k_ps[:, m * NK:(m + 1) * NK], null_k[0:1, 2 * m:2 * m + 2, :]
                                         .rearrange("p h d -> p (h d)"), at_null[0:1, :], start=False, stop=True)
                    nc.tensor.matmul(v_ps[0:NK, :], ctx[:, s, :], wkv[:, I:2 * I], start=True, stop=False)
                    nc.tensor.matmul(v_ps[0:NK, :], at_null[0:1, :], null_v[0:1, :, :].rearrange("p h d -> p (h d)"),
                                     start=False, stop=True).then_inc(projected.sem, 1)

                def back(t, s, ahead):
                    k_exped.wait(pe, t, 1)
                    kt_copied.wait_steps(pe, t)
                    settle(pe, sc.passed)
                    for m in range(4):
                        last = nc.tensor.transpose(kt_ps[0:NK, m * 128:(m + 1) * 128], ek[:, m, :], c["ident"][:, :])
                    last.then_inc(k_turned.sem, 1)
                    kt_copied.wait(pe, t, 1)
                    v_copied.wait(pe, t, 1)
                    kv_copied.wait_steps(pe, t)
                    settle(pe, sc.passed)
                    for m in range(4):
                        r = slice(m * 128, (m + 1) * 128)
                        last = nc.tensor.matmul(kv_ps[:, r], kt[:, r], v[:, r], start=True, stop=True)
                    last.then_inc(kv_done.sem, 1)
                    q_exped.wait(pe, t, 1)
                    ot_copied.wait_steps(pe, t)
                    settle(pe, sc.passed)
                    for m in range(4):
                        r = slice(m * 128, (m + 1) * 128)
                        last = nc.tensor.transpose(t_ps[:, r], q[:, 2, r], c["ident"][:, :])
                    last.then_inc(q_turned.sem, 1)
                    qt_copied.wait(pe, t, 1)
                    kv_copied.wait(pe, t, 1)
                    o_scaled.wait_steps(pe, t)
                    settle(pe, sc.passed)
                    for m in range(4):
                        r = slice(m * 128, (m + 1) * 128)
                        last = nc.tensor.matmul(o_ps[:, r], qt[:, m, :], kv[:, m, :], start=True, stop=True)
                    last.then_inc(o_done.sem, 1)
                    ahead()
                    o_gained.wait(pe, t, 1)
                    qt_copied.wait(pe, t, 1)
                    settle(pe, sc.passed)
                    for m in range(4):
                        r = slice(m * 128, (m + 1) * 128)
                        last = nc.tensor.transpose(t_ps[:, r], o[:, 3, r], c["ident"][:, :])
                    last.then_inc(o_turned.sem, 1)
                    ot_copied.wait(pe, t, 1)
                    added.wait_steps(pe, t)
                    settle(pe, sc.passed)
                    for m in range(4):
                        last = nc.tensor.matmul(y_ps[:, 0:128], ot[:, m, :], wo[:, m, :], start=(m == 0), stop=(m == 3))
                    last.then_inc(y_done.sem, 1)
                split(pe, front, back)

            @block.scalar
            def _(act):
                def front(t, s):
                    k_maxed.wait(act, t, 1)
                    if not (isinstance(t, int) and t == 0):
                        k_turned.wait_steps(act, t)
                        k_inverted.wait_steps(act, t)
                        kv_done.wait_steps(act, t)
                    settle(act, sc.passed)
                    for m in range(4):
                        last = nc.scalar.activation(ek[:, m, :], k_ps[:, m * NK:(m + 1) * NK], ACT.Exp,
                                                    bias=kmax[:, m:m + 1], accum_out=ksum[:, m:m + 1])
                    last.then_inc(k_exped.sem, 1)
                    nc.scalar.activation(v[:, :], v_ps[0:NK, :], ACT.Copy).then_inc(v_copied.sem, 1)

                def back(t, s, ahead):
                    k_turned.wait(act, t, 1)
                    nc.scalar.activation(kt[:, :], kt_ps[0:NK, :], ACT.Copy).then_inc(kt_copied.sem, 1)
                    q_shifted.wait(act, t, 1)
                    q_summed.wait_steps(act, t)
                    settle(act, sc.passed)
                    nc.scalar.activation(q[:, 2, :], qm[:, :], ACT.Exp).then_inc(q_exped.sem, 1)
                    q_turned.wait(act, t, 1)
                    nc.scalar.activation(qt[:, :, :], t_ps[:, :], ACT.Copy).then_inc(qt_copied.sem, 1)
                    ahead()
                    o_turned.wait(act, t, 1)
                    nc.scalar.activation(ot[:, :, :], t_ps[:, :], ACT.Copy).then_inc(ot_copied.sem, 1)
                split(act, front, back)

            @block.vector
            def _(dve):
                def layer_norm(t, i, src, dst, done):
                    nc.vector.bn_stats(st[:, i, :], src).then_inc(stats.sem, 1)
                    stats.wait(dve, t, 2 * i + 1)
                    settle(dve, sc.passed)
                    nc.vector.bn_aggr(mv[:, i, :], st[:, i, :]).then_inc(stats.sem, 1)
                    stats.wait(dve, t, 2 * i + 2)
                    nc.vector.tensor_scalar(ve[:, i:i + 1], mv[:, i, 1:2], LN_EPS, None, ALU.add) \
                        .then_inc(var_ready.sem, 1)
                    rstd_ready.wait(dve, t, i + 1)
                    nc.vector.tensor_scalar(dst, src, mv[:, i, 0:1], rstd[:, i:i + 1], ALU.subtract, ALU.mult) \
                        .then_inc(done.sem, 1)

                def heads(ap):
                    return ap.rearrange("p (h d) -> p h d", h=H)

                def bc(ap):
                    return ap.unsqueeze(2).to_broadcast([128, H, HD])

                def front(t, s):
                    projected.wait(dve, t, 1)
                    if not (isinstance(t, int) and t == 0):
                        q_exped.wait_steps(dve, t)
                    nc.vector.tensor_reduce(kmax[:, :], k_ps[:, 0:4 * NK].rearrange("p (m k) -> p m k", m=4), AX.X,
                                            ALU.max, negate=True).then_inc(k_maxed.sem, 1)

                def back(t, s, ahead):
                    layer_norm(t, 0, q_ps[:, :], q[:, 0, :], q_normed)
                    k_exped.wait(dve, t, 1)
                    nc.vector.reciprocal(krs[:, :], ksum[:, :]).then_inc(k_inverted.sem, 1)
                    k_inverted.wait(dve, t, 1)
                    kv_done.wait(dve, t, 1)
                    o_done.wait_steps(dve, t)
                    for h in range(2):
                        r = slice(64 * h, 64 * h + 64)
                        last = nc.vector.tensor_tensor(
                            kv[r, :, r], kv_ps[r, :].rearrange("p (m e) -> p m e", m=4)[:, :, r],
                            krs[r, :].unsqueeze(2).to_broadcast([64, 4, 64]), ALU.mult)
                    last.then_inc(kv_copied.sem, 1)
                    q_gained.wait(dve, t, 1)
                    nc.vector.tensor_reduce(qmax[:, :], heads(q[:, 1, :]), AX.X, ALU.max).then_inc(q_maxed.sem, 1)
                    q_maxed.wait(dve, t, 1)
                    nc.vector.tensor_tensor(heads(qm[:, :]), heads(q[:, 1, :]), bc(qmax[:, :]), ALU.subtract) \
                        .then_inc(q_shifted.sem, 1)
                    q_exped.wait(dve, t, 1)
                    nc.vector.tensor_reduce(qsum[:, :], heads(q[:, 2, :]), AX.X, ALU.add).then_inc(q_summed.sem, 1)
                    q_summed.wait(dve, t, 1)
                    nc.vector.reciprocal(qrs[:, :], qsum[:, :]).then_inc(q_inverted.sem, 1)
                    q_inverted.wait(dve, t, 1)
                    nc.vector.tensor_scalar(qrs[:, :], qrs[:, :], 8.0, None, ALU.mult).then_inc(q_inverted.sem, 1)
                    q_inverted.wait(dve, t, 2)
                    o_done.wait(dve, t, 1)
                    nc.vector.tensor_tensor(heads(o[:, 0, :]), heads(o_ps[:, :]), bc(qrs[:, :]), ALU.mult) \
                        .then_inc(o_scaled.sem, 1)
                    ahead()
                    o_scaled.wait(dve, t, 1)
                    layer_norm(t, 1, o[:, 0, :], o[:, 1, :], o_normed)
                    y_done.wait(dve, t, 1)
                    settle(dve, sc.passed)
                    xs = c["x"][:, t, :]
                    nc.vector.tensor_tensor(xs, y_ps[:, 0:128], xs, ALU.add).then_inc(added.sem, 1)
                split(dve, front, back)


def l0_ffn(nc, c, T):
    QMAX, MAGIC = 127.0, 12582912.0
    I = 352
    CH = [(0, 128), (128, 128), (256, 96)]
    G, N = 4, B // 4
    with Scope(nc, "l0_ffn") as sc:
        wn = sc.sb("w_natural", [128, 9, 128])
        wi = sc.sb("w_whole", [128, 9, 128])
        w_t = sc.sb("w_t", [128, 9, 128], BF16)
        sw = sc.sb("w_scale", [128, 7])
        isw = sc.sb("w_scale_inv", [128, 7])
        diag = sc.sb("diagonal", [128, 128])
        down_scale = sc.sb("down_scale", [128, 128])
        clip = sc.sb("clip", [128, 2])
        mx = sc.sb("abs_max", [128, 4])
        amax = sc.sb("abs_max_all", [128, 2])
        act_scale = sc.sb("act_scale", [128, 2])
        inv_scale = sc.sb("act_scale_inv", [128, 2])
        both = sc.sb("both_scales", [128, 6])
        hid = sc.sb("hidden", [128, 3, B * 128])
        w_ps = [sc.ps(f"w_t{i}", [128, 512]) for i in range(3)]
        items = [(clip[:, 0:1], row(T["L0_ffn_clip_x"]).to_broadcast([128, 1])),
                 (clip[:, 1:2], row(T["L0_ffn_clip_down"]).to_broadcast([128, 1]))]
        for k, n in enumerate(("gate", "up")):
            for i, (r0, rn) in enumerate(CH):
                items.append((wn[0:rn, 3 * k + i, :], T["L0_ffn_w_" + n][r0:r0 + rn, :]))
        items.append((wn[:, 6:8, :], T["L0_ffn_w_down"][:, 0:256].rearrange("h (a i) -> h a i", a=2)))
        items.append((wn[:, 8, 0:96], T["L0_ffn_w_down"][:, 256:352]))
        b = loader(nc, sc, items)
        zeroed, turned, diag_made, clipped, all_max, prep, scaled = (
            sc.semaphore(n) for n in ("zeroed", "turned", "diag_made", "clip_ready", "all_max", "prepared", "scaled"))

        sc.begin()
        with nc.Block() as block:
            @block.sync
            def _(sp):
                sp.wait_ge(zeroed, 1)
                b["dma"](sp)

            @block.gpsimd
            def _(pool):
                nc.gpsimd.memset(mx[:, :], 0.0)
                nc.gpsimd.memset(wn[:, :, :], 0.0).then_inc(zeroed, 1)
                pool.wait_ge(scaled, 1)
                nc.gpsimd.partition_all_reduce(amax[:, 0:1], mx[:, 0:1], 128, REDUCE_MAX) \
                    .then_inc(all_max, 1)

            @block.scalar
            def _(act):
                act.wait_ge(b["loaded"], 16 * b["loads"])
                nc.scalar.activation(clip[:, :], clip[:, :], ACT.Sigmoid).then_inc(clipped, 1)

            @block.tensor
            def _(pe):
                pe.wait_ge(prep, 5)
                for m in range(9):
                    last = nc.tensor.transpose(w_ps[m // 4][:, (m % 4) * 128:(m % 4) * 128 + 128], wi[:, m, :],
                                               c["ident"][:, :])
                last.then_inc(turned, 1)
                pe.wait_ge(diag_made, 1)
                nc.tensor.matmul(w_ps[2][:, 256:384], c["ones"][:, :], diag[:, :], start=True, stop=True) \
                    .then_inc(turned, 1)

            @block.vector
            def _(dve):
                dve.wait_ge(zeroed, 1)
                nc.vector.tensor_reduce(mx[:, 0:1], c["nT"][:, :], AX.X, ALU.max, apply_absolute_value=True) \
                    .then_inc(scaled, 1)
                dve.wait_ge(b["loaded"], 16 * b["loads"])
                count = [0]

                def then(ins):
                    count[0] += 1
                    ins.then_inc(prep, 1)
                    dve.wait_ge(prep, count[0])
                nc.vector.tensor_reduce(sw[:, 0:6], wn[:, 0:6, :], AX.X, ALU.max, apply_absolute_value=True)
                then(nc.vector.tensor_reduce(sw[:, 6:7], wn[:, 6:9, :], AX.XY, ALU.max, apply_absolute_value=True))
                then(nc.vector.tensor_scalar(sw[:, :], sw[:, :], 1.0 / QMAX, 1e-37, ALU.mult, ALU.max))
                then(nc.vector.reciprocal(isw[:, :], sw[:, :]))
                for m in range(9):
                    last = nc.vector.tensor_scalar(wi[:, m, :], wn[:, m, :], isw[:, min(m, 6):min(m, 6) + 1], MAGIC,
                                                   ALU.mult, ALU.add)
                then(last)
                then(nc.vector.tensor_scalar(wi[:, :, :], wi[:, :, :], MAGIC, None, ALU.subtract))
                nc.vector.tensor_scalar(diag[:, :], c["ident"][:, :], sw[:, 6:7], None, ALU.mult).then_inc(diag_made, 1)
                dve.wait_ge(turned, 2)
                for m in range(3):
                    n = (4, 4, 1)[m]
                    last = nc.vector.tensor_copy(w_t[:, 4 * m:4 * m + n, :], w_ps[m][:, 0:n * 128]
                                                 .rearrange("p (n f) -> p n f", f=128))
                nc.vector.tensor_copy(down_scale[:, :], w_ps[2][:, 256:384])
                dve.wait_ge(clipped, 1)
                dve.wait_ge(all_max, 1)
                then(nc.vector.tensor_tensor(act_scale[:, 0:1], clip[:, 0:1], amax[:, 0:1], ALU.mult))
                then(nc.vector.tensor_scalar(act_scale[:, 0:1], act_scale[:, 0:1], 1.0 / QMAX, None, ALU.mult))
                then(nc.vector.reciprocal(inv_scale[:, 0:1], act_scale[:, 0:1]))
                then(nc.vector.tensor_scalar(both[:, :], sw[:, 0:6], act_scale[:, 0:1], None, ALU.mult))

        with Scope(nc, "l0_up") as up:
            qa = up.sb("rounded", [128, 2, 512])
            xq = up.sb("x_whole", [128, 2, 512], BF16)
            sg = up.sb("silu", [128, 2, 512])
            gu = [[up.ps(f"{n}{i}", [128, 512]) for n in ("gate", "up")] for i in range(2)]
            rounded, clipped_, whole = (up.counter(n) for n in ("rounded", "clipped", "whole"))
            filled, silu_done, h_done = (up.counter(n, 3) for n in ("filled", "silu_done", "h_done"))

            def pairs(eng, body):
                with eng.Fori(0, N // 2) as it:
                    for s in range(2):
                        body(it * 2 + s, s)
            up.begin()
            with nc.Block() as block:
                @block.gpsimd
                def _(pool):
                    def body(t, s):
                        rounded.wait(pool, t, 1)
                        settle(pool, up.passed)
                        nc.gpsimd.tensor_scalar(qa[:, s, :], qa[:, s, :], MAGIC + QMAX, MAGIC - QMAX - 1, ALU.min, ALU.max) \
                            .then_inc(clipped_.sem, 1)
                        clipped_.wait(pool, t, 1)
                        filled.wait_steps(pool, t - s)
                        settle(pool, up.passed)
                        nc.gpsimd.tensor_scalar(xq[:, s, :], qa[:, s, :], MAGIC, None, ALU.subtract).then_inc(whole.sem, 1)
                    pairs(pool, body)

                @block.tensor
                def _(pe):
                    def body(t, s):
                        whole.wait(pe, t, 1)
                        for i in range(3):
                            if i == 2:
                                h_done.wait(pe, t, 1)
                            else:
                                h_done.wait_steps(pe, t)
                            settle(pe, up.passed)
                            for k in range(2):
                                last = nc.tensor.matmul(gu[i % 2][k][:, :], w_t[:, 3 * k + i, :], xq[:, s, :],
                                                        start=True, stop=True)
                            last.then_inc(filled.sem, 1)
                    pairs(pe, body)

                @block.scalar
                def _(act):
                    def body(t, s):
                        for i in range(3):
                            filled.wait(act, t, i + 1)
                            if i == 2:
                                h_done.wait(act, t, 1)
                            else:
                                h_done.wait_steps(act, t)
                            settle(act, up.passed)
                            nc.scalar.activation(sg[:, i % 2, :], gu[i % 2][0][:, :], ACT.Silu, scale=both[:, i:i + 1]) \
                                .then_inc(silu_done.sem, 1)
                    pairs(act, body)

                @block.vector
                def _(dve):
                    def body(t, s):
                        clipped_.wait_steps(dve, t - s)
                        whole.wait_steps(dve, t - s)
                        settle(dve, up.passed)
                        nc.vector.tensor_scalar(qa[:, s, :], c["nT"][:, bass.ds(t * 512, 512)], inv_scale[:, 0:1], MAGIC,
                                                ALU.mult, ALU.add).then_inc(rounded.sem, 1)
                        for i in range(3):
                            silu_done.wait(dve, t, i + 1)
                            settle(dve, up.passed)
                            nc.vector.scalar_tensor_tensor(out=hid[:, i, bass.ds(t * 512, 512)], in0=gu[i % 2][1][:, :],
                                                           scalar=both[:, 3 + i:4 + i], in1=sg[:, i % 2, :],
                                                           op0=ALU.mult, op1=ALU.mult).then_inc(h_done.sem, 1)
                    pairs(dve, body)

        with nc.Block() as block:
            @block.gpsimd
            def _(pool):
                pool.wait_ge(scaled, 3)
                nc.gpsimd.partition_all_reduce(amax[:, 1:2], mx[:, 0:1], 128, REDUCE_MAX) \
                    .then_inc(all_max, 1)

            @block.vector
            def _(dve):
                nc.vector.tensor_reduce(mx[:, 1:4], hid[:, :, :], AX.X, ALU.max, apply_absolute_value=True) \
                    .then_inc(scaled, 1)
                dve.wait_ge(scaled, 2)
                nc.vector.tensor_reduce(mx[:, 0:1], mx[:, 1:4], AX.X, ALU.max).then_inc(scaled, 1)
                dve.wait_ge(all_max, 2)
                count = [9]

                def then(ins):
                    count[0] += 1
                    ins.then_inc(prep, 1)
                    dve.wait_ge(prep, count[0])
                then(nc.vector.tensor_tensor(act_scale[:, 1:2], clip[:, 1:2], amax[:, 1:2], ALU.mult))
                then(nc.vector.tensor_scalar(act_scale[:, 1:2], act_scale[:, 1:2], 1.0 / QMAX, None, ALU.mult))
                then(nc.vector.reciprocal(inv_scale[:, 1:2], act_scale[:, 1:2]))

        with Scope(nc, "l0_down") as dn:
            qa = dn.sb("rounded", [128, 2, 3, 512])
            hq = dn.sb("h_whole", [128, 2, 3, 512], BF16)
            out = dn.sb("out", [128, 2, G, 128])
            o_ps = [dn.ps(f"out{i}", [128, 512]) for i in range(2)]
            rounded, clipped_, whole, filled, out_scaled, added = (
                dn.counter(n) for n in ("rounded", "clipped", "whole", "filled", "out_scaled", "added"))
            dn.begin()
            with nc.Block() as block:
                @block.gpsimd
                def _(pool):
                    def body(t, s):
                        rounded.wait(pool, t, 1)
                        settle(pool, dn.passed)
                        nc.gpsimd.tensor_scalar(qa[:, s, :, :], qa[:, s, :, :], MAGIC + QMAX, MAGIC - QMAX - 1, ALU.min,
                                                ALU.max).then_inc(clipped_.sem, 1)
                        out_scaled.wait(pool, t, 1)
                        settle(pool, dn.passed)
                        xs = c["x"][:, bass.ds(t * G, G), :]
                        nc.gpsimd.tensor_tensor(xs, xs, out[:, s, :, :], ALU.add).then_inc(added.sem, 1)
                    pairs(pool, body)

                @block.scalar
                def _(act):
                    def body(t, s):
                        clipped_.wait(act, t, 1)
                        filled.wait_steps(act, t - s)
                        settle(act, dn.passed)
                        nc.scalar.activation(hq[:, s, :, :], qa[:, s, :, :], ACT.Copy, bias=-MAGIC).then_inc(whole.sem, 1)
                    pairs(act, body)

                @block.tensor
                def _(pe):
                    def body(t, s):
                        whole.wait(pe, t, 1)
                        out_scaled.wait_steps(pe, t - s)
                        settle(pe, dn.passed)
                        for j in range(G):
                            for i, (r0, rn) in enumerate(CH):
                                last = nc.tensor.matmul(o_ps[s][:, j * 128:(j + 1) * 128],
                                                        hq[0:rn, s, i, j * 128:(j + 1) * 128], w_t[0:rn, 6 + i, :],
                                                        start=(i == 0), stop=(i == 2))
                        last.then_inc(filled.sem, 1)
                    pairs(pe, body)

                @block.vector
                def _(dve):
                    def body(t, s):
                        whole.wait_steps(dve, t - s)
                        settle(dve, dn.passed)
                        nc.vector.tensor_scalar(qa[:, s, :, :], hid[:, :, bass.ds(t * 512, 512)], inv_scale[:, 1:2], MAGIC,
                                                ALU.mult, ALU.add).then_inc(rounded.sem, 1)
                        filled.wait(dve, t, 1)
                        added.wait_steps(dve, t - s)
                        settle(dve, dn.passed)
                        nc.vector.scalar_tensor_tensor(out=out[:, s, :, :],
                                                       in0=o_ps[s][:, :].rearrange("p (g f) -> p g f", g=G),
                                                       scalar=act_scale[:, 1:2],
                                                       in1=down_scale[:, :].unsqueeze(1).to_broadcast([128, G, 128]),
                                                       op0=ALU.mult, op1=ALU.mult).then_inc(out_scaled.sem, 1)
                    pairs(dve, body)


def l1_ffn(nc, c, T):
    E, CAP, HD = 16, 2, 64
    W3 = 3 * HD
    G, N = 4, B // 4
    scale = float(HD) ** -0.5
    rows = nc.dram_tensor("token_rows", (S * B, D), F32, kind="Internal").ap()
    with Scope(nc, "l1_ffn") as sc:
        tok = sc.sb("tokens", [128, B, 128])
        idx = sc.sb("row_index", [128, E, CAP], U32)
        normalize(nc, c, "n1f", c["x"], 128, c["nT"], ["ln"], token_out=tok)

        with Scope(nc, "l1_route") as rt:
            wg = rt.sb("router", [128, E])
            cur = rt.sb("tiles", [128, 2, 512])
            val = rt.sb("probs", [128, B, E])
            rmax, rsum = rt.sb("row_max", [128, B]), rt.sb("row_sum", [128, B])
            iota_i, iota = rt.sb("index_int", [128, E, B], I32), rt.sb("index", [128, E, B])
            base_i, base = rt.sb("base_int", [128, 1], I32), rt.sb("base", [128, 1])
            w = dict(top=rt.sb("top", [128, 2, E]), index=rt.sb("top_index", [128, 2, E]),
                     eq=rt.sb("eq", [128, E, B])[:, :, :], rest=rt.sb("rest", [128, E, B])[:, :, :],
                     hot=[rt.sb(f"hot{i}", [128, E, B])[:, :, :] for i in range(2)])
            picked = rt.sb("picked", [128, E, CAP])
            R_ps = rt.ps("logits", [128, B * E])
            b = loader(nc, rt, [(wg[:, :], T["L1_ffn_Wg"])])
            tile_ready, routed = rt.counter("tile_ready"), rt.counter("routed")
            index_made, soft, shifted, exped, part, stored = (
                rt.semaphore(n) for n in ("index_made", "softmax_part", "shifted", "exped", "top_part", "rows_stored"))
            rt.begin()
            with nc.Block() as block:
                @block.sync
                def _(sp):
                    b["dma"](sp)
                    sp.dma_start(rows.rearrange("(p s) d -> p s d", s=B), tok[:, :, :]).then_inc(stored, 16)
                    sp.wait_ge(stored, 16)

                @block.gpsimd
                def _(pool):
                    nc.gpsimd.iota(iota_i[:, :, :], pattern=[[0, E], [1, B]], base=0, channel_multiplier=0)
                    nc.gpsimd.iota(base_i[:, :], pattern=[[0, 1]], base=0, channel_multiplier=B).then_inc(index_made, 1)
                    with pool.Fori(0, N // 2) as it:
                        for s in range(2):
                            t = it * 2 + s
                            routed.wait_steps(pool, it * 2)
                            settle(pool, rt.passed)
                            nc.gpsimd.tensor_copy(cur[:, s, :], c["nT"][:, bass.ds(t * 512, 512)]) \
                                .then_inc(tile_ready.sem, 1)

                @block.tensor
                def _(pe):
                    pe.wait_ge(b["loaded"], 16)
                    with pe.Fori(0, N // 2) as it:
                        for s in range(2):
                            t = it * 2 + s
                            tile_ready.wait(pe, t, 1)
                            settle(pe, rt.passed)
                            for j in range(G):
                                last = nc.tensor.matmul(R_ps[:, bass.ds(t * (G * E) + j * E, E)],
                                                        cur[:, s, j * 128:(j + 1) * 128], wg[:, :], start=True, stop=True)
                            last.then_inc(routed.sem, 1)

                @block.scalar
                def _(act):
                    act.wait_ge(shifted, 1)
                    nc.scalar.activation(val[:, :, :], val[:, :, :], ACT.Exp).then_inc(exped, 1)

                @block.vector
                def _(dve):
                    dve.wait_ge(index_made, 1)
                    nc.vector.tensor_copy(iota[:, :, :], iota_i[:, :, :])
                    nc.vector.tensor_copy(base[:, :], base_i[:, :]).then_inc(index_made, 1)
                    dve.wait_ge(index_made, 2)
                    dve.wait_ge(routed.sem, N + 1)
                    logits = R_ps[:, :].rearrange("p (s e) -> p s e", e=E)

                    def bc(ap):
                        return ap.unsqueeze(2).to_broadcast([128, B, E])
                    nc.vector.tensor_reduce(rmax[:, :], logits, AX.X, ALU.max).then_inc(soft, 1)
                    dve.wait_ge(soft, 1)
                    nc.vector.tensor_tensor(val[:, :, :], logits, bc(rmax[:, :]), ALU.subtract).then_inc(shifted, 1)
                    dve.wait_ge(exped, 1)
                    nc.vector.reduce_sum(rsum[:, :], val[:, :, :], axis=AX.X).then_inc(soft, 1)
                    dve.wait_ge(soft, 2)
                    nc.vector.reciprocal(rsum[:, :], rsum[:, :]).then_inc(soft, 1)
                    dve.wait_ge(soft, 3)
                    nc.vector.tensor_tensor(val[:, :, :], val[:, :, :], bc(rsum[:, :]), ALU.mult).then_inc(soft, 1)
                    dve.wait_ge(soft, 4)
                    then = top_two(nc, dve, rt, w, val[:, :, :].rearrange("p s e -> p e s"), E, B, iota[:, :, :], part)
                    for k, op in enumerate((ALU.min, ALU.max)):
                        then(nc.vector.tensor_tensor(picked[:, :, k], w["index"][:, 0, :], w["index"][:, 1, :], op))
                    then(nc.vector.tensor_scalar(picked[:, :, :], picked[:, :, :], base[:, 0:1], None, ALU.add))
                    then(nc.vector.tensor_copy(idx[:, :, :], picked[:, :, :]))

        hg = sc.sb("gathered", [128, E, CAP, 128])
        w3 = sc.sb("w_qkv", [128, E, W3])
        b3 = sc.sb("b_qkv", [1, E, W3])
        wo = sc.sb("wo", [HD, E, 128])
        bo = sc.sb("bo", [128, 128])
        gb = sc.sb("gain", [128, 2, 128])
        qkv = sc.sb("qkv", [128, E, CAP, W3])
        tile = sc.sb("expert_tile", [128, 2, CAP, 128])
        hT = sc.sb("expert_tile_t", [128, 2, CAP, 128])
        av = sc.sb("attended", [128, E, CAP, HD])
        items = [(w3[:, :, 0:HD], T["L1_ffn_Wq"].rearrange("e d f -> d e f")),
                 (w3[:, :, HD:W3], T["L1_ffn_Wkv"].rearrange("e d f -> d e f")),
                 (b3[:, :, 0:HD], T["L1_ffn_bq"].rearrange("(a e) f -> a e f", a=1)),
                 (b3[:, :, HD:W3], T["L1_ffn_bkv"].rearrange("(a e) f -> a e f", a=1)),
                 (wo[:, :, :], T["L1_ffn_Wo"].rearrange("e f d -> f e d")),
                 (bo[:, :], row(T["L1_ffn_bo"]).to_broadcast([128, 128])),
                 (gb[:, 0, :], row(T["L1_ffn_ln_g"]).to_broadcast([128, 128])),
                 (gb[:, 1, :], row(T["L1_ffn_ln_b"]).to_broadcast([128, 128]))]
        b = loader(nc, sc, items)
        gathered = sc.semaphore("gathered")

        def pairs(eng, body, n=E):
            with eng.Fori(0, n // 2) as it:
                for s in range(2):
                    body(it * 2 + s, s)

        with Scope(nc, "l1_qkv") as g_:
            t_ps = [g_.ps(f"turned{i}", [128, 512]) for i in range(2)]
            q_ps = [g_.ps(f"qkv{i}", [128, 512]) for i in range(2)]
            tile_ready, turned, turned_copied, projected, copied = (
                g_.counter(n) for n in ("tile_ready", "turned", "turned_copied", "projected", "copied"))
            g_.begin()
            with nc.Block() as block:
                @block.sync
                def _(sp):
                    b["dma"](sp)

                @block.gpsimd
                def _(pool):
                    for e in range(E):
                        for k in range(CAP):
                            nc.gpsimd.indirect_dma_start(
                                out=hg[:, e, k, :], out_offset=None, in_=rows,
                                in_offset=bass.IndirectOffsetOnAxis(ap=idx[:, e, k:k + 1], axis=0)).then_inc(gathered, 16)
                    pool.wait_ge(gathered, 16 * E * CAP)

                    def body(t, s):
                        turned.wait_steps(pool, t - s)
                        settle(pool, g_.passed)
                        nc.gpsimd.tensor_copy(tile[:, s, :, :], hg[:, t, :, :]).then_inc(tile_ready.sem, 1)
                    pairs(pool, body)

                @block.tensor
                def _(pe):
                    pe.wait_ge(b["loaded"], 16 * b["loads"])

                    def body(t, s):
                        tile_ready.wait(pe, t, 1)
                        turned_copied.wait_steps(pe, t - s)
                        settle(pe, g_.passed)
                        for k in range(CAP):
                            last = nc.tensor.transpose(t_ps[s][:, k * 128:(k + 1) * 128], tile[:, s, k, :], c["ident"][:, :])
                        last.then_inc(turned.sem, 1)
                        turned_copied.wait(pe, t, 1)
                        copied.wait_steps(pe, t - s)
                        settle(pe, g_.passed)
                        for k in range(CAP):
                            o = q_ps[s][:, k * W3:(k + 1) * W3]
                            nc.tensor.matmul(o, hT[:, s, k, :], w3[:, t, :], start=True, stop=False)
                            last = nc.tensor.matmul(o, c["ones"][0:1, :], b3[0:1, t, :], start=False, stop=True)
                        last.then_inc(projected.sem, 1)
                    pairs(pe, body)

                @block.scalar
                def _(act):
                    def body(t, s):
                        turned.wait(act, t, 1)
                        projected.wait_steps(act, t - s)
                        settle(act, g_.passed)
                        nc.scalar.activation(hT[:, s, :, :], t_ps[s][:, 0:CAP * 128], ACT.Copy) \
                            .then_inc(turned_copied.sem, 1)
                    pairs(act, body)

                @block.vector
                def _(dve):
                    def body(t, s):
                        projected.wait(dve, t, 1)
                        settle(dve, g_.passed)
                        nc.vector.tensor_copy(qkv[:, t, :, :], q_ps[s][:, 0:CAP * W3].rearrange("p (k f) -> p k f", k=CAP)) \
                            .then_inc(copied.sem, 1)
                    pairs(dve, body)

        with Scope(nc, "l1_pair") as a_:
            prod = a_.sb("products", [128, 2, E, HD])
            att = a_.sb("scores", [128, 4, E])
            pt = a_.sb("probs_t", [64, 128])
            pr = a_.sb("probs", [128, 4, E])
            nm, ssum, srs = a_.sb("neg_max", [64, 1]), a_.sb("sum", [64, 1]), a_.sb("rsum", [64, 1])
            s_ps, p_ps = a_.ps("scores_t", [64, 128]), a_.ps("probs_back", [128, 64])
            mult, summed, turned, exped, part, back, combined = (
                a_.semaphore(n) for n in ("multiplied", "summed", "turned", "exped", "soft_part", "turned_back", "combined"))
            a_.begin()
            with nc.Block() as block:
                @block.gpsimd
                def _(pool):
                    for n in range(4):
                        i, j = n // 2, n % 2
                        if n >= 2:
                            pool.wait_ge(summed, n - 1)
                        nc.gpsimd.tensor_tensor(prod[:, n % 2, :, :], qkv[:, :, i, 0:HD], qkv[:, :, j, HD:2 * HD],
                                                ALU.mult).then_inc(mult, 1)

                @block.tensor
                def _(pe):
                    pe.wait_ge(summed, 4)
                    nc.tensor.transpose(s_ps[:, :], att[:, :, :].rearrange("p n e -> p (n e)"), c["ident"][:, :]) \
                        .then_inc(turned, 1)
                    pe.wait_ge(part, 4)
                    nc.tensor.transpose(p_ps[:, :], pt[:, :], c["ident"][0:64, 0:64]).then_inc(back, 1)

                @block.scalar
                def _(act):
                    act.wait_ge(part, 2)
                    nc.scalar.activation(pt[:, :], s_ps[:, :], ACT.Exp, bias=nm[:, 0:1], scale=scale,
                                         accum_out=ssum[:, 0:1]).then_inc(exped, 1)

                @block.vector
                def _(dve):
                    for n in range(4):
                        dve.wait_ge(mult, n + 1)
                        nc.vector.reduce_sum(att[:, n, :], prod[:, n % 2, :, :], axis=AX.X).then_inc(summed, 1)
                    dve.wait_ge(turned, 1)
                    nc.vector.tensor_reduce(nm[:, :], s_ps[:, :], AX.X, ALU.max, negate=True).then_inc(part, 1)
                    dve.wait_ge(part, 1)
                    nc.vector.tensor_scalar(nm[:, :], nm[:, :], scale, None, ALU.mult).then_inc(part, 1)
                    dve.wait_ge(exped, 1)
                    nc.vector.reciprocal(srs[:, :], ssum[:, :]).then_inc(part, 1)
                    dve.wait_ge(part, 3)
                    nc.vector.tensor_scalar(pt[:, :], pt[:, :], srs[:, 0:1], None, ALU.mult).then_inc(part, 1)
                    dve.wait_ge(back, 1)
                    nc.vector.tensor_copy(pr[:, :, :], p_ps[:, :].rearrange("p (n e) -> p n e", e=E)).then_inc(part, 1)
                    dve.wait_ge(part, 5)
                    n = 0
                    for i in range(CAP):
                        for j in range(CAP):
                            if n:
                                dve.wait_ge(combined, n)
                            last = nc.vector.tensor_tensor(
                                prod[:, j, :, :], qkv[:, :, j, 2 * HD:W3],
                                pr[:, 2 * i + j, :].unsqueeze(2).to_broadcast([128, E, HD]), ALU.mult)
                        last.then_inc(combined, 1)
                        n += 1
                        dve.wait_ge(combined, n)
                        nc.vector.tensor_tensor(av[:, :, i, :], prod[:, 0, :, :], prod[:, 1, :, :], ALU.add) \
                            .then_inc(combined, 1)
                        n += 1
                    dve.wait_ge(combined, n)

        ao = hg
        with Scope(nc, "l1_out") as o_:
            t_ps = [o_.ps(f"turned{i}", [128, 512]) for i in range(2)]
            y_ps = [o_.ps(f"out{i}", [128, 512]) for i in range(2)]
            tile_ready, turned, turned_copied, projected, copied = (
                o_.counter(n) for n in ("tile_ready", "turned", "turned_copied", "projected", "copied"))
            scattered, fetched = o_.semaphore("scattered"), o_.semaphore("fetched")
            o_.begin()
            with nc.Block() as block:
                @block.sync
                def _(sp):
                    sp.wait_ge(scattered, 16 * E * CAP)
                    sp.dma_start(tok[:, :, :], rows.rearrange("(p s) d -> p s d", s=B)).then_inc(fetched, 16)
                    sp.wait_ge(fetched, 16)

                @block.gpsimd
                def _(pool):
                    def body(t, s):
                        turned.wait_steps(pool, t - s)
                        settle(pool, o_.passed)
                        nc.gpsimd.tensor_copy(tile[:, s, :, 0:HD], av[:, t, :, :]).then_inc(tile_ready.sem, 1)
                    pairs(pool, body)
                    for e in range(E):
                        pool.wait_ge(copied.sem, e + 2)
                        if e:
                            pool.wait_ge(scattered, 16 * e * CAP)
                        for k in range(CAP):
                            nc.gpsimd.indirect_dma_start(
                                out=rows, out_offset=bass.IndirectOffsetOnAxis(ap=idx[:, e, k:k + 1], axis=0),
                                in_=ao[:, e, k, :], in_offset=None, compute_op=ALU.add).then_inc(scattered, 16)
                    pool.wait_ge(scattered, 16 * E * CAP)

                @block.tensor
                def _(pe):
                    def body(t, s):
                        tile_ready.wait(pe, t, 1)
                        turned_copied.wait_steps(pe, t - s)
                        settle(pe, o_.passed)
                        for k in range(CAP):
                            last = nc.tensor.transpose(t_ps[s][0:HD, k * 128:(k + 1) * 128], tile[:, s, k, 0:HD],
                                                       c["ident"][:, :])
                        last.then_inc(turned.sem, 1)
                        turned_copied.wait(pe, t, 1)
                        copied.wait_steps(pe, t - s)
                        settle(pe, o_.passed)
                        for k in range(CAP):
                            last = nc.tensor.matmul(y_ps[s][:, k * 128:(k + 1) * 128], hT[0:HD, s, k, :], wo[:, t, :],
                                                    start=True, stop=True)
                        last.then_inc(projected.sem, 1)
                    pairs(pe, body)

                @block.scalar
                def _(act):
                    def body(t, s):
                        turned.wait(act, t, 1)
                        projected.wait_steps(act, t - s)
                        settle(act, o_.passed)
                        nc.scalar.activation(hT[0:HD, s, :, :], t_ps[s][0:HD, 0:CAP * 128], ACT.Copy) \
                            .then_inc(turned_copied.sem, 1)
                    pairs(act, body)

                @block.vector
                def _(dve):
                    def body(t, s):
                        projected.wait(dve, t, 1)
                        settle(dve, o_.passed)
                        nc.vector.tensor_tensor(ao[:, t, :, :], y_ps[s][:, 0:CAP * 128].rearrange("p (k f) -> p k f", k=CAP),
                                                bo[:, :].unsqueeze(1).to_broadcast([128, CAP, 128]), ALU.add) \
                            .then_inc(copied.sem, 1)
                    pairs(dve, body)

        normalize(nc, c, "n1y", tok, 128, c["nT"], ["ln"], token_out=tok)
        with Scope(nc, "l1_res") as r_:
            part = r_.semaphore("part")
            r_.begin()
            with nc.Block() as block:
                @block.vector
                def _(dve):
                    for i, (in0, in1, out, op) in enumerate((
                            (tok, gb[:, 0, :], tok, ALU.mult), (tok, gb[:, 1, :], tok, ALU.add), (tok, None, c["x"], ALU.add))):
                        if i:
                            dve.wait_ge(part, i)
                        in1 = c["x"][:, :, :] if in1 is None else in1.unsqueeze(1).to_broadcast([128, B, 128])
                        nc.vector.tensor_tensor(out[:, :, :], in0[:, :, :], in1, op).then_inc(part, 1)


def program(nc, T, out, stop):
    with ExitStack() as keep:
        def sb(name, shape, dt=F32):
            return keep.enter_context(nc.sbuf_tensor(name, shape, dt))
        c = dict(x=sb("x_tokens", [128, B, 128]), nT=sb("normed_t", [128, B * 128]),
                 ctx=sb("context", [SC, B, 128]), cT=sb("context_t", [128, B * (SC + 1)]),
                 ident=sb("ident", [128, 128]), ones=sb("ones", [128, 128]),
                 neg_half=sb("neg_half", [128, 4]), head_mask=sb("head_mask", [128, 4, 4]),
                 mask8=sb("mask8", [128, 4]))
        inputs_in = nc.alloc_semaphore("inputs_in")
        with nc.Block() as block:
            @block.sync
            def _(sp):
                sp.dma_start(c["x"][:, :, :], T["x"].rearrange("b s d -> s b d")).then_inc(inputs_in, 16)
                sp.dma_start(c["ctx"][:, :, :], T["ctx_1024"].rearrange("b s d -> s b d")).then_inc(inputs_in, 16)
                sp.wait_ge(inputs_in, 32)
        nc.clear_and_free_semaphores([inputs_in])
        nc.all_engine_barrier()
        make_consts(nc, c)
        def l1_cross(nc, c, T):
            with Scope(nc, "l1_norms") as sc:
                wb = sc.sb("scale_shift", [128, 4])
                b = loader(nc, sc, [(wb[:, i:i + 1], column(T["L1_xattn_" + n]))
                                    for i, n in enumerate(("ln1_w", "ln1_b", "ln2_w", "ln2_b"))])
                sc.begin()
                with nc.Block() as block:
                    @block.sync
                    def _(sp):
                        b["dma"](sp)
                        sp.wait_ge(b["loaded"], 16 * b["loads"])
                normalize(nc, c, "n1x", c["x"], 128, c["nT"], ["ln", "ln"], scale=wb[:, 2:3], shift=wb[:, 3:4])
                normalize(nc, c, "n1c", c["ctx"], SC, c["cT"], ["ln"], scale=wb[:, 0:1], shift=wb[:, 1:2])
            l1_cross_attention(nc, c, T)

        stages = [
            lambda: (normalize(nc, c, "n0a", c["x"], 128, c["nT"], ["ln"]), l0_attention(nc, c, T)),
            lambda: (normalize(nc, c, "n0x", c["x"], 128, c["nT"], ["ln", "rms"]),
                     normalize(nc, c, "n0c", c["ctx"], SC, c["cT"], ["rms"]), l0_cross_attention(nc, c, T)),
            lambda: (normalize(nc, c, "n0f", c["x"], 128, c["nT"], ["ln"]), l0_ffn(nc, c, T)),
            lambda: (normalize(nc, c, "n1a", c["x"], 128, c["nT"], ["ln"]), l1_attention(nc, c, T)),
            lambda: l1_cross(nc, c, T),
            lambda: l1_ffn(nc, c, T),
            lambda: (normalize(nc, c, "n2a", c["x"], 128, c["nT"], ["ln"]), l2_attention(nc, c, T)),
            lambda: (normalize(nc, c, "n2x", c["x"], 128, c["nT"], ["ln"]),
                     normalize(nc, c, "n2c", c["ctx"], SC, c["cT"], []), l2_cross_attention(nc, c, T)),
            lambda: (normalize(nc, c, "n2f", c["x"], 128, c["nT"], ["ln"]), l2_ffn(nc, c, T)),
            lambda: (normalize(nc, c, "n3a", c["x"], 128, c["nT"], ["ln"]), l3_attention(nc, c, T)),
            lambda: (normalize(nc, c, "n3x", c["x"], 128, c["nT"], ["ln"]),
                     normalize(nc, c, "n3c", c["ctx"], SC, c["cT"], []), l3_cross_attention(nc, c, T)),
            lambda: (normalize(nc, c, "n3f", c["x"], 128, c["nT"], ["ln"]), l3_ffn(nc, c, T)),
        ]
        for f in stages[:stop]:
            f()
        stored = nc.alloc_semaphore("stored")
        nc.all_engine_barrier()
        with nc.Block() as block:
            @block.sync
            def _(sp):
                sp.dma_start(out.rearrange("b s d -> s b d"), c["x"][:, :, :]).then_inc(stored, 16)
                sp.wait_ge(stored, 16)


_T = ["L0_attn_qkv_w", "L0_attn_proj_w", "L1_attn_Wq", "L1_attn_Wk", "L1_attn_Wv",
      "L2_ffn_shared_gate", "L2_ffn_shared_up", "L2_ffn_shared_down", "L2_ffn_router_w", "L3_ffn_router_w",
      "L3_xattn_Wo", "L3_xattn_Wq", "L3_xattn_Wk", "L3_xattn_Wv"]


def kernel(**inputs):
    import numpy as np
    import concourse.bacc as bacc
    from concourse import mybir as mb
    from concourse.bass_utils import run_bass_kernel_spmd as run

    nc = bacc.Bacc("TRN2", target_bir_lowering=False, num_devices=1)
    arrays, T = {}, {}
    for name, a in inputs.items():
        if name == "L1_ffn_attn_mask":
            continue
        a = np.asarray(a)
        if name in _T:
            a = a.T
        if name == "mask_BxS2_bk0":
            pass
        a = np.ascontiguousarray(a)
        arrays["in_" + name] = a
        T[name] = nc.dram_tensor("in_" + name, a.shape, mb.dt.from_np(a.dtype), kind="ExternalInput").ap()
    half = np.arange(16, dtype=np.float32)
    timescale = np.float32(10000.0) ** (np.float32(2.0 / 32) * half)
    pos = np.concatenate([np.arange(77, 77 + 128), np.arange(77)]).astype(np.float32)
    rad = (pos[None, :] / timescale[:, None]).astype(np.float32)
    cos, sin = np.cos(rad), np.sin(rad)
    rope = np.stack([np.tile(np.concatenate([cos, cos]), (4, 1)), np.tile(np.concatenate([-sin, sin]), (4, 1))], 1)
    arrays["in_rope"] = np.ascontiguousarray(rope.astype(np.float32))
    T["rope"] = nc.dram_tensor("in_rope", arrays["in_rope"].shape, mb.dt.float32, kind="ExternalInput").ap()
    out = nc.dram_tensor("out_0", (B, S, D), mb.dt.float32, kind="ExternalOutput").ap()
    program(nc, T, out, 99)
    r = run(nc, [arrays], core_ids=[0])
    return r.results[0]["out_0"]
```

```python
import numpy as np
from contextlib import ExitStack

import concourse.bass as bass
import concourse.mybir as mybir

F32 = mybir.dt.float32
BF16 = mybir.dt.bfloat16
U8 = mybir.dt.uint8
U32 = mybir.dt.uint32
I32 = mybir.dt.int32
ALU = mybir.AluOpType
ACT = mybir.ActivationFunctionType
AX = mybir.AxisListType
REDUCE_MAX = bass.bass_isa.ReduceOp.max

B, S, D = 32, 128, 128
SC = 77
LN_EPS = 1e-5
RMS_EPS = 1e-6


class Signal:

    def __init__(self, scope, name, per_step=1):
        self.sem, self.n = scope.semaphore(name), per_step
        scope.signals.append(self)

    def wait(self, eng, t, k):
        eng.wait_ge(self.sem, t * self.n + (k + 1))

    def wait_steps(self, eng, t):
        eng.wait_ge(self.sem, t * self.n + 1)


class Scope:

    def __init__(self, nc, name):
        self.nc, self.name, self.stack, self.sems, self.signals = nc, name, ExitStack(), [], []

    def __enter__(self):
        self.passed = self.semaphore("waits_passed")
        return self

    def sb(self, name, shape, dt=F32):
        return self.stack.enter_context(self.nc.sbuf_tensor(f"{self.name}_{name}", shape, dt))

    def ps(self, name, shape, dt=F32):
        return self.stack.enter_context(self.nc.psum_tensor(f"{self.name}_{name}", shape, dt))

    def semaphore(self, name):
        sem = self.nc.alloc_semaphore(f"{self.name}_{name}")
        self.sems.append(sem)
        return sem

    def counter(self, name, per_step=1):
        return Signal(self, name, per_step)

    def begin(self):
        for s in self.signals:
            self.nc.gpsimd.sem_inc(s.sem, 1)
        self.signals.clear()
        self.nc.all_engine_barrier()

    def __exit__(self, failure, *_):
        if failure:
            return
        self.stack.close()
        self.nc.clear_and_free_semaphores(self.sems)


def settle(eng, passed):
    eng.sem_inc(passed, 1)


def make_consts(nc, c):
    made = nc.alloc_semaphore("consts_made")
    with nc.Block() as block:
        @block.gpsimd
        def _(pool):
            nc.gpsimd.memset(c["ident"][:, :], 1.0)
            nc.gpsimd.memset(c["ones"][:, :], 1.0)
            nc.gpsimd.memset(c["neg_half"][:, :], -0.5)
            nc.gpsimd.memset(c["head_mask"][:, :, :], 1.0).then_inc(made, 1)
            pool.wait_ge(made, 1)
            nc.gpsimd.affine_select(out=c["ident"][:, :], in_=c["ident"][:, :], compare_op=ALU.is_equal, fill=0.0,
                                    base=0, pattern=[[-1, 128]], channel_multiplier=1).then_inc(made, 1)
            m = c["head_mask"]
            nc.gpsimd.affine_select(out=m[:, :, :], in_=m[:, :, :], compare_op=ALU.is_ge, fill=0.0,
                                    base=0, pattern=[[-8, 4], [-32, 4]], channel_multiplier=1).then_inc(made, 1)
            pool.wait_ge(made, 3)
            nc.gpsimd.affine_select(out=m[:, :, :], in_=m[:, :, :], compare_op=ALU.is_ge, fill=0.0,
                                    base=7, pattern=[[8, 4], [32, 4]], channel_multiplier=-1).then_inc(made, 1)

        @block.vector
        def _(dve):
            dve.wait_ge(made, 4)
            nc.vector.reduce_sum(c["mask8"][:, :], c["head_mask"][:, :, :], axis=AX.X)
    nc.clear_and_free_semaphores([made])
    nc.all_engine_barrier()


def normalize(nc, c, name, src, P, dstT, stages, scale=None, shift=None, token_out=None,
              loads=None):
    G, W = 8, 4
    N = B // G
    ln = stages[:1] == ["ln"]
    two = len(stages) == 2
    eps = [LN_EPS if kind == "ln" else RMS_EPS for kind in stages]
    with Scope(nc, name) as sc:
        st = sc.sb("stats", [P, G, 6])
        mv = sc.sb("mean_var", [P, G, 2])
        ve = sc.sb("var_eps", [P, G])
        part = sc.sb("factor_parts", [P, 3, G])
        mean = sc.sb("mean", [P, B])
        factor = sc.sb("factor", [P, B])
        xn = sc.sb("xn", [P, 2, W, 128])
        ps = [sc.ps(f"tp{i}", [128, 512]) for i in range(2)]
        stats_done = sc.counter("stats_done", 2 if ln else 3)
        var_ready = sc.counter("var_ready")
        part_done = sc.counter("part_done", 5)
        mean_kept = sc.counter("mean_kept")
        factor_ready = sc.counter("factor_ready")
        subtracted = [sc.counter(f"subtracted{g}") for g in range(2)]
        normed = [sc.counter(f"normed{g}") for g in range(2)]
        transposed = [sc.counter(f"transposed{g}") for g in range(2)]
        evacuated = [sc.counter(f"evacuated{g}") for g in range(2)]
        kept = [sc.counter(f"kept{g}") for g in range(2)]

        def apply(eng, alu, t, g):
            r = bass.ds(t * G + g * W, W)
            if stages:
                factor_ready.wait(eng, t, 1)
            if ln:
                mean_kept.wait(eng, t, 1)
            if dstT is not None:
                transposed[g].wait_steps(eng, t)
            if token_out is not None:
                kept[g].wait_steps(eng, t)
            settle(eng, sc.passed)
            first = src[:, r, :]
            if not stages:
                alu.tensor_copy(xn[:, g, :, :], first).then_inc(normed[g].sem, 1)
                return
            if ln:
                alu.tensor_tensor(xn[:, g, :, :], first, mean[:, r].unsqueeze(2).to_broadcast([P, W, 128]),
                                  ALU.subtract).then_inc(subtracted[g].sem, 1)
                subtracted[g].wait(eng, t, 1)
                settle(eng, sc.passed)
                first = xn[:, g, :, :]
            alu.tensor_tensor(xn[:, g, :, :], first, factor[:, r].unsqueeze(2).to_broadcast([P, W, 128]),
                              ALU.mult).then_inc(normed[g].sem, 1)

        sc.begin()
        with nc.Block() as block:
            @block.sync
            def _(sp):
                if loads:
                    loads["dma"](sp)

            @block.gpsimd
            def _(pool):
                if loads and "prepare_pool" in loads:
                    loads["prepare_pool"](pool)

                def factors(t):
                    out = factor[:, bass.ds(t * G, G)]
                    var_ready.wait(pool, t, 1)
                    settle(pool, sc.passed)
                    half = c["neg_half"][0:P, 0:G]
                    if not two:
                        nc.gpsimd.tensor_tensor(out, ve[:, :], half, ALU.pow).then_inc(factor_ready.sem, 1)
                        return
                    nc.gpsimd.tensor_tensor(part[:, 0, :], ve[:, :], half, ALU.pow).then_inc(part_done.sem, 1)
                    part_done.wait(pool, t, 1)
                    settle(pool, sc.passed)
                    nc.gpsimd.tensor_tensor(part[:, 1, :], part[:, 0, :], mv[:, :, 1], ALU.mult) \
                        .then_inc(part_done.sem, 1)
                    part_done.wait(pool, t, 2)
                    settle(pool, sc.passed)
                    nc.gpsimd.tensor_tensor(part[:, 1, :], part[:, 1, :], part[:, 0, :], ALU.mult) \
                        .then_inc(part_done.sem, 1)
                    part_done.wait(pool, t, 3)
                    settle(pool, sc.passed)
                    nc.gpsimd.tensor_scalar(part[:, 2, :], part[:, 1, :], eps[1], None, ALU.add) \
                        .then_inc(part_done.sem, 1)
                    part_done.wait(pool, t, 4)
                    settle(pool, sc.passed)
                    nc.gpsimd.tensor_tensor(part[:, 2, :], part[:, 2, :], half, ALU.pow).then_inc(part_done.sem, 1)
                    part_done.wait(pool, t, 5)
                    settle(pool, sc.passed)
                    nc.gpsimd.tensor_tensor(out, part[:, 2, :], part[:, 0, :], ALU.mult).then_inc(factor_ready.sem, 1)

                if stages:
                    factors(0)
                    with pool.Fori(0, N - 1) as t:
                        factors(t + 1)
                        apply(pool, nc.gpsimd, t, 1)
                    apply(pool, nc.gpsimd, N - 1, 1)
                else:
                    with pool.Fori(0, N) as t:
                        apply(pool, nc.gpsimd, t, 1)

            @block.tensor
            def _(pe):
                if dstT is None:
                    return
                with pe.Fori(0, N) as t:
                    for g in range(2):
                        evacuated[g].wait_steps(pe, t)
                        normed[g].wait(pe, t, 1)
                        settle(pe, sc.passed)
                        for j in range(W):
                            last = nc.tensor.transpose(ps[g][:, j * P:(j + 1) * P], xn[:, g, j, :],
                                                       c["ident"][0:P, 0:P])
                        last.then_inc(transposed[g].sem, 1)

            @block.scalar
            def _(act):
                with act.Fori(0, N) as t:
                    for g in range(2):
                        if token_out is not None:
                            normed[g].wait(act, t, 1)
                            settle(act, sc.passed)
                            nc.scalar.activation(token_out[:, bass.ds(t * G + g * W, W), :], xn[:, g, :, :],
                                                 ACT.Copy).then_inc(kept[g].sem, 1)
                        if dstT is None:
                            continue
                        dst = dstT[:, bass.ds((t * G + g * W) * P, W * P)]
                        transposed[g].wait(act, t, 1)
                        settle(act, sc.passed)
                        if scale is not None:
                            i = nc.scalar.activation(dst, ps[g][:, 0:W * P], ACT.Identity, scale=scale[:, 0:1],
                                                     bias=shift[:, 0:1])
                        else:
                            i = nc.scalar.activation(dst, ps[g][:, 0:W * P], ACT.Copy)
                        i.then_inc(evacuated[g].sem, 1)

            @block.vector
            def _(dve):
                def statistics(t):
                    factor_ready.wait_steps(dve, t)
                    settle(dve, sc.passed)
                    for j in range(G):
                        last = nc.vector.bn_stats(st[:, j, :], src[:, t * G + j, :])
                    last.then_inc(stats_done.sem, 1)
                    stats_done.wait(dve, t, 1)
                    settle(dve, sc.passed)
                    for j in range(G):
                        last = nc.vector.bn_aggr(mv[:, j, :], st[:, j, :])
                    last.then_inc(stats_done.sem, 1)
                    stats_done.wait(dve, t, 2)
                    if ln:
                        nc.vector.tensor_scalar(ve[:, :], mv[:, :, 1], eps[0], None, ALU.add).then_inc(var_ready.sem, 1)
                        nc.vector.tensor_copy(mean[:, bass.ds(t * G, G)], mv[:, :, 0]).then_inc(mean_kept.sem, 1)
                    else:
                        nc.vector.tensor_tensor(ve[:, :], mv[:, :, 0], mv[:, :, 0], ALU.mult) \
                            .then_inc(stats_done.sem, 1)
                        stats_done.wait(dve, t, 3)
                        nc.vector.scalar_tensor_tensor(out=ve[:, :], in0=ve[:, :], scalar=eps[0], in1=mv[:, :, 1],
                                                       op0=ALU.add, op1=ALU.add).then_inc(var_ready.sem, 1)

                if stages:
                    statistics(0)
                    with dve.Fori(0, N - 1) as t:
                        statistics(t + 1)
                        apply(dve, nc.vector, t, 0)
                    apply(dve, nc.vector, N - 1, 0)
                else:
                    with dve.Fori(0, N) as t:
                        apply(dve, nc.vector, t, 0)


def attention(nc, c, name, cfg, load, before):
    with Scope(nc, name) as sc:
        b = load(sc)
        start_loads(sc, b, before)
        H, U, TK = cfg["heads"], cfg["units"], cfg["keys"]
        NB, R = 2, min(4, U)
        LAG = 3
        WLAG = cfg["weigh_lag"]
        HU = H // U
        DV = cfg["dv"]
        GP = cfg["proj_groups"]
        kchunks = cfg["key_chunks"]
        KC = len(kchunks)
        WO = H * DV
        NP = (WO + 511) // 512
        PW = min(512, WO)
        post, masked = cfg.get("post"), cfg.get("masked")
        nmax = sc.sb("neg_max", [128, H])
        sums = sc.sb("sums", [128, 2, H])
        rsum = sc.sb("rsum", [128, 2, HU])
        P_sb = sc.sb("probs", [128, R, HU, TK])
        PT_sb = sc.sb("probs_t", [128, 2, HU, KC, 128])
        OT_sb = sc.sb("heads_out_t", [128, 2, WO // 128, 128])
        Sm = sc.sb("masked_scores", [128, NB, HU, TK]) if masked else None
        S_ps = [sc.ps(f"scores{i}", [128, 512]) for i in range(NB)]
        PT_ps = sc.ps("pt", [128, 512])
        O_ps = [sc.ps(f"o{i}", [128, 512]) for i in range(2)]
        pr_ps = [sc.ps(f"proj{i}", [128, 512]) for i in range(2)]
        out_ps = sc.ps("out", [128, 512])

        tile_ready = sc.counter("tile_ready")
        projected = sc.counter("projected", GP)
        proj_copied = sc.counter("proj_copied", GP)
        posted = sc.counter("posted")
        post_part = sc.counter("post_part", 2)
        scored = sc.counter("scored", U)
        mask_part = sc.counter("mask_part", U)
        maxed = sc.counter("maxed", U)
        exped = sc.counter("exped", U)
        turned = sc.counter("turned", U)
        turned_copied = sc.counter("turned_copied", U)
        weighted = sc.counter("weighted", U)
        inverted = sc.counter("inverted", U)
        divided = sc.counter("divided", U)
        piece_copied = sc.counter("piece_copied", NP)
        out_filled = sc.counter("out_filled")
        biased = sc.counter("biased")
        added = sc.counter("added")
        loaded, nloads = b["loaded"], b["loads"]

        def back(sig, eng, t, k, lag):
            v = k - lag + 1
            if not isinstance(t, int) or t * sig.n + v > 0:
                sig.wait(eng, t, v)

        def lagging(t, s, u, first, lag):
            if u >= lag:
                return t, s, u - lag
            return None if first else (t - 1, 1 - s, u - lag + U)

        def steps(eng, before, slot, after):
            before()
            for u in range(U):
                slot(0, 0, u, True, False)
            with eng.Fori(0, (B - 2) // 2) as it:
                for s in range(2):
                    for u in range(U):
                        slot(it * 2 + 1 + s, (1 + s) % 2, u, False, False)
            for u in range(U):
                slot(B - 1, (B - 1) % 2, u, False, True)
            after()

        drain = [(B - 1, (B - 1) % 2, u) for u in range(U - WLAG, U)]
        sched = cfg["schedule"]

        sc.begin()
        with nc.Block() as block:
            @block.gpsimd
            def _(pool):
                if "bo" in b:
                    pool.wait_ge(loaded, 16 * nloads)

                def tile_copy(t, s):
                    if not isinstance(t, int) or t >= 2:
                        projected.wait_steps(pool, t - 1)
                    settle(pool, sc.passed)
                    for dst, src in b["tiles"](t, s):
                        last = nc.gpsimd.tensor_copy(dst, src)
                    last.then_inc(tile_ready.sem, 1)

                def slot(t, s, u, first, last):
                    if u == 0 and not last:
                        tile_copy(t + 1, 1 - s)
                    if u == 1 and "bo" in b:
                        settle(pool, sc.passed)
                        nc.gpsimd.tensor_tensor(c["x"][:, t, :], c["x"][:, t, :], b["bo"], ALU.add) \
                            .then_inc(biased.sem, 1)
                steps(pool, lambda: tile_copy(0, 0), slot, lambda: None)

            @block.tensor
            def _(pe):
                pe.wait_ge(loaded, 16 * nloads)
                if "prepared" in b:
                    pe.wait_ge(b["prepared"][0], b["prepared"][1])

                def proj(t, s, g):
                    if g == 0:
                        tile_ready.wait(pe, t, 1)
                    if g >= 2:
                        proj_copied.wait(pe, t, g - 1)
                    elif g == 0 and not (isinstance(t, int) and t == 0):
                        proj_copied.wait_steps(pe, t)
                    elif g == 1 and cfg.get("first_feeds"):
                        proj_copied.wait(pe, t, 1)
                    settle(pe, sc.passed)
                    cfg["proj"](b, g, s, pr_ps[g % 2]).then_inc(projected.sem, 1)

                def scores(t, s, u):
                    if u == 0:
                        if post:
                            posted.wait(pe, t, 1)
                        proj_copied.wait(pe, t, GP - len(cfg["v_groups"]))
                    back(exped, pe, t, u, NB)
                    settle(pe, sc.passed)
                    cfg["scores"](b, u, s, S_ps[u % NB]).then_inc(scored.sem, 1)

                def turn(t, u):
                    divided.wait(pe, t, u + 1)
                    back(turned_copied, pe, t, u, 1)
                    settle(pe, sc.passed)
                    for j in range(HU):
                        for kc, (k0, kn) in enumerate(kchunks):
                            o = (j * KC + kc) * 128
                            last = nc.tensor.transpose(PT_ps[0:kn, o:o + 128], P_sb[:, u % R, j, k0:k0 + kn],
                                                       c["ident"][:, :])
                    last.then_inc(turned.sem, 1)

                def weigh(t, s, u):
                    turned_copied.wait(pe, t, u + 1)
                    if u == 0:
                        proj_copied.wait(pe, t, GP)
                    if u * NP % U == 0:
                        back(piece_copied, pe, t, u * NP // U, 2)
                    settle(pe, sc.passed)
                    for j in range(HU):
                        h = cfg["unit_heads"](u)[j]
                        last = cfg["weigh"](b, h, s, O_ps[s if NP == 1 else h * NP // H],
                                            [PT_sb[0:kn, u % 2, j, kc, :] for kc, (k0, kn) in enumerate(kchunks)])
                    last.then_inc(weighted.sem, 1)

                def output(t, s):
                    piece_copied.wait(pe, t, NP)
                    back(added, pe, t, 0, 1)
                    settle(pe, sc.passed)
                    n = WO // 128
                    for m in range(n):
                        last = nc.tensor.matmul(out_ps[:, 0:128], OT_sb[:, s, m, :], b["wo"](m),
                                                start=(m == 0), stop=(m == n - 1))
                    last.then_inc(out_filled.sem, 1)

                def slot(t, s, u, first, last):
                    old = lagging(t, s, u, first, LAG)
                    if old:
                        turn(old[0], old[2])
                    old = lagging(t, s, u, first, WLAG)
                    if old and WLAG > LAG:
                        weigh(*old)
                    scores(t, s, u)
                    for kind, g in sched[u]:
                        if kind == "p" and not last:
                            proj(t + 1, 1 - s, g)
                        if kind == "o" and not first:
                            output(t - 1, 1 - s)
                    if old and WLAG == LAG:
                        weigh(*old)

                def before():
                    for g in range(GP):
                        proj(0, 0, g)

                def after():
                    for t, s, u in drain:
                        v = u + WLAG - LAG
                        if v < U:
                            turn(t, v)
                        weigh(t, s, u)
                    output(B - 1, (B - 1) % 2)
                steps(pe, before, slot, after)

            @block.scalar
            def _(act):
                act.wait_ge(loaded, 16 * nloads)
                if "prepare_act" in b:
                    b["prepare_act"](act)

                def copy_proj(t, s, g):
                    projected.wait(act, t, g + 1)
                    if not (isinstance(t, int) and t < 2):
                        if g in cfg["v_groups"]:
                            weighted.wait_steps(act, t - 1)
                        else:
                            scored.wait_steps(act, t - 1)
                    if g == 0 and post and not (isinstance(t, int) and t == 0):
                        posted.wait_steps(act, t)
                    settle(act, sc.passed)
                    cfg["copy"](b, g, s, pr_ps[g % 2]).then_inc(proj_copied.sem, 1)

                def exps(t, s, u):
                    maxed.wait(act, t, u + 1)
                    back(turned, act, t, u, R)
                    for j in range(HU):
                        h = cfg["unit_heads"](u)[j]
                        src = Sm[:, u % NB, j, :] if masked else S_ps[u % NB][:, j * TK:(j + 1) * TK]
                        last = nc.scalar.activation(P_sb[:, u % R, j, :], src, ACT.Exp, bias=nmax[:, h:h + 1],
                                                    accum_out=sums[:, s, h:h + 1])
                    last.then_inc(exped.sem, 1)

                def copy_piece(t, s, p):
                    weighted.wait(act, t, (p + 1) * U // NP)
                    back(out_filled, act, t, 0, 2)
                    n = PW // 128
                    nc.scalar.activation(OT_sb[:, s, p * n:p * n + n, :], O_ps[s if NP == 1 else p][:, 0:PW],
                                         ACT.Copy).then_inc(piece_copied.sem, 1)

                def finish(t, s, u):
                    if (u + 1) * NP % U == 0:
                        copy_piece(t, s, (u + 1) * NP // U - 1)

                def slot(t, s, u, first, last):
                    old = lagging(t, s, u, first, WLAG)
                    if old and WLAG > LAG:
                        finish(*old)
                    groups = [] if last else [g for kind, g in sched[u] if kind == "p"]
                    for g in groups[:2]:
                        copy_proj(t + 1, 1 - s, g)
                    exps(t, s, u)
                    for g in groups[2:]:
                        copy_proj(t + 1, 1 - s, g)
                    if old and WLAG == LAG:
                        finish(*old)

                def before():
                    for g in range(GP):
                        copy_proj(0, 0, g)

                def after():
                    for old in drain:
                        finish(*old)
                steps(act, before, slot, after)

            @block.vector
            def _(dve):
                if "prepare_dve" in b:
                    b["prepare_dve"](dve)

                def maxima(t, s, u):
                    scored.wait(dve, t, u + 1)
                    if masked:
                        back(exped, dve, t, u, NB)
                        settle(dve, sc.passed)
                        fill, bound = b["mask"](t)
                        nc.vector.scalar_tensor_tensor(out=Sm[:, u % NB, 0, :], in0=S_ps[u % NB][:, 0:TK], scalar=fill,
                                                       in1=bound, op0=ALU.max, op1=ALU.min).then_inc(mask_part.sem, 1)
                        mask_part.wait(dve, t, u + 1)
                        src = Sm[:, u % NB, :, :]
                    else:
                        src = S_ps[u % NB][:, 0:HU * TK].rearrange("p (h k) -> p h k", h=HU)
                    nm = b["columns"](nmax, u) if "columns" in b else nmax[:, u * HU:(u + 1) * HU]
                    nc.vector.tensor_reduce(nm, src, AX.X, ALU.max, negate=True).then_inc(maxed.sem, 1)

                def copy_turned(t, u):
                    turned.wait(dve, t, u + 1)
                    back(weighted, dve, t, u, 2)
                    if KC == 1:
                        kn = kchunks[0][1]
                        last = nc.vector.tensor_copy(PT_sb[0:kn, u % 2, :, 0, :], PT_ps[0:kn, 0:HU * 128]
                                                     .rearrange("p (h q) -> p h q", h=HU))
                    else:
                        src = PT_ps[:, :].rearrange("p (h k q) -> p h k q", h=HU, k=KC)
                        for kc, (k0, kn) in enumerate(kchunks):
                            last = nc.vector.tensor_copy(PT_sb[0:kn, u % 2, :, kc, :], src[0:kn, :, kc, :])
                    last.then_inc(turned_copied.sem, 1)

                def divide(t, s, u):
                    exped.wait(dve, t, u + 1)
                    sm = b["columns"](sums[:, s, :], u) if "columns" in b else sums[:, s, u * HU:(u + 1) * HU]
                    nc.vector.reciprocal(rsum[:, u % 2, :], sm).then_inc(inverted.sem, 1)
                    inverted.wait(dve, t, u + 1)
                    nc.vector.tensor_tensor(P_sb[:, u % R, :, :], P_sb[:, u % R, :, :],
                                            rsum[:, u % 2, :].unsqueeze(2).to_broadcast([128, HU, TK]), ALU.mult) \
                        .then_inc(divided.sem, 1)

                def add(t):
                    out_filled.wait(dve, t, 1)
                    if "bo" in b:
                        biased.wait(dve, t, 1)
                    settle(dve, sc.passed)
                    xs = c["x"][:, t, :]
                    nc.vector.tensor_tensor(xs, out_ps[:, 0:128], xs, ALU.add).then_inc(added.sem, 1)

                def do_post(t, s):
                    proj_copied.wait(dve, t, 1)
                    cfg["post"](dve, b, t, s, post_part, posted)

                def slot(t, s, u, first, last):
                    old = lagging(t, s, u, first, LAG)
                    if u >= 2:
                        divide(t, s, u - 2)
                    elif not first:
                        divide(t - 1, 1 - s, u - 2 + U)
                    if old:
                        copy_turned(old[0], old[2])
                    maxima(t, s, u)
                    if post and u == cfg["post_slot"] and not last:
                        do_post(t + 1, 1 - s)
                    if u == U - 1 and not first:
                        add(t - 1)

                def after():
                    for u in (U - 2, U - 1):
                        divide(B - 1, (B - 1) % 2, u)
                    for u in range(U - LAG, U):
                        copy_turned(B - 1, u)
                    add(B - 1)
                steps(dve, (lambda: do_post(0, 0)) if post else (lambda: None), slot, after)


def loader(nc, sc, items, name="loaded"):
    loaded = sc.semaphore(name)

    def dma(sp):
        for dst, src in items:
            sp.dma_start(dst, src, allow_slow_non_contiguous=True).then_inc(loaded, 16)
    return dict(loaded=loaded, loads=len(items), dma=dma)


def start_loads(sc, b, before):
    sc.begin()
    before(b)


def spread_values(nc, v, s, src, keys):
    for j in range(4):
        last = nc.scalar.activation(v[0:keys, s, :, j, 8 * j:8 * j + 8],
                                    src.rearrange("p (u j d) -> p u j d", j=4, d=8)[:, :, j, :], ACT.Copy)
    return last


def weigh_small(nc, b, h, s, bank, pts):
    u, j = h // 4, h % 4
    return nc.tensor.matmul(bank[32 * u:32 * u + 32, 0:128], b["vb"][:, s, u, j, :], pts[0],
                            start=(j == 0), stop=(j == 3))


def l0_attention(nc, c, T, before):
    H, HD = 16, 8
    scale = float(HD) ** -0.5

    def load(sc):
        w = sc.sb("wqkv", [128, 384])
        wo = sc.sb("wo", [128, 128])
        bqk = sc.sb("bqk", [128, 2])
        bv = sc.sb("bv", [1, 128])
        bo = sc.sb("bo", [128, 128])
        bq_s = sc.sb("bq_scaled", [128, 1])
        bk_m = sc.sb("bk_masked", [128, 4])
        cur = sc.sb("tile", [128, 2, 128])
        q = sc.sb("q_t", [128, 2, 128])
        km = sc.sb("k_t", [128, 2, 4, 128])
        v = sc.sb("v", [128, 2, 4, 4, 32])
        zeroed = sc.semaphore("zeroed")
        biases = sc.semaphore("biases_ready")
        qb = T["L0_attn_qkv_b"]
        b = loader(nc, sc, [(w[:, :], T["L0_attn_qkv_w"]), (wo[:, :], T["L0_attn_proj_w"]),
                            (bqk[:, :], qb[0:256].rearrange("(a p) -> p a", p=128)),
                            (bv[:, :], qb[256:384].rearrange("(a p) -> a p", a=1)),
                            (bo[:, :], T["L0_attn_proj_b"].rearrange("(a p) -> a p", a=1).to_broadcast([128, 128]))])

        def prepare_act(act):
            nc.scalar.activation(bq_s[:, :], bqk[:, 0:1], ACT.Copy, scale=scale)
            nc.scalar.activation(bk_m[:, :], c["mask8"][:, :], ACT.Copy, scale=bqk[:, 1:2]).then_inc(biases, 1)
            act.wait_ge(biases, 1)
            act.wait_ge(zeroed, 1)

        b.update(w=w, bq=bq_s, bk=bk_m, bv=bv, cur=cur, q=q, km=km, vb=v, prepare_act=prepare_act,
                 tiles=lambda t, s: [(cur[:, s, :], c["nT"][:, bass.ds(t * 128, 128)])],
                 prepare_pool=lambda pool: nc.gpsimd.memset(v[:, :, :, :, :], 0.0).then_inc(zeroed, 1),
                 wo=lambda m: wo[:, :], bo=bo[:, :])
        return b

    def proj(b, g, s, bank):
        t = b["cur"][:, s, :]
        if g == 0:
            for i in range(2):
                last = nc.tensor.matmul(bank[:, i * 128:(i + 1) * 128], b["w"][:, i * 128:(i + 1) * 128], t,
                                        start=True, stop=True)
            return last
        nc.tensor.matmul(bank[:, 0:128], t, b["w"][:, 256:384], start=True, stop=False)
        return nc.tensor.matmul(bank[:, 0:128], c["ones"][0:1, :], b["bv"][:, :], start=False, stop=True)

    def copy(b, g, s, bank):
        if g == 0:
            nc.scalar.activation(b["q"][:, s, :], bank[:, 0:128], ACT.Identity, bias=b["bq"][:, 0:1], scale=scale)
            for j in range(4):
                last = nc.scalar.activation(b["km"][:, s, j, :], bank[:, 128:256], ACT.Identity,
                                            bias=b["bk"][:, j:j + 1], scale=c["mask8"][:, j:j + 1])
            return last
        return spread_values(nc, b["vb"], s, bank[:, 0:128], 128)

    def scores(b, u, s, bank):
        r = slice(32 * u, 32 * u + 32)
        return nc.tensor.matmul(bank[:, :], b["q"][r, s, :], b["km"][r, s, :, :].rearrange("p j k -> p (j k)"),
                                start=True, stop=True)

    attention(nc, c, "l0_attn", dict(weigh_lag=3, heads=H, units=4, v_groups=(1,), schedule=[[("p", 0)], [], [], [("p", 1), ("o", 0)]], keys=128, dv=HD, proj_groups=2, weigh=lambda *a: weigh_small(nc, *a),
                                     key_chunks=[(0, 128)], proj=proj, copy=copy, scores=scores,
                                     unit_heads=lambda u: [4 * u + j for j in range(4)]), load, before)


def row(ap):
    return ap.rearrange("(a p) -> a p", a=1)


def column(ap):
    return ap.rearrange("(p a) -> p a", a=1)


def l0_cross_attention(nc, c, T, before):
    H, HD = 4, 32
    MASK_FILL, UNBOUNDED = -2.3819763e+38, 3.4028234e+38
    NQK = 128 + SC

    def load(sc):
        wq = sc.sb("wq", [128, 2, 4, 32])
        wk = sc.sb("wk", [128, 2, 4, 32])
        wv = sc.sb("wv", [128, 32])
        wo = sc.sb("wo", [128, 128])
        rms = sc.sb("rms", [128, 2])
        table = sc.sb("rope", [128, 2, NQK])
        cur = sc.sb("tile", [128, 2, NQK])
        raw = sc.sb("raw", [128, 2, NQK])
        turned = sc.sb("rotated", [128, 2, NQK])
        qk = sc.sb("qk_t", [128, 2, NQK])
        v = sc.sb("v", [SC, 2, 32])
        bits = sc.sb("mask_bytes", [128, B * SC], U8)
        keep = sc.sb("keep", [128, B * SC])
        fill = sc.sb("fill", [128, B * SC])
        scaled = sc.semaphore("weights_scaled")
        masks = sc.semaphore("masks_ready")
        qw, kw = T["L0_xattn_q_w"], T["L0_xattn_kv_w"]
        items = [(wv[:, :], kw[1, 0]), (wo[:, :], T["L0_xattn_out_w"].rearrange("n h d -> (n h) d")),
                 (rms[:, 0:1], column(T["L0_xattn_rms_scale"])), (table[:, :, :], T["rope"]),
                 (bits[:, :], T["mask_BxS2_bk0"].rearrange("(a b) k -> a (b k)", a=1).to_broadcast([128, B * SC])),
                 (wq[:, 0, :, :], qw.rearrange("n d h -> d n h"))]
        for half in range(2):
            o, i = slice(16 * half, 16 * half + 16), slice(16 - 16 * half, 32 - 16 * half)
            items.append((wq[:, 1, :, o], qw[:, :, i].rearrange("n d h -> d n h")))
            for n in range(4):
                items.append((wk[:, 1, n, o], kw[0, 0, :, i]))
        for n in range(4):
            items.append((wk[:, 0, n, :], kw[0, 0]))
        b = loader(nc, sc, items)

        def prepare_act(act):
            nc.scalar.activation(rms[:, 1:2], rms[:, 0:1], ACT.Copy, bias=1.0).then_inc(scaled, 1)
            act.wait_ge(scaled, 1)
            for w in (wq[:, :, :, :], wk[:, :, :, :], wv[:, :]):
                last = nc.scalar.activation(w, w, ACT.Copy, scale=rms[:, 1:2])
            last.then_inc(scaled, 1)

        def prepare_dve(dve):
            dve.wait_ge(b["loaded"], 16 * b["loads"])
            nc.vector.tensor_copy(keep[:, :], bits[:, :]).then_inc(masks, 1)
            dve.wait_ge(masks, 1)
            nc.vector.tensor_scalar(fill[:, :], keep[:, :], -MASK_FILL, MASK_FILL, ALU.mult, ALU.add)
            nc.vector.tensor_scalar(keep[:, :], keep[:, :], UNBOUNDED, None, ALU.mult).then_inc(masks, 1)
            dve.wait_ge(masks, 2)
            nc.vector.tensor_tensor(fill[:, :], fill[:, :], keep[:, :], ALU.add).then_inc(masks, 1)
            dve.wait_ge(masks, 3)

        b.update(wq=wq, wk=wk, wv=wv, cur=cur, raw=raw, turned=turned, qk=qk, vb=v, table=table,
                 prepare_act=prepare_act, prepare_dve=prepare_dve, prepared=(scaled, 2),
                 tiles=lambda t, s: [(cur[:, s, 0:128], c["nT"][:, bass.ds(t * 128, 128)]),
                                     (cur[:, s, 128:NQK], c["cT"][:, bass.ds(t * SC, SC)])],
                 mask=lambda t: (MASK_FILL, fill[:, bass.ds(t * SC, SC)]),
                 wo=lambda m: wo[:, :])
        return b

    def proj(b, g, s, bank):
        if g == 0:
            for i in range(2):
                o = i * NQK
                nc.tensor.matmul(bank[:, o:o + 128], b["wq"][:, i, :, :].rearrange("p n h -> p (n h)"),
                                 b["cur"][:, s, 0:128], start=True, stop=True)
                last = nc.tensor.matmul(bank[:, o + 128:o + NQK], b["wk"][:, i, :, :].rearrange("p n h -> p (n h)"),
                                        b["cur"][:, s, 128:NQK], start=True, stop=True)
            return last
        return nc.tensor.matmul(bank[0:SC, 0:32], b["cur"][:, s, 128:NQK], b["wv"][:, :], start=True, stop=True)

    def copy(b, g, s, bank):
        if g == 0:
            return nc.scalar.activation(b["raw"][:, :, :], bank[:, 0:2 * NQK], ACT.Copy)
        return nc.scalar.activation(b["vb"][:, s, :], bank[0:SC, 0:32], ACT.Copy)

    def post(dve, b, t, s, part, posted):
        for i in range(2):
            last = nc.vector.tensor_tensor(b["turned"][:, i, :], b["raw"][:, i, :], b["table"][:, i, :], ALU.mult)
        last.then_inc(part.sem, 1)
        part.wait(dve, t, 1)
        nc.vector.tensor_tensor(b["qk"][:, s, :], b["turned"][:, 0, :], b["turned"][:, 1, :], ALU.add) \
            .then_inc(part.sem, 1)
        part.wait(dve, t, 2)
        nc.vector.tensor_scalar(b["qk"][:, s, 0:128], b["qk"][:, s, 0:128], float(HD) ** -0.5, None, ALU.mult) \
            .then_inc(posted.sem, 1)

    def scores(b, u, s, bank):
        r = slice(32 * u, 32 * u + 32)
        return nc.tensor.matmul(bank[:, 0:SC], b["qk"][r, s, 0:128], b["qk"][r, s, 128:NQK], start=True, stop=True)

    def weigh(b, h, s, bank, pts):
        return nc.tensor.matmul(bank[32 * h:32 * h + 32, 0:128], b["vb"][:, s, :], pts[0], start=True, stop=True)

    attention(nc, c, "l0_xattn", dict(weigh_lag=3, heads=H, units=4, keys=SC, dv=HD, proj_groups=2, weigh=weigh,
                                      v_groups=(1,), post_slot=1, schedule=[[("p", 0)], [], [], [("p", 1), ("o", 0)]],
                                      key_chunks=[(0, SC)], proj=proj, copy=copy, scores=scores, post=post,
                                      masked=True, unit_heads=lambda u: [u]), load, before)


def l1_cross_attention(nc, c, T, before):
    H, HD = 16, 64
    NK = SC + 128

    def load(sc):
        wq = sc.sb("wq", [128, 1024])
        wkv = sc.sb("wkv", [128, 2048])
        wo = sc.sb("wo", [128, 8, 128])
        cur = sc.sb("tile", [128, 2, NK])
        q = sc.sb("q_t", [128, 2, 8, 128])
        k = sc.sb("k_t", [128, 2, 8, NK])
        v = sc.sb("v", [128, 2, 2, 1024])
        b = loader(nc, sc, [(wq[:, :], T["L1_xattn_Wq"]), (wkv[:, :], T["L1_xattn_Wkv"]),
                            (wo[:, :, :], T["L1_xattn_Wo"].rearrange("(m p) d -> p m d", p=128))])

        def columns(nmax, u):
            o = 4 * (u // 2) + u % 2
            return nmax[:, o:o + 3:2]

        b.update(wq=wq, wkv=wkv, cur=cur, q=q, k=k, vb=v, columns=columns,
                 tiles=lambda t, s: [(cur[:, s, SC:NK], c["nT"][:, bass.ds(t * 128, 128)]),
                                     (cur[:, s, 0:SC], c["cT"][:, bass.ds(t * SC, SC)])],
                 wo=lambda m: wo[:, m, :])
        return b

    def proj(b, g, s, bank):
        if g < 2:
            for m in range(4):
                n = 4 * g + m
                last = nc.tensor.matmul(bank[:, m * 128:(m + 1) * 128], b["wq"][:, n * 128:(n + 1) * 128],
                                        b["cur"][:, s, SC:NK], start=True, stop=True)
        elif g < 6:
            for m in range(2):
                n = 2 * (g - 2) + m
                last = nc.tensor.matmul(bank[:, m * NK:(m + 1) * NK], b["wkv"][:, n * 128:(n + 1) * 128],
                                        b["cur"][:, s, :], start=True, stop=True)
        else:
            part, half = (g - 6) // 2, (g - 6) % 2
            t = b["cur"][:, s, SC:NK] if part else b["cur"][:, s, 0:SC]
            last = nc.tensor.matmul(bank[0:(SC, 128)[part], :], t,
                                    b["wkv"][:, 1024 + half * 512:1536 + half * 512], start=True, stop=True)
        return last

    def copy(b, g, s, bank):
        if g < 2:
            return nc.scalar.activation(b["q"][:, s, 4 * g:4 * g + 4, :], bank[:, :], ACT.Copy,
                                        scale=float(HD) ** -0.5)
        if g < 6:
            n = 2 * (g - 2)
            return nc.scalar.activation(b["k"][:, s, n:n + 2, :], bank[:, 0:2 * NK], ACT.Copy)
        part, half = (g - 6) // 2, (g - 6) % 2
        p = (SC, 128)[part]
        return nc.scalar.activation(b["vb"][0:p, s, part, half * 512:half * 512 + 512], bank[0:p, :], ACT.Copy)

    def scores(b, u, s, bank):
        r = slice(64 * (u % 2), 64 * (u % 2) + 64)
        for j in range(2):
            m = 2 * (u // 2) + j
            last = nc.tensor.matmul(bank[:, j * NK:(j + 1) * NK], b["q"][r, s, m, :], b["k"][r, s, m, :],
                                    start=True, stop=True)
        return last

    def weigh(b, h, s, bank, pts):
        r, m = 64 * (h % 2), h // 2 % 4
        for kc in range(2):
            last = nc.tensor.matmul(bank[r:r + 64, m * 128:(m + 1) * 128],
                                    b["vb"][0:(SC, 128)[kc], s, kc, h * HD:(h + 1) * HD], pts[kc],
                                    start=(kc == 0), stop=(kc == 1))
        return last

    attention(nc, c, "l1_xattn", dict(weigh_lag=4, heads=H, units=8, v_groups=(6, 7, 8, 9),
                                      schedule=[[("p", 0), ("p", 1)], [("p", 2), ("p", 3)], [("p", 4)],
                                                [("p", 5)], [("p", 6), ("o", 0)], [("p", 7)], [("p", 8)], [("p", 9)]],
                                       keys=NK, dv=HD, proj_groups=10, weigh=weigh,
                                      key_chunks=[(0, SC), (SC, 128)], proj=proj, copy=copy, scores=scores,
                                      unit_heads=lambda u: [4 * (u // 2) + u % 2 + 2 * j for j in range(2)]), load, before)


def l3_attention(nc, c, T, before):
    H, DK, DC = 8, 128, 32
    DB = DC + 1
    KR = 64
    scale = float(DK + DC) ** -0.5
    with Scope(nc, "l3_prep") as pre:
        wc = pre.sb("w_query", [DB, H, KR + 32])
        wg = pre.sb("w_out", [128, 2, 128])
        bg = pre.sb("b_out", [128, 128])
        wdq = pre.sb("w_down_q", [128, DB])
        wdk = pre.sb("w_down_k", [128, KR + 32])
        bdq = pre.sb("b_down_q", [DB, 1])
        bdk = pre.sb("b_down_k", [KR + 32, 1])
        filled, loaded = pre.semaphore("filled"), pre.semaphore("loaded")

        with Scope(nc, "l3_fold") as sc:
            ups = sc.sb("w_up", [DB, 3, H * DK])
            turned_w = sc.sb("w_up_t", [128, 3, H, DB])
            wo = sc.sb("wo", [128, H, 128])
            bo = sc.sb("bo", [1, 128])
            bias_row = sc.sb("bias_row", [1, 128])
            turned, copied, folded = (sc.semaphore(n) for n in ("turned", "copied", "folded"))
            items = [(wo[:, :, :], T["L3_attn_W_O"].rearrange("(m p) d -> p m d", p=128)),
                     (bo[:, :], row(T["L3_attn_b_O"])), (wdq[:, 0:DC], T["L3_attn_W_DQ"]),
                     (wdk[:, 0:DC], T["L3_attn_W_DKV"]), (wdk[:, KR:], T["L3_attn_W_KR"]),
                     (bdq[0:DC, :], column(T["L3_attn_b_DQ"])), (bdk[0:DC, :], column(T["L3_attn_b_DKV"])),
                     (bdk[KR:, :], column(T["L3_attn_b_KR"])),
                     (wc[0:DC, :, KR:], T["L3_attn_W_QR"].rearrange("k (h d) -> k h d", h=H)),
                     (wc[DC:DB, :, KR:], row(T["L3_attn_b_QR"]).rearrange("k (h d) -> k h d", h=H))]
            for i, n in enumerate(("UQ", "UK", "UV")):
                items += [(ups[0:DC, i, :], T["L3_attn_W_" + n]), (ups[DC:DB, i, :], row(T["L3_attn_b_" + n]))]
            def fill(pool):
                for tile in (wc[:, :, :], wdq[:, :], wdk[:, :], bdq[:, :]):
                    nc.gpsimd.memset(tile, 0.0)
                nc.gpsimd.memset(bdk[:, :], 0.0).then_inc(filled, 1)
                pool.wait_ge(filled, 1)
                nc.gpsimd.memset(bdq[DC:DB, :], 1.0).then_inc(filled, 1)
                pool.wait_ge(filled, 2)
                nc.gpsimd.memset(bdk[DC:DB, :], 1.0).then_inc(filled, 1)
                pool.wait_ge(filled, 3)

            def dma(sp):
                sp.wait_ge(filled, 3)
                for dst, src in items:
                    sp.dma_start(dst, src, allow_slow_non_contiguous=True).then_inc(loaded, 16)
            start_loads(sc, dict(prepare_pool=fill, dma=dma), before)
            up_ps = [sc.ps(f"up{i}", [128, 512]) for i in range(3)]
            m_ps, g_ps, b_ps = (sc.ps(n, [128, 512]) for n in ("m_ps", "g_ps", "b_ps"))
            sc.begin()
            with nc.Block() as block:
                @block.tensor
                def _(pe):
                    pe.wait_ge(loaded, 16 * len(items))
                    for i in range(3):
                        for h in range(H):
                            last = nc.tensor.transpose(up_ps[i][:, h * DB:(h + 1) * DB],
                                                       ups[:, i, h * DK:(h + 1) * DK], c["ident"][0:DB, 0:DB])
                    last.then_inc(turned, 1)
                    pe.wait_ge(copied, 3)
                    for h in range(H):
                        nc.tensor.matmul(m_ps[0:DB, h * DB:(h + 1) * DB], turned_w[:, 0, h, :], turned_w[:, 1, h, :],
                                         start=True, stop=True)
                    for h in range(H):
                        r = 32 * (h % 4)
                        nc.tensor.matmul(g_ps[r:r + 32, (h // 4) * 128:(h // 4 + 1) * 128], turned_w[:, 2, h, 0:DC],
                                         wo[:, h, :], start=True, stop=True)
                    for h in range(H):
                        nc.tensor.matmul(b_ps[0:1, 0:128], turned_w[:, 2, h, DC:DB], wo[:, h, :], start=(h == 0),
                                         stop=False)
                    nc.tensor.matmul(b_ps[0:1, 0:128], c["ones"][0:1, 0:1], bo[:, :], start=False, stop=True) \
                        .then_inc(folded, 1)
                    pe.wait_ge(copied, 4)
                    nc.tensor.matmul(b_ps[:, 128:256], c["ones"][0:1, :], bias_row[:, :], start=True, stop=True) \
                        .then_inc(folded, 1)

                @block.vector
                def _(dve):
                    dve.wait_ge(turned, 1)
                    for i in range(3):
                        nc.vector.tensor_copy(turned_w[:, i, :, :], up_ps[i][:, 0:H * DB].rearrange("p (h j) -> p h j", h=H)) \
                            .then_inc(copied, 1)
                    dve.wait_ge(folded, 1)
                    nc.vector.tensor_copy(wc[:, :, 0:DB], m_ps[0:DB, 0:H * DB].rearrange("p (h j) -> p h j", h=H))
                    nc.vector.tensor_copy(wg[:, :, :], g_ps[:, 0:256].rearrange("p (m d) -> p m d", m=2))
                    nc.vector.tensor_copy(bias_row[:, :], b_ps[0:1, 0:128]).then_inc(copied, 1)
                    dve.wait_ge(folded, 2)
                    nc.vector.tensor_copy(bg[:, :], b_ps[:, 128:256])

        def load(sc):
            cur = sc.sb("tile", [128, 2, 128])
            cq = sc.sb("compressed_q", [DB, 128])
            kk = sc.sb("keys", [KR + 32, 2, 128])
            qq = sc.sb("queries", [KR + 32, 2, H, 128])
            v = sc.sb("values", [128, 2, DC])
            return dict(loaded=loaded, loads=len(items), dma=lambda sp: None, cur=cur, cq=cq, kk=kk, qq=qq, vb=v,
                        tiles=lambda t, s: [(cur[:, s, :], c["nT"][:, bass.ds(t * 128, 128)])],
                        wo=lambda m: wg[:, m, :], bo=bg[:, :])

        def proj(b, g, s, bank):
            if g == 0:
                nc.tensor.matmul(bank[0:DB, 0:128], wdq[:, :], b["cur"][:, s, :], start=True, stop=True)
                return nc.tensor.matmul(bank[0:KR + 32, 128:256], wdk[:, :], b["cur"][:, s, :], start=True, stop=True)
            if g < 3:
                for m in range(4):
                    last = nc.tensor.matmul(bank[0:KR + 32, m * 128:(m + 1) * 128], wc[:, 4 * (g - 1) + m, :],
                                            b["cq"][:, :], start=True, stop=True)
                return last
            return nc.tensor.transpose(bank[:, 0:DC], b["kk"][0:DC, s, :], c["ident"][0:DC, 0:DC])

        def copy(b, g, s, bank):
            if g == 0:
                nc.scalar.activation(b["cq"][:, :], bank[0:DB, 0:128], ACT.Identity, bias=bdq[:, :])
                return nc.scalar.activation(b["kk"][:, s, :], bank[0:KR + 32, 128:256], ACT.Identity, bias=bdk[:, :])
            if g < 3:
                h = 4 * (g - 1)
                return nc.scalar.activation(b["qq"][:, s, h:h + 4, :], bank[0:KR + 32, :], ACT.Copy, scale=scale)
            return nc.scalar.activation(b["vb"][:, s, :], bank[:, 0:DC], ACT.Copy)

        def scores(b, u, s, bank):
            for j in range(2):
                last = nc.tensor.matmul(bank[:, j * 128:(j + 1) * 128], b["qq"][:, s, 2 * u + j, :], b["kk"][:, s, :],
                                        start=True, stop=True)
            return last

        def weigh(b, h, s, bank, pts):
            r = 32 * (h % 4)
            return nc.tensor.matmul(bank[r:r + 32, (h // 4) * 128:(h // 4 + 1) * 128], b["vb"][:, s, :], pts[0],
                                    start=True, stop=True)

        attention(nc, c, "l3_attn", dict(weigh_lag=3, heads=H, units=4, v_groups=(3,), keys=128, dv=DC, proj_groups=4, weigh=weigh,
                                         schedule=[[("p", 0)], [("p", 1)], [("p", 2)], [("p", 3), ("o", 0)]],
                                         key_chunks=[(0, 128)], proj=proj, copy=copy, scores=scores, first_feeds=True,
                                         unit_heads=lambda u: [2 * u + j for j in range(2)]), load,
                  lambda b: None)


def l3_cross_attention(nc, c, T, before):
    H, HD = 16, 8

    def load(sc):
        w = sc.sb("w_heads", [128, 3, 128])
        wo = sc.sb("wo", [128, 128])
        bo = sc.sb("bo", [128, 128])
        cur = sc.sb("tile", [128, 2, 128 + SC])
        q = sc.sb("q_t", [128, 2, 128])
        km = sc.sb("k_t", [128, 2, 4, SC])
        v = sc.sb("v", [SC, 2, 4, 4, 32])
        w8 = sc.sb("w_rows", [128, 3, HD])
        diag = sc.sb("own_columns", [128, H])
        mask_made, spread = sc.semaphore("mask_made"), sc.semaphore("weights_spread")
        items = [(wo[:, :], T["L3_xattn_Wo"]), (bo[:, :], row(T["L3_xattn_bo"]).to_broadcast([128, 128]))]
        for i, n in enumerate(("Wq", "Wk", "Wv")):
            items.append((w8[:, i, :], T["L3_xattn_" + n].unsqueeze(0).to_broadcast([H, HD, HD])))
        b = loader(nc, sc, items)

        def prepare_pool(pool):
            nc.gpsimd.memset(v[:, :, :, :, :], 0.0)
            nc.gpsimd.memset(diag[:, :], 1.0).then_inc(mask_made, 1)
            pool.wait_ge(mask_made, 1)
            nc.gpsimd.affine_select(out=diag[:, :], in_=diag[:, :], compare_op=ALU.is_ge, fill=0.0, base=0,
                                    pattern=[[-HD, H]], channel_multiplier=1).then_inc(mask_made, 1)
            pool.wait_ge(mask_made, 2)
            nc.gpsimd.affine_select(out=diag[:, :], in_=diag[:, :], compare_op=ALU.is_ge, fill=0.0, base=HD - 1,
                                    pattern=[[HD, H]], channel_multiplier=-1).then_inc(mask_made, 1)

        def prepare_dve(dve):
            dve.wait_ge(mask_made, 3)
            dve.wait_ge(b["loaded"], 16 * b["loads"])
            for i in range(3):
                last = nc.vector.tensor_tensor(w[:, i, :].rearrange("p (h d) -> p h d", h=H),
                                               w8[:, i, :].unsqueeze(1).to_broadcast([128, H, HD]),
                                               diag[:, :].unsqueeze(2).to_broadcast([128, H, HD]), ALU.mult)
            last.then_inc(spread, 1)

        b.update(w=w, cur=cur, q=q, km=km, vb=v, prepare_pool=prepare_pool, prepare_dve=prepare_dve,
                 prepared=(spread, 1),
                 tiles=lambda t, s: [(cur[:, s, 0:128], c["nT"][:, bass.ds(t * 128, 128)]),
                                     (cur[:, s, 128:128 + SC], c["cT"][:, bass.ds(t * SC, SC)])],
                 wo=lambda m: wo[:, :], bo=bo[:, :])
        return b

    def proj(b, g, s, bank):
        tq, tk = b["cur"][:, s, 0:128], b["cur"][:, s, 128:128 + SC]
        if g == 0:
            nc.tensor.matmul(bank[:, 0:128], b["w"][:, 0, :], tq, start=True, stop=True)
            return nc.tensor.matmul(bank[:, 128:128 + SC], b["w"][:, 1, :], tk, start=True, stop=True)
        return nc.tensor.matmul(bank[0:SC, 0:128], tk, b["w"][:, 2, :], start=True, stop=True)

    def copy(b, g, s, bank):
        if g == 0:
            nc.scalar.activation(b["q"][:, s, :], bank[:, 0:128], ACT.Copy, scale=float(D) ** -0.5)
            for j in range(4):
                last = nc.scalar.activation(b["km"][:, s, j, :], bank[:, 128:128 + SC], ACT.Copy,
                                            scale=c["mask8"][:, j:j + 1])
            return last
        return spread_values(nc, b["vb"], s, bank[0:SC, 0:128], SC)

    def scores(b, u, s, bank):
        r = slice(32 * u, 32 * u + 32)
        return nc.tensor.matmul(bank[:, 0:4 * SC], b["q"][r, s, :], b["km"][r, s, :, :].rearrange("p j k -> p (j k)"),
                                start=True, stop=True)

    attention(nc, c, "l3_xattn", dict(weigh_lag=3, heads=H, units=4, v_groups=(1,), schedule=[[("p", 0)], [], [], [("p", 1), ("o", 0)]],
                                       keys=SC, dv=HD, proj_groups=2, weigh=lambda *a: weigh_small(nc, *a),
                                      key_chunks=[(0, SC)], proj=proj, copy=copy, scores=scores,
                                      unit_heads=lambda u: [4 * u + j for j in range(4)]), load, before)


def top_two(nc, dve, sc, w, val, n, m, first_of, part):
    count = [0]

    def then(ins):
        count[0] += 1
        ins.then_inc(part, 1)
        dve.wait_ge(part, count[0])

    def bc(ap):
        return ap.unsqueeze(2).to_broadcast([128, n, m])
    src = val
    for r in range(2):
        then(nc.vector.tensor_reduce(w["top"][:, r, 0:n], src, AX.X, ALU.max))
        then(nc.vector.tensor_tensor(w["eq"], src, bc(w["top"][:, r, 0:n]), ALU.is_equal))
        then(nc.vector.tensor_scalar(w["eq"], w["eq"], -float(m), float(m), ALU.mult, ALU.add))
        then(nc.vector.tensor_tensor(w["eq"], w["eq"], first_of, ALU.add))
        then(nc.vector.tensor_reduce(w["index"][:, r, 0:n], w["eq"], AX.X, ALU.min))
        then(nc.vector.tensor_tensor(w["hot"][r], first_of, bc(w["index"][:, r, 0:n]), ALU.is_equal))
        if r == 0:
            then(nc.vector.tensor_scalar(w["rest"], w["hot"][0], -1.0e38, None, ALU.mult))
            then(nc.vector.tensor_tensor(w["rest"], w["rest"], val, ALU.add))
            src = w["rest"]
    return then


def route_and_mix(nc, c, T, name, E, sigmoid_first, router, bias, experts, before):
    shared = len(experts) > 1
    NE = E + (1 if shared else 0)
    G, N = 4, B // 4
    with Scope(nc, name) as sc:
        wg = sc.sb("w_gate", [128, NE, 256])
        wu = sc.sb("w_up", [128, NE, 256])
        wd = sc.sb("w_down", [128, NE, 2, 128])
        weights = sc.sb("token_weights", [128, B, NE])
        cur = sc.sb("tiles", [128, 2, 512])
        items = []
        for first, (g, u, d) in zip((0, E), experts):
            r = slice(first, first + g.shape[0])
            items += [(wg[:, r, :], g.rearrange("e k i -> k e i")), (wu[:, r, :], u.rearrange("e k i -> k e i"))]
            for i in range(2):
                items.append((wd[:, r, i, :], d.rearrange("e (i p) d -> i p e d", p=128)[i]))
        b = loader(nc, sc, items)
        rw = sc.sb("router", [128, E])
        rb = sc.sb("router_bias", [1, E])
        rl = loader(nc, sc, [(rw[:, :], router)] + ([(rb[:, :], bias)] if bias is not None else []), "router_loaded")

        def dma(sp):
            rl["dma"](sp)
            b["dma"](sp)
        start_loads(sc, dict(dma=dma), before)

        with Scope(nc, name + "_route") as rt:
            iota_i = rt.sb("index_int", [128, B, E], I32)
            iota = rt.sb("index", [128, B, E])
            val = rt.sb("values", [128, B, E])
            w = dict(top=rt.sb("top", [128, 2, B]), index=rt.sb("top_index", [128, 2, B]),
                     eq=rt.sb("eq", [128, B, E])[:, :, :], rest=rt.sb("rest", [128, B, E])[:, :, :],
                     hot=[rt.sb(f"hot{i}", [128, B, E])[:, :, :] for i in range(2)])
            gates = rt.sb("gates", [128, 2, B])
            total = rt.sb("total", [128, B])
            R_ps = rt.ps("logits", [128, B * E])
            tile_ready = [rt.counter(f"tile_ready{s}") for s in range(2)]
            routed = [rt.counter(f"routed{s}") for s in range(2)]
            index_made, values_ready, top_part, gates_ready, sig_done = (
                rt.semaphore(n) for n in ("index_made", "values_ready", "top_part", "gates_ready", "sig_done"))
            rt.begin()
            with nc.Block() as block:
                @block.gpsimd
                def _(pool):
                    nc.gpsimd.iota(iota_i[:, :, :], pattern=[[0, B], [1, E]], base=0, channel_multiplier=0) \
                        .then_inc(index_made, 1)

                @block.tensor
                def _(pe):
                    pe.wait_ge(rl["loaded"], 16 * rl["loads"])
                    with pe.Fori(0, N // 2) as it:
                        for s in range(2):
                            t = it * 2 + s
                            tile_ready[s].wait(pe, it, 1)
                            settle(pe, rt.passed)
                            for j in range(G):
                                o = R_ps[:, bass.ds(t * (G * E) + j * E, E)]
                                last = nc.tensor.matmul(o, cur[:, s, j * 128:(j + 1) * 128], rw[:, :],
                                                        start=True, stop=bias is None)
                                if bias is not None:
                                    last = nc.tensor.matmul(o, c["ones"][0:1, :], rb[:, :], start=False, stop=True)
                            last.then_inc(routed[s].sem, 1)

                @block.scalar
                def _(act):
                    with act.Fori(0, N // 2) as it:
                        routed[1].wait_steps(act, it)
                        settle(act, rt.passed)
                        nc.scalar.activation(cur[:, 1, :], c["nT"][:, bass.ds((it * 2 + 1) * 512, 512)],
                                             ACT.Copy).then_inc(tile_ready[1].sem, 1)
                    act.wait_ge(routed[0].sem, N // 2 + 1)
                    act.wait_ge(routed[1].sem, N // 2 + 1)
                    flat = val[:, :, :].rearrange("p b e -> p (b e)")
                    nc.scalar.activation(flat, R_ps[:, :], ACT.Sigmoid if sigmoid_first else ACT.Copy) \
                        .then_inc(values_ready, 1)
                    if not sigmoid_first:
                        act.wait_ge(gates_ready, 1)
                        nc.scalar.activation(gates[:, :, :], w["top"][:, :, :], ACT.Sigmoid).then_inc(sig_done, 1)

                @block.vector
                def _(dve):
                    dve.wait_ge(index_made, 1)
                    nc.vector.tensor_copy(iota[:, :, :], iota_i[:, :, :]).then_inc(index_made, 1)
                    dve.wait_ge(index_made, 2)
                    with dve.Fori(0, N // 2) as it:
                        routed[0].wait_steps(dve, it)
                        settle(dve, rt.passed)
                        nc.vector.tensor_copy(cur[:, 0, :], c["nT"][:, bass.ds(it * 1024, 512)]) \
                            .then_inc(tile_ready[0].sem, 1)
                    dve.wait_ge(values_ready, 1)
                    then = top_two(nc, dve, rt, w, val[:, :, :], B, E, iota[:, :, :], top_part)
                    g = w["top"]
                    if not sigmoid_first:
                        then(nc.vector.tensor_copy(total[:, :], g[:, 0, :]))
                        nc.vector.tensor_copy(total[:, :], g[:, 1, :]).then_inc(gates_ready, 1)
                        dve.wait_ge(gates_ready, 1)
                        dve.wait_ge(sig_done, 1)
                        g = gates
                    then(nc.vector.tensor_tensor(total[:, :], g[:, 0, :], g[:, 1, :], ALU.add))
                    if not sigmoid_first:
                        then(nc.vector.tensor_scalar(total[:, :], total[:, :], 1e-10, None, ALU.add))
                    then(nc.vector.reciprocal(total[:, :], total[:, :]))
                    for r in range(2):
                        then(nc.vector.tensor_tensor(g[:, r, :], g[:, r, :], total[:, :], ALU.mult))
                        then(nc.vector.tensor_tensor(w["hot"][r], w["hot"][r],
                                                     g[:, r, :].unsqueeze(2).to_broadcast([128, B, E]), ALU.mult))
                    if shared:
                        then(nc.vector.memset(weights[:, :, E:NE], 1.0))
                    then(nc.vector.tensor_tensor(weights[:, :, 0:E], w["hot"][0], w["hot"][1], ALU.add))

        SG = sc.sb("silu", [128, 2, 512])
        Hb = sc.sb("hidden", [128, 2, 2, 512])
        A = sc.sb("weighted_out", [128, 2, 512])
        gu = [[sc.ps(f"{n}{i}", [128, 512]) for n in ("gate", "up")] for i in range(2)]
        Yp = [sc.ps(f"down{i}", [128, 512]) for i in range(2)]
        tile_ready = sc.counter("tile_ready")
        hidden_done = sc.counter("gate_up_done", 2 * NE)
        silu_done = sc.counter("silu_done", 2 * NE)
        h_done = sc.counter("h_done", 2 * NE)
        down_done = sc.counter("down_done", NE)
        weighted = sc.counter("weighted", NE)
        added = sc.counter("added", NE)

        def two_back(sig, eng, t, n):
            if not isinstance(t, int) or t * sig.n + n >= 2:
                sig.wait(eng, t, n - 1)

        def parity(s, e):
            return (s * NE + e) % 2

        def steps(eng, body, last):
            body(0, 0, True)
            with eng.Fori(0, (N - 2) // 2) as it:
                for s in range(2):
                    body(it * 2 + 1 + s, (1 + s) % 2, False)
            body(N - 1, (N - 1) % 2, False)
            last(N - 1, (N - 1) % 2)

        sc.begin()
        with nc.Block() as block:
            @block.gpsimd
            def _(pool):
                def tiles(t, s):
                    if not isinstance(t, int) or t >= 2:
                        hidden_done.wait_steps(pool, t - 1)
                    settle(pool, sc.passed)
                    nc.gpsimd.tensor_copy(cur[:, s, :], c["nT"][:, bass.ds(t * 512, 512)]).then_inc(tile_ready.sem, 1)

                def body(t, s, first):
                    if first:
                        tiles(0, 0)
                    if not (isinstance(t, int) and t == N - 1):
                        tiles(t + 1, 1 - s)
                    for e in range(NE):
                        weighted.wait(pool, t, e + 1)
                        added.wait(pool, t, e)
                        settle(pool, sc.passed)
                        xs = c["x"][:, bass.ds(t * G, G), :]
                        nc.gpsimd.tensor_tensor(xs, xs, A[:, parity(s, e), :].rearrange("p (g d) -> p g d", g=G),
                                                ALU.add).then_inc(added.sem, 1)
                steps(pool, body, lambda t, s: None)

            @block.tensor
            def _(pe):
                pe.wait_ge(b["loaded"], 16 * b["loads"])

                def up(t, s, n):
                    two_back(h_done, pe, t, n)
                    settle(pe, sc.passed)
                    e, i = n // 2, n % 2
                    for w_, o in ((wg, gu[n % 2][0]), (wu, gu[n % 2][1])):
                        last = nc.tensor.matmul(o[:, :], w_[:, e, i * 128:(i + 1) * 128], cur[:, s, :],
                                                start=True, stop=True)
                    last.then_inc(hidden_done.sem, 1)

                def down(t, s, e):
                    h_done.wait(pe, t, 2 * e + 2)
                    two_back(weighted, pe, t, e)
                    settle(pe, sc.passed)
                    p = parity(s, e)
                    for j in range(G):
                        for i in range(2):
                            last = nc.tensor.matmul(Yp[p][:, j * 128:(j + 1) * 128],
                                                    Hb[:, p, i, j * 128:(j + 1) * 128], wd[:, e, i, :],
                                                    start=(i == 0), stop=(i == 1))
                    last.then_inc(down_done.sem, 1)

                def body(t, s, first):
                    tile_ready.wait(pe, t, 1)
                    for e in range(NE):
                        up(t, s, 2 * e)
                        up(t, s, 2 * e + 1)
                        if e:
                            down(t, s, e - 1)
                        elif not first:
                            down(t - 1, 1 - s, NE - 1)
                steps(pe, body, lambda t, s: down(t, s, NE - 1))

            @block.scalar
            def _(act):
                def body(t, s, first):
                    for n in range(2 * NE):
                        hidden_done.wait(act, t, n + 1)
                        two_back(h_done, act, t, n)
                        nc.scalar.activation(SG[:, n % 2, :], gu[n % 2][0][:, :], ACT.Silu).then_inc(silu_done.sem, 1)
                steps(act, body, lambda t, s: None)

            @block.vector
            def _(dve):
                def weigh(t, s, e):
                    down_done.wait(dve, t, e + 1)
                    two_back(added, dve, t, e)
                    p = parity(s, e)
                    nc.vector.tensor_tensor(A[:, p, :].rearrange("p (g d) -> p g d", g=G),
                                            Yp[p][:, :].rearrange("p (g d) -> p g d", g=G),
                                            weights[:, bass.ds(t * G, G), e:e + 1].to_broadcast([128, G, 128]),
                                            ALU.mult).then_inc(weighted.sem, 1)

                def body(t, s, first):
                    for n in range(2 * NE):
                        e, i = n // 2, n % 2
                        silu_done.wait(dve, t, n + 1)
                        two_back(down_done, dve, t, e)
                        nc.vector.tensor_tensor(Hb[:, parity(s, e), i, :], SG[:, n % 2, :], gu[n % 2][1][:, :],
                                                ALU.mult).then_inc(h_done.sem, 1)
                        if i and e:
                            weigh(t, s, e - 1)
                        elif i and not first:
                            weigh(t - 1, 1 - s, NE - 1)
                steps(dve, body, lambda t, s: weigh(t, s, NE - 1))


def l2_ffn(nc, c, T, before):
    def one(name):
        return T["L2_ffn_shared_" + name].unsqueeze(0)
    route_and_mix(nc, c, T, "l2_ffn", 8, True, T["L2_ffn_router_w"], row(T["L2_ffn_routing_bias"]),
                  [(T["L2_ffn_gate_w"], T["L2_ffn_up_w"], T["L2_ffn_down_w"]), (one("gate"), one("up"), one("down"))],
                  before)


def l3_ffn(nc, c, T, before):
    route_and_mix(nc, c, T, "l3_ffn", 8, False, T["L3_ffn_router_w"], None,
                  [(T["L3_ffn_w_gate"], T["L3_ffn_w_up"], T["L3_ffn_w_down"])], before)


def l1_attention(nc, c, T, before):
    G, N = 4, B // 4
    scale = float(D) ** -0.5
    with Scope(nc, "l1_attn") as sc:
        w = sc.sb("w", [128, 3, 128])
        bq = sc.sb("bq", [128, 1])
        bk = sc.sb("bk", [128, 1])
        bv = sc.sb("bv", [1, 128])
        bq_s = sc.sb("bq_scaled", [128, 1])
        causal = sc.sb("causal", [128, 128])
        cur = sc.sb("tiles", [128, 2, 512])
        q = sc.sb("q_t", [128, 2, 512])
        k = sc.sb("k_t", [128, 2, 512])
        v = sc.sb("v", [128, 2, G, 128])
        Sm = sc.sb("masked", [128, 2, G, 128])
        P = sc.sb("probs", [128, 2, G, 128])
        nmax = sc.sb("neg_max", [128, 2, G])
        sums = sc.sb("sums", [128, 2, G])
        rs = sc.sb("rsum", [128, 2, G])
        items = [(w[:, i, :], T["L1_attn_W" + n]) for i, n in enumerate("qkv")]
        items += [(bq[:, :], column(T["L1_attn_bq"])), (bk[:, :], column(T["L1_attn_bk"])), (bv[:, :], row(T["L1_attn_bv"]))]
        b = loader(nc, sc, items)
        start_loads(sc, b, before)
        q_ps, k_ps, v_ps = (sc.ps(n, [128, 512]) for n in ("q_ps", "k_ps", "v_ps"))
        s_ps, o_ps = sc.ps("s_ps", [128, 512]), sc.ps("o_ps", [128, 512])
        names = ("tile_ready", "qk_done", "v_done", "qk_copied", "scored", "masked", "maxed", "exped", "inverted",
                 "v_scaled", "out_done", "added")
        tile_ready, qk_done, v_done, qk_copied, scored, masked_, maxed, exped, inverted, v_scaled, out_done, added = (
            sc.counter(n) for n in names)
        causal_made, bias_ready = sc.semaphore("causal_made"), sc.semaphore("bias_ready")

        def pairs(eng, body):
            with eng.Fori(0, N // 2) as it:
                for s in range(2):
                    body(it * 2 + s, s)

        sc.begin()
        with nc.Block() as block:
            @block.gpsimd
            def _(pool):
                nc.gpsimd.memset(causal[:, :], 0.0).then_inc(causal_made, 1)
                pool.wait_ge(causal_made, 1)
                nc.gpsimd.affine_select(out=causal[:, :], in_=causal[:, :], compare_op=ALU.is_ge, fill=-3.0e38,
                                        base=0, pattern=[[1, 128]], channel_multiplier=-1).then_inc(causal_made, 1)

                def body(t, s):
                    v_done.wait_steps(pool, t - s)
                    settle(pool, sc.passed)
                    nc.gpsimd.tensor_copy(cur[:, s, :], c["nT"][:, bass.ds(t * 512, 512)]).then_inc(tile_ready.sem, 1)
                pairs(pool, body)

            @block.tensor
            def _(pe):
                pe.wait_ge(b["loaded"], 16 * b["loads"])

                def body(t, s):
                    tile_ready.wait(pe, t, 1)
                    qk_copied.wait_steps(pe, t)
                    settle(pe, sc.passed)
                    nc.tensor.matmul(q_ps[:, :], w[:, 0, :], cur[:, s, :], start=True, stop=True)
                    nc.tensor.matmul(k_ps[:, :], w[:, 1, :], cur[:, s, :], start=True, stop=True) \
                        .then_inc(qk_done.sem, 1)
                    v_scaled.wait_steps(pe, t)
                    settle(pe, sc.passed)
                    for j in range(G):
                        o = v_ps[:, j * 128:(j + 1) * 128]
                        nc.tensor.matmul(o, cur[:, s, j * 128:(j + 1) * 128], w[:, 2, :], start=True, stop=False)
                        last = nc.tensor.matmul(o, c["ones"][0:1, :], bv[:, :], start=False, stop=True)
                    last.then_inc(v_done.sem, 1)
                    qk_copied.wait(pe, t, 1)
                    masked_.wait_steps(pe, t)
                    settle(pe, sc.passed)
                    for j in range(G):
                        r = slice(j * 128, (j + 1) * 128)
                        last = nc.tensor.matmul(s_ps[:, r], k[:, s, r], q[:, s, r], start=True, stop=True)
                    last.then_inc(scored.sem, 1)
                    v_scaled.wait(pe, t, 1)
                    added.wait_steps(pe, t)
                    settle(pe, sc.passed)
                    for j in range(G):
                        last = nc.tensor.matmul(o_ps[:, j * 128:(j + 1) * 128], P[:, s, j, :], v[:, s, j, :],
                                                start=True, stop=True)
                    last.then_inc(out_done.sem, 1)
                pairs(pe, body)

            @block.scalar
            def _(act):
                act.wait_ge(b["loaded"], 16 * b["loads"])
                nc.scalar.activation(bq_s[:, :], bq[:, :], ACT.Copy, scale=scale).then_inc(bias_ready, 1)
                act.wait_ge(bias_ready, 1)

                def body(t, s):
                    qk_done.wait(act, t, 1)
                    scored.wait_steps(act, t)
                    settle(act, sc.passed)
                    nc.scalar.activation(q[:, s, :], q_ps[:, :], ACT.Identity, bias=bq_s[:, 0:1], scale=scale)
                    nc.scalar.activation(k[:, s, :], k_ps[:, :], ACT.Identity, bias=bk[:, 0:1]) \
                        .then_inc(qk_copied.sem, 1)
                    maxed.wait(act, t, 1)
                    out_done.wait_steps(act, t)
                    settle(act, sc.passed)
                    for j in range(G):
                        last = nc.scalar.activation(P[:, s, j, :], Sm[:, s, j, :], ACT.Exp, bias=nmax[:, s, j:j + 1],
                                                    accum_out=sums[:, s, j:j + 1])
                    last.then_inc(exped.sem, 1)
                pairs(act, body)

            @block.vector
            def _(dve):
                dve.wait_ge(causal_made, 2)

                def body(t, s):
                    scored.wait(dve, t, 1)
                    nc.vector.tensor_tensor(Sm[:, s, :, :], s_ps[:, :].rearrange("p (g i) -> p g i", g=G),
                                            causal[:, :].unsqueeze(1).to_broadcast([128, G, 128]), ALU.add) \
                        .then_inc(masked_.sem, 1)
                    masked_.wait(dve, t, 1)
                    nc.vector.tensor_reduce(nmax[:, s, :], Sm[:, s, :, :], AX.X, ALU.max, negate=True) \
                        .then_inc(maxed.sem, 1)
                    exped.wait(dve, t, 1)
                    nc.vector.reciprocal(rs[:, s, :], sums[:, s, :]).then_inc(inverted.sem, 1)
                    inverted.wait(dve, t, 1)
                    v_done.wait(dve, t, 1)
                    nc.vector.tensor_tensor(v[:, s, :, :], v_ps[:, :].rearrange("p (g i) -> p g i", g=G),
                                            rs[:, s, :].unsqueeze(2).to_broadcast([128, G, 128]), ALU.mult) \
                        .then_inc(v_scaled.sem, 1)
                    out_done.wait(dve, t, 1)
                    settle(dve, sc.passed)
                    xs = c["x"][:, bass.ds(t * G, G), :]
                    nc.vector.tensor_tensor(xs, o_ps[:, :].rearrange("p (g i) -> p g i", g=G), xs, ALU.add) \
                        .then_inc(added.sem, 1)
                pairs(dve, body)


def l2_attention(nc, c, T, before):
    G, N, H = 4, B // 4, 16
    const = 1.0 / float(np.sqrt(np.float32(D // H))) / D
    with Scope(nc, "l2_attn") as sc:
        w = sc.sb("w", [128, 4, 128])
        bo = sc.sb("bo", [128, 128])
        cur = sc.sb("tiles", [128, 2, 512])
        e_ = sc.sb("exps", [128, 2, 2, G, 128])
        et = sc.sb("exps_t", [128, 2, 2, G, 128])
        v = sc.sb("v", [128, 2, G, 128])
        kv = sc.sb("kv", [128, 2, G, 128])
        yt = sc.sb("y_t", [128, 2, 512])
        out = sc.sb("out", [128, 2, G, 128])
        nmax = sc.sb("neg_max", [128, 2, 2, G])
        sums = sc.sb("sums", [128, 2, 2, G])
        rs = sc.sb("rsum", [128, 2, 2, G])
        b = loader(nc, sc, [(w[:, i, :], T["L2_attn_W" + n]) for i, n in enumerate("qkvo")] +
                   [(bo[:, :], row(T["L2_attn_bo"]).to_broadcast([128, 128]))])
        start_loads(sc, b, before)
        names = ("q_ps", "k_ps", "v_ps", "qt_ps", "kt_ps", "kv_ps", "y_ps", "o_ps")
        q_ps, k_ps, v_ps, qt_ps, kt_ps, kv_ps, y_ps, o_ps = (sc.ps(n, [128, 512]) for n in names)
        names = ("tile_ready", "projected", "maxed", "exped", "v_copied", "turned", "turned_copied", "inverted",
                 "kv_done", "kv_copied", "y_done", "y_copied", "out_done", "out_scaled")
        (tile_ready, projected, maxed, exped, v_copied, turned, turned_copied, inverted, kv_done, kv_copied, y_done,
         y_copied, out_done, out_scaled) = (sc.counter(n) for n in names)
        added = sc.counter("added", 2)
        scaled = sc.counter("divisors_scaled")

        def pairs(eng, front, back):
            front(0, 0)
            with eng.Fori(0, (N - 2) // 2) as it:
                for s in range(2):
                    t = it * 2 + 1 + s
                    front(t, (1 + s) % 2)
                    back(it * 2 + s, s)
            front(N - 1, (N - 1) % 2)
            back(N - 2, (N - 2) % 2)
            back(N - 1, (N - 1) % 2)

        sc.begin()
        with nc.Block() as block:
            @block.gpsimd
            def _(pool):
                pool.wait_ge(b["loaded"], 16 * b["loads"])

                def front(t, s):
                    if not isinstance(t, int) or t >= 2:
                        projected.wait_steps(pool, t - 1)
                    settle(pool, sc.passed)
                    nc.gpsimd.tensor_copy(cur[:, s, :], c["nT"][:, bass.ds(t * 512, 512)]).then_inc(tile_ready.sem, 1)

                def back(t, s):
                    out_scaled.wait(pool, t, 1)
                    settle(pool, sc.passed)
                    nc.gpsimd.tensor_tensor(out[:, s, :, :], out[:, s, :, :],
                                            bo[:, :].unsqueeze(1).to_broadcast([128, G, 128]), ALU.add) \
                        .then_inc(added.sem, 1)
                    added.wait(pool, t, 1)
                    settle(pool, sc.passed)
                    xs = c["x"][:, bass.ds(t * G, G), :]
                    nc.gpsimd.tensor_tensor(xs, xs, out[:, s, :, :], ALU.add).then_inc(added.sem, 1)
                pairs(pool, front, back)

            @block.tensor
            def _(pe):
                pe.wait_ge(b["loaded"], 16 * b["loads"])

                def front(t, s):
                    tile_ready.wait(pe, t, 1)
                    exped.wait_steps(pe, t)
                    v_copied.wait_steps(pe, t)
                    settle(pe, sc.passed)
                    nc.tensor.matmul(k_ps[:, :], w[:, 1, :], cur[:, s, :], start=True, stop=True)
                    for i, o in ((0, q_ps), (2, v_ps)):
                        for j in range(G):
                            last = nc.tensor.matmul(o[:, j * 128:(j + 1) * 128], cur[:, s, j * 128:(j + 1) * 128],
                                                    w[:, i, :], start=True, stop=True)
                    last.then_inc(projected.sem, 1)

                def back(t, s):
                    exped.wait(pe, t, 1)
                    turned_copied.wait_steps(pe, t)
                    settle(pe, sc.passed)
                    for i, o in ((0, qt_ps), (1, kt_ps)):
                        for j in range(G):
                            last = nc.tensor.transpose(o[:, j * 128:(j + 1) * 128], e_[:, s, i, j, :], c["ident"][:, :])
                    last.then_inc(turned.sem, 1)
                    turned_copied.wait(pe, t, 1)
                    v_copied.wait(pe, t, 1)
                    kv_copied.wait_steps(pe, t)
                    settle(pe, sc.passed)
                    for j in range(G):
                        last = nc.tensor.matmul(kv_ps[:, j * 128:(j + 1) * 128], et[:, s, 1, j, :], v[:, s, j, :],
                                                start=True, stop=True)
                    last.then_inc(kv_done.sem, 1)
                    kv_copied.wait(pe, t, 1)
                    y_copied.wait_steps(pe, t)
                    settle(pe, sc.passed)
                    for j in range(G):
                        last = nc.tensor.matmul(y_ps[:, j * 128:(j + 1) * 128], kv[:, s, j, :], et[:, s, 0, j, :],
                                                start=True, stop=True)
                    last.then_inc(y_done.sem, 1)
                    y_copied.wait(pe, t, 1)
                    out_scaled.wait_steps(pe, t)
                    settle(pe, sc.passed)
                    for j in range(G):
                        last = nc.tensor.matmul(o_ps[:, j * 128:(j + 1) * 128], yt[:, s, j * 128:(j + 1) * 128],
                                                w[:, 3, :], start=True, stop=True)
                    last.then_inc(out_done.sem, 1)
                pairs(pe, front, back)

            @block.scalar
            def _(act):
                def front(t, s):
                    maxed.wait(act, t, 1)
                    if not isinstance(t, int) or t >= 2:
                        turned.wait_steps(act, t - 1)
                        inverted.wait_steps(act, t - 1)
                        kv_done.wait_steps(act, t - 1)
                    settle(act, sc.passed)
                    for i, o in ((0, q_ps), (1, k_ps)):
                        for j in range(G):
                            last = nc.scalar.activation(e_[:, s, i, j, :], o[:, j * 128:(j + 1) * 128], ACT.Exp,
                                                        bias=nmax[:, s, i, j:j + 1], accum_out=sums[:, s, i, j:j + 1])
                    last.then_inc(exped.sem, 1)
                    nc.scalar.activation(v[:, s, :, :], v_ps[:, :], ACT.Copy).then_inc(v_copied.sem, 1)

                def back(t, s):
                    y_done.wait(act, t, 1)
                    nc.scalar.activation(yt[:, s, :], y_ps[:, :], ACT.Copy).then_inc(y_copied.sem, 1)
                pairs(act, front, back)

            @block.vector
            def _(dve):
                def front(t, s):
                    projected.wait(dve, t, 1)
                    settle(dve, sc.passed)
                    for i, o in ((0, q_ps), (1, k_ps)):
                        last = nc.vector.tensor_reduce(nmax[:, s, i, :], o[:, :].rearrange("p (g f) -> p g f", g=G),
                                                       AX.X, ALU.max, negate=True)
                    last.then_inc(maxed.sem, 1)

                def back(t, s):
                    exped.wait(dve, t, 1)
                    nc.vector.reciprocal(rs[:, s, :, :], sums[:, s, :, :]).then_inc(inverted.sem, 1)
                    inverted.wait(dve, t, 1)
                    nc.vector.tensor_scalar(rs[:, s, 1, :], rs[:, s, 1, :], const, None, ALU.mult) \
                        .then_inc(scaled.sem, 1)
                    turned.wait(dve, t, 1)
                    for i, o in ((0, qt_ps), (1, kt_ps)):
                        last = nc.vector.tensor_copy(et[:, s, i, :, :], o[:, :].rearrange("p (g f) -> p g f", g=G))
                    last.then_inc(turned_copied.sem, 1)
                    kv_done.wait(dve, t, 1)
                    scaled.wait(dve, t, 1)
                    nc.vector.tensor_tensor(kv[:, s, :, :], kv_ps[:, :].rearrange("p (g f) -> p g f", g=G),
                                            rs[:, s, 1, :].unsqueeze(2).to_broadcast([128, G, 128]), ALU.mult) \
                        .then_inc(kv_copied.sem, 1)
                    out_done.wait(dve, t, 1)
                    if not isinstance(t, int) or t >= 2:
                        added.wait_steps(dve, t - s)
                    nc.vector.tensor_tensor(out[:, s, :, :], o_ps[:, :].rearrange("p (g f) -> p g f", g=G),
                                            rs[:, s, 0, :].unsqueeze(2).to_broadcast([128, G, 128]), ALU.mult) \
                        .then_inc(out_scaled.sem, 1)
                pairs(dve, front, back)


def l2_cross_attention(nc, c, T, before):
    H, HD, I = 8, 64, 512
    NK = SC + 1
    with Scope(nc, "l2_xattn") as sc:
        wq = sc.sb("wq", [128, I])
        wkv = sc.sb("wkv", [128, 2 * I])
        wo = sc.sb("wo", [128, 4, 128])
        gains = sc.sb("gains", [128, 4, I])
        null_k = sc.sb("null_k", [1, H, HD])
        cur = sc.sb("tile", [128, 2, 128])
        ctx = sc.sb("context_tile", [128, 2, SC])
        centred = sc.sb("centred", [128, 2, I])
        gained = sc.sb("gained", [128, 2, I])
        shifted = sc.sb("q_shifted", [128, I])
        eq = sc.sb("q_exps", [128, I])
        ek = sc.sb("k_exps", [128, 4, NK])
        v = sc.sb("v", [NK, 2, I])
        qt = sc.sb("q_t", [128, 4, 128])
        kt = sc.sb("k_t", [NK, I])
        kv = sc.sb("kv", [128, 4, 128])
        o = sc.sb("o", [128, I])
        ot = sc.sb("o_t", [128, 4, 128])
        st = sc.sb("stats", [128, 2, 6])
        mv = sc.sb("mean_var", [128, 2, 2])
        ve = sc.sb("var_eps", [128, 2])
        rstd = sc.sb("rstd", [128, 2])
        kmax, ksum, krs = sc.sb("k_neg_max", [128, 4]), sc.sb("k_sums", [128, 2, 4]), sc.sb("k_rsum", [128, 4])
        qmax, qsum, qrs = sc.sb("q_max", [128, H]), sc.sb("q_sums", [128, H]), sc.sb("q_rsum", [128, H])
        items = [(wq[:, :], T["L2_xattn_Wq"]), (wkv[:, :], T["L2_xattn_Wkv"]),
                 (wo[:, :, :], T["L2_xattn_Wout"].rearrange("(m p) d -> p m d", p=128)),
                 (null_k[:, :, :], T["L2_xattn_null_kv"][0:1, :].unsqueeze(1).to_broadcast([1, H, HD]))]
        for s in range(2):
            items.append((v[SC:NK, s, :].rearrange("p (h d) -> p h d", h=H),
                          T["L2_xattn_null_kv"][1:2, :].unsqueeze(1).to_broadcast([1, H, HD])))
        for i, n in enumerate(("ln_q_g", "ln_q_b", "ln_out_g", "ln_out_b")):
            items.append((gains[:, i, :], row(T["L2_xattn_" + n]).to_broadcast([128, I])))
        b = loader(nc, sc, items)
        start_loads(sc, b, before)
        q_ps, k_ps, v_ps, t_ps, kt_ps, kv_ps, o_ps, y_ps = (
            sc.ps(n, [128, 512]) for n in ("q_ps", "k_ps", "v_ps", "t_ps", "kt_ps", "kv_ps", "o_ps", "y_ps"))
        names = ("tile_ready", "projected", "k_maxed", "k_exped", "v_copied", "k_turned", "kt_copied", "kv_done",
                 "k_inverted", "kv_copied", "q_maxed", "q_shifted", "q_exped", "q_turned", "qt_copied", "q_summed",
                 "o_done", "o_scaled", "o_turned", "ot_copied", "y_done", "added")
        (tile_ready, projected, k_maxed, k_exped, v_copied, k_turned, kt_copied, kv_done, k_inverted, kv_copied,
         q_maxed, q_shifted, q_exped, q_turned, qt_copied, q_summed, o_done, o_scaled, o_turned, ot_copied, y_done,
         added) = (sc.counter(n) for n in names)
        q_inverted = sc.counter("q_inverted", 2)
        stats = [sc.counter(n + "_stats", 2) for n in "qo"]
        var_ready, rstd_ready, centre_done, scale_done, gain_done = (
            [sc.counter(f"{n}_{what}") for n in "qo"] for what in ("var", "rstd", "centred", "rescaled", "gained"))
        zeroed = sc.semaphore("zeroed")

        def slots(eng, slot):
            for t in range(3):
                slot(t, t % 2, [0 <= t - k < B for k in range(4)])
            with eng.Fori(0, (B - 4) // 2) as it:
                for u in range(2):
                    slot(it * 2 + 3 + u, (3 + u) % 2, [True] * 4)
            for t in range(B - 1, B + 3):
                slot(t, t % 2, [0 <= t - k < B for k in range(4)])

        def heads(ap):
            return ap.rearrange("p (h d) -> p h d", h=H)

        def bc(ap):
            return ap.unsqueeze(2).to_broadcast([128, H, HD])

        sc.begin()
        with nc.Block() as block:
            @block.gpsimd
            def _(pool):
                nc.gpsimd.memset(kv[:, :, :], 0.0).then_inc(zeroed, 1)
                pool.wait_ge(b["loaded"], 16 * b["loads"])

                def tiles(t, s):
                    projected.wait_steps(pool, t if isinstance(t, int) and t < 2 else t - 1)
                    settle(pool, sc.passed)
                    nc.gpsimd.tensor_copy(cur[:, s, :], c["nT"][:, bass.ds(t * 128, 128)])
                    nc.gpsimd.tensor_copy(ctx[:, s, :], c["cT"][:, bass.ds(t * SC, SC)]).then_inc(tile_ready.sem, 1)

                def power(t, i):
                    var_ready[i].wait(pool, t, 1)
                    settle(pool, sc.passed)
                    nc.gpsimd.tensor_tensor(rstd[:, i:i + 1], ve[:, i:i + 1], c["neg_half"][:, 0:1], ALU.pow) \
                        .then_inc(rstd_ready[i].sem, 1)

                def gain_shift(t, i, used):
                    scale_done[i].wait(pool, t, 1)
                    used.wait_steps(pool, t)
                    settle(pool, sc.passed)
                    nc.gpsimd.tensor_tensor(gained[:, i, :], centred[:, i, :], gains[:, 2 * i + 1, :], ALU.add) \
                        .then_inc(gain_done[i].sem, 1)

                def slot(t, s, on):
                    if on[1]:
                        q_maxed.wait(pool, t - 1, 1)
                        q_exped.wait_steps(pool, t - 1)
                        settle(pool, sc.passed)
                        nc.gpsimd.tensor_tensor(heads(shifted[:, :]), heads(gained[:, 0, :]), bc(qmax[:, :]),
                                                ALU.subtract).then_inc(q_shifted.sem, 1)
                    if on[0]:
                        power(t, 0)
                        gain_shift(t, 0, q_shifted)
                    if on[0] and not (isinstance(t, int) and t == B - 1):
                        tiles(t + 1, 1 - s)
                    if on[2]:
                        power(t - 2, 1)
                        gain_shift(t - 2, 1, o_turned)
                tiles(0, 0)
                slots(pool, slot)

            @block.tensor
            def _(pe):
                pe.wait_ge(zeroed, 1)
                pe.wait_ge(b["loaded"], 16 * b["loads"])
                for m in range(4):
                    nc.tensor.matmul(k_ps[:, m * NK + SC:(m + 1) * NK], null_k[0:1, 2 * m:2 * m + 2, :]
                                     .rearrange("p h d -> p (h d)"), c["ones"][0:1, 0:1], start=True, stop=True)

                def slot(t, s, on):
                    if on[2]:
                        q_exped.wait(pe, t - 2, 1)
                        ot_copied.wait_steps(pe, t - 3 if on[3] else 0)
                        settle(pe, sc.passed)
                        for m in range(4):
                            r = slice(m * 128, (m + 1) * 128)
                            last = nc.tensor.transpose(t_ps[:, r], eq[:, r], c["ident"][:, :])
                        last.then_inc(q_turned.sem, 1)
                    if on[0]:
                        tile_ready.wait(pe, t, 1)
                        centre_done[0].wait_steps(pe, t)
                        k_exped.wait_steps(pe, t)
                        v_copied.wait_steps(pe, t)
                        settle(pe, sc.passed)
                        for m in range(4):
                            nc.tensor.matmul(k_ps[:, m * NK:m * NK + SC], wkv[:, m * 128:(m + 1) * 128], ctx[:, s, :],
                                             start=True, stop=True)
                        nc.tensor.matmul(q_ps[:, :], cur[:, s, :], wq[:, :], start=True, stop=True)
                        nc.tensor.matmul(v_ps[0:SC, :], ctx[:, s, :], wkv[:, I:2 * I], start=True, stop=True) \
                            .then_inc(projected.sem, 1)
                    if on[1]:
                        k_exped.wait(pe, t - 1, 1)
                        kt_copied.wait_steps(pe, t - 1)
                        settle(pe, sc.passed)
                        for m in range(4):
                            last = nc.tensor.transpose(kt_ps[0:NK, m * 128:(m + 1) * 128], ek[:, m, :],
                                                       c["ident"][:, :])
                        last.then_inc(k_turned.sem, 1)
                    if on[2]:
                        qt_copied.wait(pe, t - 2, 1)
                        kv_copied.wait(pe, t - 2, 1)
                        o_scaled.wait_steps(pe, t - 2)
                        settle(pe, sc.passed)
                        for m in range(4):
                            r = slice(m * 128, (m + 1) * 128)
                            last = nc.tensor.matmul(o_ps[:, r], qt[:, m, :], kv[:, m, :], start=True, stop=True)
                        last.then_inc(o_done.sem, 1)
                    if on[3]:
                        gain_done[1].wait(pe, t - 3, 1)
                        settle(pe, sc.passed)
                        for m in range(4):
                            r = slice(m * 128, (m + 1) * 128)
                            last = nc.tensor.transpose(t_ps[:, r], gained[:, 1, r], c["ident"][:, :])
                        last.then_inc(o_turned.sem, 1)
                    if on[1]:
                        kt_copied.wait(pe, t - 1, 1)
                        v_copied.wait(pe, t - 1, 1)
                        kv_copied.wait_steps(pe, t - 1)
                        settle(pe, sc.passed)
                        for m in range(4):
                            r = slice(m * 128, (m + 1) * 128)
                            last = nc.tensor.matmul(kv_ps[:, r], kt[:, r], v[:, 1 - s, r], start=True, stop=True)
                        last.then_inc(kv_done.sem, 1)
                    if on[3]:
                        ot_copied.wait(pe, t - 3, 1)
                        added.wait_steps(pe, t - 3)
                        settle(pe, sc.passed)
                        for m in range(4):
                            last = nc.tensor.matmul(y_ps[:, 0:128], ot[:, m, :], wo[:, m, :], start=(m == 0),
                                                    stop=(m == 3))
                        last.then_inc(y_done.sem, 1)
                slots(pe, slot)

            @block.scalar
            def _(act):
                def scale(t, i):
                    centre_done[i].wait(act, t, 1)
                    rstd_ready[i].wait(act, t, 1)
                    settle(act, sc.passed)
                    nc.scalar.activation(centred[:, i, :], centred[:, i, :], ACT.Copy, scale=rstd[:, i:i + 1]) \
                        .then_inc(scale_done[i].sem, 1)

                def slot(t, s, on):
                    if on[2]:
                        q_turned.wait(act, t - 2, 1)
                        o_done.wait_steps(act, t - 2)
                        settle(act, sc.passed)
                        nc.scalar.activation(qt[:, :, :], t_ps[:, :], ACT.Copy).then_inc(qt_copied.sem, 1)
                    if on[0]:
                        k_maxed.wait(act, t, 1)
                        k_turned.wait_steps(act, t)
                        k_inverted.wait_steps(act, t - 1 if on[1] else 0)
                        settle(act, sc.passed)
                        for m in range(4):
                            last = nc.scalar.activation(ek[:, m, :], k_ps[:, m * NK:(m + 1) * NK], ACT.Exp,
                                                        bias=kmax[:, m:m + 1], accum_out=ksum[:, s, m:m + 1])
                        last.then_inc(k_exped.sem, 1)
                        kv_done.wait_steps(act, t - 1 if on[1] else 0)
                        settle(act, sc.passed)
                        nc.scalar.activation(v[0:SC, s, :], v_ps[0:SC, :], ACT.Copy).then_inc(v_copied.sem, 1)
                    if on[1]:
                        k_turned.wait(act, t - 1, 1)
                        kv_done.wait_steps(act, t - 1)
                        settle(act, sc.passed)
                        nc.scalar.activation(kt[:, :], kt_ps[0:NK, :], ACT.Copy).then_inc(kt_copied.sem, 1)
                    if on[3]:
                        o_turned.wait(act, t - 3, 1)
                        y_done.wait_steps(act, t - 3)
                        settle(act, sc.passed)
                        nc.scalar.activation(ot[:, :, :], t_ps[:, :], ACT.Copy).then_inc(ot_copied.sem, 1)
                    if on[1]:
                        q_shifted.wait(act, t - 1, 1)
                        q_summed.wait_steps(act, t - 1)
                        q_turned.wait_steps(act, t - 1)
                        settle(act, sc.passed)
                        nc.scalar.activation(eq[:, :], shifted[:, :], ACT.Exp).then_inc(q_exped.sem, 1)
                    if on[0]:
                        scale(t, 0)
                    if on[2]:
                        scale(t - 2, 1)
                slots(act, slot)

            @block.vector
            def _(dve):
                def centre(t, i, src):
                    nc.vector.bn_stats(st[:, i, :], src).then_inc(stats[i].sem, 1)
                    stats[i].wait(dve, t, 1)
                    settle(dve, sc.passed)
                    nc.vector.bn_aggr(mv[:, i, :], st[:, i, :]).then_inc(stats[i].sem, 1)
                    stats[i].wait(dve, t, 2)
                    rstd_ready[i].wait_steps(dve, t)
                    settle(dve, sc.passed)
                    nc.vector.tensor_scalar(ve[:, i:i + 1], mv[:, i, 1:2], LN_EPS, None, ALU.add) \
                        .then_inc(var_ready[i].sem, 1)
                    gain_done[i].wait_steps(dve, t)
                    settle(dve, sc.passed)
                    nc.vector.scalar_tensor_tensor(out=centred[:, i, :], in0=src, scalar=mv[:, i, 0:1],
                                                   in1=gains[:, 2 * i, :], op0=ALU.subtract, op1=ALU.mult) \
                        .then_inc(centre_done[i].sem, 1)

                def slot(t, s, on):
                    if on[1]:
                        gain_done[0].wait(dve, t - 1, 1)
                        q_shifted.wait_steps(dve, t - 1)
                        settle(dve, sc.passed)
                        nc.vector.tensor_reduce(qmax[:, :], heads(gained[:, 0, :]), AX.X, ALU.max) \
                            .then_inc(q_maxed.sem, 1)
                    if on[0]:
                        projected.wait(dve, t, 1)
                        k_exped.wait_steps(dve, t)
                        settle(dve, sc.passed)
                        nc.vector.tensor_reduce(kmax[:, :], k_ps[:, 0:4 * NK].rearrange("p (m k) -> p m k", m=4), AX.X,
                                                ALU.max, negate=True).then_inc(k_maxed.sem, 1)
                        centre(t, 0, q_ps[:, :])
                    if on[2]:
                        q_exped.wait(dve, t - 2, 1)
                        nc.vector.tensor_reduce(qsum[:, :], heads(eq[:, :]), AX.X, ALU.add).then_inc(q_summed.sem, 1)
                        q_summed.wait(dve, t - 2, 1)
                        nc.vector.reciprocal(qrs[:, :], qsum[:, :]).then_inc(q_inverted.sem, 1)
                        q_inverted.wait(dve, t - 2, 1)
                        nc.vector.tensor_scalar(qrs[:, :], qrs[:, :], 8.0, None, ALU.mult).then_inc(q_inverted.sem, 1)
                        q_inverted.wait(dve, t - 2, 2)
                        o_done.wait(dve, t - 2, 1)
                        nc.vector.tensor_tensor(heads(o[:, :]), heads(o_ps[:, :]), bc(qrs[:, :]), ALU.mult) \
                            .then_inc(o_scaled.sem, 1)
                        o_scaled.wait(dve, t - 2, 1)
                        centre(t - 2, 1, o[:, :])
                    if on[1]:
                        k_exped.wait(dve, t - 1, 1)
                        nc.vector.reciprocal(krs[:, :], ksum[:, 1 - s, :]).then_inc(k_inverted.sem, 1)
                        k_inverted.wait(dve, t - 1, 1)
                        kv_done.wait(dve, t - 1, 1)
                        o_done.wait_steps(dve, t - 1)
                        settle(dve, sc.passed)
                        for h in range(2):
                            r = slice(64 * h, 64 * h + 64)
                            last = nc.vector.tensor_tensor(
                                kv[r, :, r], kv_ps[r, :].rearrange("p (m e) -> p m e", m=4)[:, :, r],
                                krs[r, :].unsqueeze(2).to_broadcast([64, 4, 64]), ALU.mult)
                        last.then_inc(kv_copied.sem, 1)
                    if on[3]:
                        y_done.wait(dve, t - 3, 1)
                        settle(dve, sc.passed)
                        xs = c["x"][:, t - 3, :]
                        nc.vector.tensor_tensor(xs, y_ps[:, 0:128], xs, ALU.add).then_inc(added.sem, 1)
                slots(dve, slot)


def l0_ffn(nc, c, T, before):
    QMAX, MAGIC = 127.0, 12582912.0
    I = 352
    CH = [(0, 128), (128, 128), (256, 96)]
    G, N = 4, B // 4
    with Scope(nc, "l0_ffn") as sc:
        wn = sc.sb("w_natural", [128, 9, 128])
        wi = sc.sb("w_whole", [128, 9, 128])
        w_t = sc.sb("w_t", [128, 9, 128], BF16)
        sw = sc.sb("w_scale", [128, 7])
        isw = sc.sb("w_scale_inv", [128, 7])
        diag = sc.sb("diagonal", [128, 128])
        down_scale = sc.sb("down_scale", [128, 128])
        clip = sc.sb("clip", [128, 2])
        mx = sc.sb("abs_max", [128, 4])
        amax = sc.sb("abs_max_all", [128, 2])
        act_scale = sc.sb("act_scale", [128, 2])
        inv_scale = sc.sb("act_scale_inv", [128, 2])
        both = sc.sb("both_scales", [128, 6])
        hid = sc.sb("hidden", [128, 3, B * 128])
        items = [(clip[:, 0:1], row(T["L0_ffn_clip_x"]).to_broadcast([128, 1])),
                 (clip[:, 1:2], row(T["L0_ffn_clip_down"]).to_broadcast([128, 1]))]
        for k, n in enumerate(("gate", "up")):
            for i, (r0, rn) in enumerate(CH):
                items.append((wn[0:rn, 3 * k + i, :], T["L0_ffn_w_" + n][r0:r0 + rn, :]))
        items.append((wn[:, 6:8, :], T["L0_ffn_w_down"][:, 0:256].rearrange("h (a i) -> h a i", a=2)))
        items.append((wn[:, 8, 0:96], T["L0_ffn_w_down"][:, 256:352]))
        b = loader(nc, sc, items)
        zeroed, turned, diag_made, clipped, all_max, prep, scaled = (
            sc.semaphore(n) for n in ("zeroed", "turned", "diag_made", "clip_ready", "all_max", "prepared", "scaled"))

        def fill(pool):
            nc.gpsimd.memset(mx[:, :], 0.0)
            nc.gpsimd.memset(wn[:, :, :], 0.0).then_inc(zeroed, 1)

        def dma(sp):
            sp.wait_ge(zeroed, 1)
            b["dma"](sp)
        start_loads(sc, dict(prepare_pool=fill, dma=dma), before)

        w_ps = [sc.ps(f"w_t{i}", [128, 512]) for i in range(3)]
        with nc.Block() as block:
            @block.gpsimd
            def _(pool):
                pool.wait_ge(scaled, 1)
                nc.gpsimd.partition_all_reduce(amax[:, 0:1], mx[:, 0:1], 128, REDUCE_MAX) \
                    .then_inc(all_max, 1)

            @block.scalar
            def _(act):
                act.wait_ge(b["loaded"], 16 * b["loads"])
                nc.scalar.activation(clip[:, :], clip[:, :], ACT.Sigmoid).then_inc(clipped, 1)

            @block.tensor
            def _(pe):
                pe.wait_ge(prep, 5)
                for m in range(9):
                    last = nc.tensor.transpose(w_ps[m // 4][:, (m % 4) * 128:(m % 4) * 128 + 128], wi[:, m, :],
                                               c["ident"][:, :])
                last.then_inc(turned, 1)
                pe.wait_ge(diag_made, 1)
                nc.tensor.matmul(w_ps[2][:, 256:384], c["ones"][:, :], diag[:, :], start=True, stop=True) \
                    .then_inc(turned, 1)

            @block.vector
            def _(dve):
                dve.wait_ge(zeroed, 1)
                nc.vector.tensor_reduce(mx[:, 0:1], c["nT"][:, :], AX.X, ALU.max, apply_absolute_value=True) \
                    .then_inc(scaled, 1)
                dve.wait_ge(b["loaded"], 16 * b["loads"])
                count = [0]

                def then(ins):
                    count[0] += 1
                    ins.then_inc(prep, 1)
                    dve.wait_ge(prep, count[0])
                nc.vector.tensor_reduce(sw[:, 0:6], wn[:, 0:6, :], AX.X, ALU.max, apply_absolute_value=True)
                then(nc.vector.tensor_reduce(sw[:, 6:7], wn[:, 6:9, :], AX.XY, ALU.max, apply_absolute_value=True))
                then(nc.vector.tensor_scalar(sw[:, :], sw[:, :], 1.0 / QMAX, 1e-37, ALU.mult, ALU.max))
                then(nc.vector.reciprocal(isw[:, :], sw[:, :]))
                for m in range(9):
                    last = nc.vector.tensor_scalar(wi[:, m, :], wn[:, m, :], isw[:, min(m, 6):min(m, 6) + 1], MAGIC,
                                                   ALU.mult, ALU.add)
                then(last)
                then(nc.vector.tensor_scalar(wi[:, :, :], wi[:, :, :], MAGIC, None, ALU.subtract))
                nc.vector.tensor_scalar(diag[:, :], c["ident"][:, :], sw[:, 6:7], None, ALU.mult).then_inc(diag_made, 1)
                dve.wait_ge(turned, 2)
                for m in range(3):
                    n = (4, 4, 1)[m]
                    last = nc.vector.tensor_copy(w_t[:, 4 * m:4 * m + n, :], w_ps[m][:, 0:n * 128]
                                                 .rearrange("p (n f) -> p n f", f=128))
                nc.vector.tensor_copy(down_scale[:, :], w_ps[2][:, 256:384])
                dve.wait_ge(clipped, 1)
                dve.wait_ge(all_max, 1)
                then(nc.vector.tensor_tensor(act_scale[:, 0:1], clip[:, 0:1], amax[:, 0:1], ALU.mult))
                then(nc.vector.tensor_scalar(act_scale[:, 0:1], act_scale[:, 0:1], 1.0 / QMAX, None, ALU.mult))
                then(nc.vector.reciprocal(inv_scale[:, 0:1], act_scale[:, 0:1]))
                then(nc.vector.tensor_scalar(both[:, :], sw[:, 0:6], act_scale[:, 0:1], None, ALU.mult))

        with Scope(nc, "l0_up") as up:
            qa = up.sb("rounded", [128, 2, 512])
            xq = up.sb("x_whole", [128, 2, 512], BF16)
            sg = up.sb("silu", [128, 2, 512])
            gu = [[up.ps(f"{n}{i}", [128, 512]) for n in ("gate", "up")] for i in range(2)]
            rounded, clipped_, whole = (up.counter(n) for n in ("rounded", "clipped", "whole"))
            filled, silu_done, h_done = (up.counter(n, 3) for n in ("filled", "silu_done", "h_done"))

            def pairs(eng, body):
                with eng.Fori(0, N // 2) as it:
                    for s in range(2):
                        body(it * 2 + s, s)
            up.begin()
            with nc.Block() as block:
                @block.tensor
                def _(pe):
                    def body(t, s):
                        whole.wait(pe, t, 1)
                        for i in range(3):
                            if i == 2:
                                h_done.wait(pe, t, 1)
                            else:
                                h_done.wait_steps(pe, t)
                            settle(pe, up.passed)
                            for k in range(2):
                                last = nc.tensor.matmul(gu[i % 2][k][:, :], w_t[:, 3 * k + i, :], xq[:, s, :],
                                                        start=True, stop=True)
                            last.then_inc(filled.sem, 1)
                    pairs(pe, body)

                @block.scalar
                def _(act):
                    def body(t, s):
                        for i in range(3):
                            filled.wait(act, t, i + 1)
                            if i == 2:
                                h_done.wait(act, t, 1)
                            else:
                                h_done.wait_steps(act, t)
                            settle(act, up.passed)
                            nc.scalar.activation(sg[:, i % 2, :], gu[i % 2][0][:, :], ACT.Silu, scale=both[:, i:i + 1]) \
                                .then_inc(silu_done.sem, 1)
                    pairs(act, body)

                @block.vector
                def _(dve):
                    def quantize(t, s):
                        filled.wait_steps(dve, t if isinstance(t, int) and t < 1 else t - 1)
                        settle(dve, up.passed)
                        nc.vector.tensor_scalar(qa[:, s, :], c["nT"][:, bass.ds(t * 512, 512)], inv_scale[:, 0:1], QMAX,
                                                ALU.mult, ALU.min).then_inc(rounded.sem, 1)
                        rounded.wait(dve, t, 1)
                        settle(dve, up.passed)
                        nc.vector.tensor_scalar(qa[:, s, :], qa[:, s, :], -QMAX - 1, MAGIC, ALU.max, ALU.add) \
                            .then_inc(clipped_.sem, 1)
                        clipped_.wait(dve, t, 1)
                        settle(dve, up.passed)
                        nc.vector.tensor_scalar(xq[:, s, :], qa[:, s, :], MAGIC, None, ALU.subtract) \
                            .then_inc(whole.sem, 1)

                    def body(t, s):
                        for i in range(3):
                            silu_done.wait(dve, t, i + 1)
                            settle(dve, up.passed)
                            nc.vector.scalar_tensor_tensor(out=hid[:, i, bass.ds(t * 512, 512)], in0=gu[i % 2][1][:, :],
                                                           scalar=both[:, 3 + i:4 + i], in1=sg[:, i % 2, :],
                                                           op0=ALU.mult, op1=ALU.mult).then_inc(h_done.sem, 1)
                    quantize(0, 0)
                    with dve.Fori(0, N // 2 - 1) as it:
                        for s in range(2):
                            quantize(it * 2 + 1 + s, 1 - s)
                            body(it * 2 + s, s)
                    quantize(N - 1, 1)
                    body(N - 2, 0)
                    body(N - 1, 1)

        with nc.Block() as block:
            @block.gpsimd
            def _(pool):
                pool.wait_ge(scaled, 3)
                nc.gpsimd.partition_all_reduce(amax[:, 1:2], mx[:, 0:1], 128, REDUCE_MAX) \
                    .then_inc(all_max, 1)

            @block.vector
            def _(dve):
                nc.vector.tensor_reduce(mx[:, 1:4], hid[:, :, :], AX.X, ALU.max, apply_absolute_value=True) \
                    .then_inc(scaled, 1)
                dve.wait_ge(scaled, 2)
                nc.vector.tensor_reduce(mx[:, 0:1], mx[:, 1:4], AX.X, ALU.max).then_inc(scaled, 1)
                dve.wait_ge(all_max, 2)
                count = [9]

                def then(ins):
                    count[0] += 1
                    ins.then_inc(prep, 1)
                    dve.wait_ge(prep, count[0])
                then(nc.vector.tensor_tensor(act_scale[:, 1:2], clip[:, 1:2], amax[:, 1:2], ALU.mult))
                then(nc.vector.tensor_scalar(act_scale[:, 1:2], act_scale[:, 1:2], 1.0 / QMAX, None, ALU.mult))
                then(nc.vector.reciprocal(inv_scale[:, 1:2], act_scale[:, 1:2]))

        with Scope(nc, "l0_down") as dn:
            qa = dn.sb("rounded", [128, 2, 3, 512])
            hq = dn.sb("h_whole", [128, 2, 3, 512], BF16)
            out = dn.sb("out", [128, 2, G, 128])
            o_ps = [dn.ps(f"out{i}", [128, 512]) for i in range(2)]
            rounded, clipped_, whole, filled, out_scaled, added = (
                dn.counter(n) for n in ("rounded", "clipped", "whole", "filled", "out_scaled", "added"))
            dn.begin()
            with nc.Block() as block:
                @block.gpsimd
                def _(pool):
                    def body(t, s):
                        out_scaled.wait(pool, t, 1)
                        settle(pool, dn.passed)
                        xs = c["x"][:, bass.ds(t * G, G), :]
                        nc.gpsimd.tensor_tensor(xs, xs, out[:, s, :, :], ALU.add).then_inc(added.sem, 1)
                    pairs(pool, body)

                @block.scalar
                def _(act):
                    def body(t, s):
                        clipped_.wait(act, t, 1)
                        filled.wait_steps(act, t - s)
                        settle(act, dn.passed)
                        nc.scalar.activation(hq[:, s, :, :], qa[:, s, :, :], ACT.Copy, bias=-MAGIC).then_inc(whole.sem, 1)
                    pairs(act, body)

                @block.tensor
                def _(pe):
                    def body(t, s):
                        whole.wait(pe, t, 1)
                        out_scaled.wait_steps(pe, t - s)
                        settle(pe, dn.passed)
                        for j in range(G):
                            for i, (r0, rn) in enumerate(CH):
                                last = nc.tensor.matmul(o_ps[s][:, j * 128:(j + 1) * 128],
                                                        hq[0:rn, s, i, j * 128:(j + 1) * 128], w_t[0:rn, 6 + i, :],
                                                        start=(i == 0), stop=(i == 2))
                        last.then_inc(filled.sem, 1)
                    pairs(pe, body)

                @block.vector
                def _(dve):
                    def quantize(t, s):
                        whole.wait_steps(dve, t if isinstance(t, int) else t - 1)
                        settle(dve, dn.passed)
                        nc.vector.tensor_scalar(qa[:, s, :, :], hid[:, :, bass.ds(t * 512, 512)], inv_scale[:, 1:2],
                                                QMAX, ALU.mult, ALU.min).then_inc(rounded.sem, 1)
                        rounded.wait(dve, t, 1)
                        settle(dve, dn.passed)
                        nc.vector.tensor_scalar(qa[:, s, :, :], qa[:, s, :, :], -QMAX - 1, MAGIC, ALU.max, ALU.add) \
                            .then_inc(clipped_.sem, 1)

                    def body(t, s):
                        filled.wait(dve, t, 1)
                        added.wait_steps(dve, t - s)
                        settle(dve, dn.passed)
                        nc.vector.scalar_tensor_tensor(out=out[:, s, :, :],
                                                       in0=o_ps[s][:, :].rearrange("p (g f) -> p g f", g=G),
                                                       scalar=act_scale[:, 1:2],
                                                       in1=down_scale[:, :].unsqueeze(1).to_broadcast([128, G, 128]),
                                                       op0=ALU.mult, op1=ALU.mult).then_inc(out_scaled.sem, 1)
                    quantize(0, 0)
                    with dve.Fori(0, N // 2 - 1) as it:
                        for s in range(2):
                            quantize(it * 2 + 1 + s, 1 - s)
                            body(it * 2 + s, s)
                    quantize(N - 1, 1)
                    body(N - 2, 0)
                    body(N - 1, 1)


def l1_ffn(nc, c, T):
    E, CAP, HD = 16, 2, 64
    W3 = 3 * HD
    G, N = 4, B // 4
    scale = float(HD) ** -0.5
    rows = nc.dram_tensor("token_rows", (S * B, D), F32, kind="Internal").ap()
    with Scope(nc, "l1_ffn") as sc:
        tok = sc.sb("tokens", [128, B, 128])
        idx = sc.sb("row_index", [128, E, CAP], U32)
        hg = sc.sb("gathered", [128, E, CAP, 128])
        w3 = sc.sb("w_qkv", [128, E, W3])
        b3 = sc.sb("b_qkv", [128, E, W3])
        wo = sc.sb("wo", [HD, E, 128])
        bo = sc.sb("bo", [128, 128])
        gb = sc.sb("gain", [128, 2, 128])
        qkv = sc.sb("qkv", [128, E, CAP, W3])
        tile = sc.sb("expert_tile", [128, 2, CAP, 128])
        hT = sc.sb("expert_tile_t", [128, 2, CAP, 128])
        av = sc.sb("attended", [128, E, CAP, HD])
        wg = sc.sb("router", [128, E])
        items = [(wg[:, :], T["L1_ffn_Wg"]), (w3[:, :, 0:HD], T["L1_ffn_Wq"].rearrange("e d f -> d e f")),
                 (w3[:, :, HD:W3], T["L1_ffn_Wkv"].rearrange("e d f -> d e f")),
                 (b3[:, :, 0:HD], T["L1_ffn_bq"].unsqueeze(0).to_broadcast([128, E, HD])),
                 (b3[:, :, HD:W3], T["L1_ffn_bkv"].unsqueeze(0).to_broadcast([128, E, 2 * HD])),
                 (wo[:, :, :], T["L1_ffn_Wo"].rearrange("e f d -> f e d")),
                 (bo[:, :], row(T["L1_ffn_bo"]).to_broadcast([128, 128])),
                 (gb[:, 0, :], row(T["L1_ffn_ln_g"]).to_broadcast([128, 128])),
                 (gb[:, 1, :], row(T["L1_ffn_ln_b"]).to_broadcast([128, 128]))]
        b = loader(nc, sc, items)
        GE = 4
        gathered = [sc.semaphore(f"gathered{i}") for i in range(E // GE)]

        start_loads(sc, b, lambda b: normalize(nc, c, "n1f", c["x"], 128, c["nT"], ["ln"], token_out=tok, loads=b))

        with Scope(nc, "l1_route") as rt:
            cur = rt.sb("tiles", [128, 2, 512])
            val = rt.sb("probs", [128, B, E])
            rmax, rsum = rt.sb("row_max", [128, B]), rt.sb("row_sum", [128, B])
            iota_i, iota = rt.sb("index_int", [128, E, B], I32), rt.sb("index", [128, E, B])
            base_i, base = rt.sb("base_int", [128, 1], I32), rt.sb("base", [128, 1])
            w = dict(top=rt.sb("top", [128, 2, E]), index=rt.sb("top_index", [128, 2, E]),
                     eq=rt.sb("eq", [128, E, B])[:, :, :], rest=rt.sb("rest", [128, E, B])[:, :, :],
                     hot=[rt.sb(f"hot{i}", [128, E, B])[:, :, :] for i in range(2)])
            picked = rt.sb("picked", [128, E, CAP])
            R_ps = rt.ps("logits", [128, B * E])
            tile_ready = [rt.counter(f"tile_ready{s}") for s in range(2)]
            routed = [rt.counter(f"routed{s}") for s in range(2)]
            index_made, soft, shifted, exped, part, stored = (
                rt.semaphore(n) for n in ("index_made", "softmax_part", "shifted", "exped", "top_part", "rows_stored"))
            rt.begin()
            with nc.Block() as block:
                @block.sync
                def _(sp):
                    sp.dma_start(rows.rearrange("(p s) d -> p s d", s=B), tok[:, :, :]).then_inc(stored, 16)
                    sp.wait_ge(stored, 16)

                @block.gpsimd
                def _(pool):
                    nc.gpsimd.iota(iota_i[:, :, :], pattern=[[0, E], [1, B]], base=0, channel_multiplier=0)
                    nc.gpsimd.iota(base_i[:, :], pattern=[[0, 1]], base=0, channel_multiplier=B).then_inc(index_made, 1)

                @block.tensor
                def _(pe):
                    pe.wait_ge(b["loaded"], 16 * b["loads"])
                    with pe.Fori(0, N // 2) as it:
                        for s in range(2):
                            t = it * 2 + s
                            tile_ready[s].wait(pe, it, 1)
                            settle(pe, rt.passed)
                            for j in range(G):
                                last = nc.tensor.matmul(R_ps[:, bass.ds(t * (G * E) + j * E, E)],
                                                        cur[:, s, j * 128:(j + 1) * 128], wg[:, :], start=True, stop=True)
                            last.then_inc(routed[s].sem, 1)

                @block.scalar
                def _(act):
                    with act.Fori(0, N // 2) as it:
                        routed[1].wait_steps(act, it)
                        settle(act, rt.passed)
                        nc.scalar.activation(cur[:, 1, :], c["nT"][:, bass.ds((it * 2 + 1) * 512, 512)],
                                             ACT.Copy).then_inc(tile_ready[1].sem, 1)
                    act.wait_ge(shifted, 1)
                    nc.scalar.activation(val[:, :, :], val[:, :, :], ACT.Exp).then_inc(exped, 1)

                @block.vector
                def _(dve):
                    dve.wait_ge(index_made, 1)
                    nc.vector.tensor_copy(iota[:, :, :], iota_i[:, :, :])
                    nc.vector.tensor_copy(base[:, :], base_i[:, :]).then_inc(index_made, 1)
                    dve.wait_ge(index_made, 2)
                    with dve.Fori(0, N // 2) as it:
                        routed[0].wait_steps(dve, it)
                        settle(dve, rt.passed)
                        nc.vector.tensor_copy(cur[:, 0, :], c["nT"][:, bass.ds(it * 1024, 512)]) \
                            .then_inc(tile_ready[0].sem, 1)
                    for sig in routed:
                        dve.wait_ge(sig.sem, N // 2 + 1)
                    logits = R_ps[:, :].rearrange("p (s e) -> p s e", e=E)

                    def bc(ap):
                        return ap.unsqueeze(2).to_broadcast([128, B, E])
                    nc.vector.tensor_reduce(rmax[:, :], logits, AX.X, ALU.max).then_inc(soft, 1)
                    dve.wait_ge(soft, 1)
                    nc.vector.tensor_tensor(val[:, :, :], logits, bc(rmax[:, :]), ALU.subtract).then_inc(shifted, 1)
                    dve.wait_ge(exped, 1)
                    nc.vector.reduce_sum(rsum[:, :], val[:, :, :], axis=AX.X).then_inc(soft, 1)
                    dve.wait_ge(soft, 2)
                    nc.vector.reciprocal(rsum[:, :], rsum[:, :]).then_inc(soft, 1)
                    dve.wait_ge(soft, 3)
                    nc.vector.tensor_tensor(val[:, :, :], val[:, :, :], bc(rsum[:, :]), ALU.mult).then_inc(soft, 1)
                    dve.wait_ge(soft, 4)
                    then = top_two(nc, dve, rt, w, val[:, :, :].rearrange("p s e -> p e s"), E, B, iota[:, :, :], part)
                    for k, op in enumerate((ALU.min, ALU.max)):
                        then(nc.vector.tensor_tensor(picked[:, :, k], w["index"][:, 0, :], w["index"][:, 1, :], op))
                    then(nc.vector.tensor_scalar(picked[:, :, :], picked[:, :, :], base[:, 0:1], None, ALU.add))
                    then(nc.vector.tensor_copy(idx[:, :, :], picked[:, :, :]))

        def pairs(eng, body, n=E):
            with eng.Fori(0, n // 2) as it:
                for s in range(2):
                    body(it * 2 + s, s)

        with Scope(nc, "l1_qkv") as g_:
            t_ps = [g_.ps(f"turned{i}", [128, 512]) for i in range(2)]
            q_ps = [g_.ps(f"qkv{i}", [128, 512]) for i in range(2)]
            tile_ready, turned, turned_copied, projected, copied = (
                g_.counter(n) for n in ("tile_ready", "turned", "turned_copied", "projected", "copied"))
            g_.begin()
            with nc.Block() as block:
                @block.gpsimd
                def _(pool):
                    for e in range(E):
                        for k in range(CAP):
                            nc.gpsimd.indirect_dma_start(
                                out=hg[:, e, k, :], out_offset=None, in_=rows,
                                in_offset=bass.IndirectOffsetOnAxis(ap=idx[:, e, k:k + 1], axis=0)).then_inc(gathered[e // GE], 16)

                @block.tensor
                def _(pe):
                    pe.wait_ge(b["loaded"], 16 * b["loads"])

                    def body(t, s):
                        tile_ready.wait(pe, t, 1)
                        turned_copied.wait_steps(pe, t - s)
                        settle(pe, g_.passed)
                        for k in range(CAP):
                            last = nc.tensor.transpose(t_ps[s][:, k * 128:(k + 1) * 128], tile[:, s, k, :], c["ident"][:, :])
                        last.then_inc(turned.sem, 1)
                        turned_copied.wait(pe, t, 1)
                        copied.wait_steps(pe, t - s)
                        settle(pe, g_.passed)
                        for k in range(CAP):
                            last = nc.tensor.matmul(q_ps[s][:, k * W3:(k + 1) * W3], hT[:, s, k, :], w3[:, t, :],
                                                    start=True, stop=True)
                        last.then_inc(projected.sem, 1)
                    pairs(pe, body)

                @block.scalar
                def _(act):
                    def body(t, s):
                        turned.wait(act, t, 1)
                        projected.wait_steps(act, t - s)
                        settle(act, g_.passed)
                        nc.scalar.activation(hT[:, s, :, :], t_ps[s][:, 0:CAP * 128], ACT.Copy) \
                            .then_inc(turned_copied.sem, 1)
                    pairs(act, body)

                @block.vector
                def _(dve):
                    def tiles(t, s):
                        turned.wait_steps(dve, t - 1 if not isinstance(t, int) else max(t - 1, 0))
                        settle(dve, g_.passed)
                        nc.vector.tensor_copy(tile[:, s, :, :], hg[:, t, :, :]).then_inc(tile_ready.sem, 1)

                    def keep(t, s):
                        projected.wait(dve, t, 1)
                        settle(dve, g_.passed)
                        nc.vector.tensor_tensor(qkv[:, t, :, :], q_ps[s][:, 0:CAP * W3].rearrange("p (k f) -> p k f", k=CAP),
                                                b3[:, t, :].unsqueeze(1).to_broadcast([128, CAP, W3]), ALU.add) \
                            .then_inc(copied.sem, 1)
                    for i in range(E // GE):
                        dve.wait_ge(gathered[i], 16 * GE * CAP)
                        if i == 0:
                            for t in range(GE):
                                tiles(t, t % 2)
                                if t:
                                    keep(t - 1, 1 - t % 2)
                            continue
                        with dve.Fori(0, GE // 2) as it:
                            for s in range(2):
                                t = it * 2 + i * GE + s
                                tiles(t, s)
                                keep(t - 1, 1 - s)
                    keep(E - 1, (E - 1) % 2)

        with Scope(nc, "l1_pair") as a_:
            prod = a_.sb("products", [128, 2, E, HD])
            att = a_.sb("scores", [128, 4, E])
            pt = a_.sb("probs_t", [64, 128])
            pr = a_.sb("probs", [128, 4, E])
            nm, ssum, srs = a_.sb("neg_max", [64, 1]), a_.sb("sum", [64, 1]), a_.sb("rsum", [64, 1])
            s_ps, p_ps = a_.ps("scores_t", [64, 128]), a_.ps("probs_back", [128, 64])
            mult, summed, turned, exped, part, back, combined = (
                a_.semaphore(n) for n in ("multiplied", "summed", "turned", "exped", "soft_part", "turned_back", "combined"))
            a_.begin()
            with nc.Block() as block:
                @block.gpsimd
                def _(pool):
                    for n in range(4):
                        i, j = n // 2, n % 2
                        if n >= 2:
                            pool.wait_ge(summed, n - 1)
                        nc.gpsimd.tensor_tensor(prod[:, n % 2, :, :], qkv[:, :, i, 0:HD], qkv[:, :, j, HD:2 * HD],
                                                ALU.mult).then_inc(mult, 1)

                @block.tensor
                def _(pe):
                    pe.wait_ge(summed, 4)
                    nc.tensor.transpose(s_ps[:, :], att[:, :, :].rearrange("p n e -> p (n e)"), c["ident"][:, :]) \
                        .then_inc(turned, 1)
                    pe.wait_ge(part, 4)
                    nc.tensor.transpose(p_ps[:, :], pt[:, :], c["ident"][0:64, 0:64]).then_inc(back, 1)

                @block.scalar
                def _(act):
                    act.wait_ge(part, 2)
                    nc.scalar.activation(pt[:, :], s_ps[:, :], ACT.Exp, bias=nm[:, 0:1], scale=scale,
                                         accum_out=ssum[:, 0:1]).then_inc(exped, 1)

                @block.vector
                def _(dve):
                    for n in range(4):
                        dve.wait_ge(mult, n + 1)
                        nc.vector.reduce_sum(att[:, n, :], prod[:, n % 2, :, :], axis=AX.X).then_inc(summed, 1)
                    dve.wait_ge(turned, 1)
                    nc.vector.tensor_reduce(nm[:, :], s_ps[:, :], AX.X, ALU.max, negate=True).then_inc(part, 1)
                    dve.wait_ge(part, 1)
                    nc.vector.tensor_scalar(nm[:, :], nm[:, :], scale, None, ALU.mult).then_inc(part, 1)
                    dve.wait_ge(exped, 1)
                    nc.vector.reciprocal(srs[:, :], ssum[:, :]).then_inc(part, 1)
                    dve.wait_ge(part, 3)
                    nc.vector.tensor_scalar(pt[:, :], pt[:, :], srs[:, 0:1], None, ALU.mult).then_inc(part, 1)
                    dve.wait_ge(back, 1)
                    nc.vector.tensor_copy(pr[:, :, :], p_ps[:, :].rearrange("p (n e) -> p n e", e=E)).then_inc(part, 1)
                    dve.wait_ge(part, 5)
                    n = 0
                    for i in range(CAP):
                        for j in range(CAP):
                            if n:
                                dve.wait_ge(combined, n)
                            last = nc.vector.tensor_tensor(
                                prod[:, j, :, :], qkv[:, :, j, 2 * HD:W3],
                                pr[:, 2 * i + j, :].unsqueeze(2).to_broadcast([128, E, HD]), ALU.mult)
                        last.then_inc(combined, 1)
                        n += 1
                        dve.wait_ge(combined, n)
                        nc.vector.tensor_tensor(av[:, :, i, :], prod[:, 0, :, :], prod[:, 1, :, :], ALU.add) \
                            .then_inc(combined, 1)
                        n += 1
                    dve.wait_ge(combined, n)

        ao = hg
        with Scope(nc, "l1_out") as o_:
            t_ps = [o_.ps(f"turned{i}", [128, 512]) for i in range(2)]
            y_ps = [o_.ps(f"out{i}", [128, 512]) for i in range(2)]
            tile_ready, turned, turned_copied, projected, copied = (
                o_.counter(n) for n in ("tile_ready", "turned", "turned_copied", "projected", "copied"))
            scattered, fetched = o_.semaphore("scattered"), o_.semaphore("fetched")
            o_.begin()
            with nc.Block() as block:
                @block.sync
                def _(sp):
                    sp.wait_ge(scattered, 16 * E * CAP)
                    sp.dma_start(tok[:, :, :], rows.rearrange("(p s) d -> p s d", s=B)).then_inc(fetched, 16)
                    sp.wait_ge(fetched, 16)

                @block.gpsimd
                def _(pool):
                    for e in range(E):
                        pool.wait_ge(copied.sem, e + 2)
                        if e:
                            pool.wait_ge(scattered, 16 * e * CAP)
                        for k in range(CAP):
                            nc.gpsimd.indirect_dma_start(
                                out=rows, out_offset=bass.IndirectOffsetOnAxis(ap=idx[:, e, k:k + 1], axis=0),
                                in_=ao[:, e, k, :], in_offset=None, compute_op=ALU.add).then_inc(scattered, 16)
                    pool.wait_ge(scattered, 16 * E * CAP)

                @block.tensor
                def _(pe):
                    def body(t, s):
                        tile_ready.wait(pe, t, 1)
                        turned_copied.wait_steps(pe, t - s)
                        settle(pe, o_.passed)
                        for k in range(CAP):
                            last = nc.tensor.transpose(t_ps[s][0:HD, k * 128:(k + 1) * 128], tile[:, s, k, 0:HD],
                                                       c["ident"][:, :])
                        last.then_inc(turned.sem, 1)
                        turned_copied.wait(pe, t, 1)
                        copied.wait_steps(pe, t - s)
                        settle(pe, o_.passed)
                        for k in range(CAP):
                            last = nc.tensor.matmul(y_ps[s][:, k * 128:(k + 1) * 128], hT[0:HD, s, k, :], wo[:, t, :],
                                                    start=True, stop=True)
                        last.then_inc(projected.sem, 1)
                    pairs(pe, body)

                @block.scalar
                def _(act):
                    def tiles(t, s):
                        turned.wait_steps(act, t if isinstance(t, int) else t - 1)
                        settle(act, o_.passed)
                        nc.scalar.activation(tile[:, s, :, 0:HD], av[:, t, :, :], ACT.Copy).then_inc(tile_ready.sem, 1)

                    def body(t, s):
                        turned.wait(act, t, 1)
                        projected.wait_steps(act, t - s)
                        settle(act, o_.passed)
                        nc.scalar.activation(hT[0:HD, s, :, :], t_ps[s][0:HD, 0:CAP * 128], ACT.Copy) \
                            .then_inc(turned_copied.sem, 1)
                    tiles(0, 0)
                    with act.Fori(0, E // 2 - 1) as it:
                        for s in range(2):
                            tiles(it * 2 + 1 + s, 1 - s)
                            body(it * 2 + s, s)
                    tiles(E - 1, 1)
                    body(E - 2, 0)
                    body(E - 1, 1)

                @block.vector
                def _(dve):
                    def body(t, s):
                        projected.wait(dve, t, 1)
                        settle(dve, o_.passed)
                        nc.vector.tensor_tensor(ao[:, t, :, :], y_ps[s][:, 0:CAP * 128].rearrange("p (k f) -> p k f", k=CAP),
                                                bo[:, :].unsqueeze(1).to_broadcast([128, CAP, 128]), ALU.add) \
                            .then_inc(copied.sem, 1)
                    pairs(dve, body)

        normalize(nc, c, "n1y", tok, 128, None, ["ln"], token_out=tok)
        with Scope(nc, "l1_res") as r_:
            part = [r_.semaphore(f"part{i}") for i in range(2)]
            r_.begin()

            def gain_and_add(eng, alu, sem, r):
                n = r.stop - r.start
                gain, shift = (gb[:, i, :].unsqueeze(1).to_broadcast([128, n, 128]) for i in range(2))
                for i, (out, in1, op) in enumerate(((tok, gain, ALU.mult), (tok, shift, ALU.add),
                                                    (c["x"], c["x"][:, r, :], ALU.add))):
                    if i:
                        eng.wait_ge(sem, i)
                    alu.tensor_tensor(out[:, r, :], tok[:, r, :], in1, op).then_inc(sem, 1)
            with nc.Block() as block:
                @block.vector
                def _(dve):
                    gain_and_add(dve, nc.vector, part[0], slice(0, 22))

                @block.gpsimd
                def _(pool):
                    gain_and_add(pool, nc.gpsimd, part[1], slice(22, B))


def program(nc, T, out):
    with ExitStack() as keep:
        def sb(name, shape, dt=F32):
            return keep.enter_context(nc.sbuf_tensor(name, shape, dt))
        c = dict(x=sb("x_tokens", [128, B, 128]), nT=sb("normed_t", [128, B * 128]),
                 ctx=sb("context", [SC, B, 128]), cT=sb("context_t", [128, B * (SC + 1)]),
                 ident=sb("ident", [128, 128]), ones=sb("ones", [128, 128]),
                 neg_half=sb("neg_half", [128, 8]), head_mask=sb("head_mask", [128, 4, 4]),
                 mask8=sb("mask8", [128, 4]))
        inputs_in = nc.alloc_semaphore("inputs_in")
        with nc.Block() as block:
            @block.sync
            def _(sp):
                sp.dma_start(c["x"][:, :, :], T["x"].rearrange("b s d -> s b d")).then_inc(inputs_in, 16)
                sp.dma_start(c["ctx"][:, :, :], T["ctx_1024"].rearrange("b s d -> s b d")).then_inc(inputs_in, 16)
                sp.wait_ge(inputs_in, 32)
        nc.clear_and_free_semaphores([inputs_in])
        nc.all_engine_barrier()
        make_consts(nc, c)
        def normed(name, kinds=("ln",)):
            return lambda b: normalize(nc, c, name, c["x"], 128, c["nT"], list(kinds), loads=b)

        def l0_cross_norms(loads):
            normalize(nc, c, "n0x", c["x"], 128, c["nT"], ["ln", "rms"], loads=loads)
            normalize(nc, c, "n0c", c["ctx"], SC, c["cT"], ["rms"])

        def l1_cross_norms(loads):
            with Scope(nc, "l1_norms") as sc:
                wb = sc.sb("scale_shift", [128, 4])
                b = loader(nc, sc, [(wb[:, i:i + 1], column(T["L1_xattn_" + n]))
                                    for i, n in enumerate(("ln1_w", "ln1_b", "ln2_w", "ln2_b"))])
                sc.begin()
                with nc.Block() as block:
                    @block.sync
                    def _(sp):
                        b["dma"](sp)
                        sp.wait_ge(b["loaded"], 16 * b["loads"])
                normalize(nc, c, "n1x", c["x"], 128, c["nT"], ["ln", "ln"], scale=wb[:, 2:3], shift=wb[:, 3:4],
                          loads=loads)
                normalize(nc, c, "n1c", c["ctx"], SC, c["cT"], ["ln"], scale=wb[:, 0:1], shift=wb[:, 1:2])

        def l2_cross_norms(loads):
            normalize(nc, c, "n2x", c["x"], 128, c["nT"], ["ln"], loads=loads)
            normalize(nc, c, "n2c", c["ctx"], SC, c["cT"], [])

        l0_attention(nc, c, T, normed("n0a"))
        l0_cross_attention(nc, c, T, l0_cross_norms)
        l0_ffn(nc, c, T, normed("n0f"))
        l1_attention(nc, c, T, normed("n1a"))
        l1_cross_attention(nc, c, T, l1_cross_norms)
        l1_ffn(nc, c, T)
        l2_attention(nc, c, T, normed("n2a"))
        l2_cross_attention(nc, c, T, l2_cross_norms)
        l2_ffn(nc, c, T, normed("n2f"))
        l3_attention(nc, c, T, normed("n3a"))
        l3_cross_attention(nc, c, T, normed("n3x"))
        l3_ffn(nc, c, T, normed("n3f"))
        stored = nc.alloc_semaphore("stored")
        nc.all_engine_barrier()
        with nc.Block() as block:
            @block.sync
            def _(sp):
                sp.dma_start(out.rearrange("b s d -> s b d"), c["x"][:, :, :]).then_inc(stored, 16)
                sp.wait_ge(stored, 16)


_T = ["L0_attn_qkv_w", "L0_attn_proj_w", "L1_attn_Wq", "L1_attn_Wk", "L1_attn_Wv",
      "L2_ffn_shared_gate", "L2_ffn_shared_up", "L2_ffn_shared_down", "L2_ffn_router_w", "L3_ffn_router_w",
      "L3_xattn_Wo", "L3_xattn_Wq", "L3_xattn_Wk", "L3_xattn_Wv"]


def kernel(**inputs):
    import numpy as np
    import concourse.bacc as bacc
    from concourse import mybir as mb
    from concourse.bass_utils import run_bass_kernel_spmd as run

    nc = bacc.Bacc("TRN2", target_bir_lowering=False, num_devices=1)
    arrays, T = {}, {}
    for name, a in inputs.items():
        if name == "L1_ffn_attn_mask":
            continue
        a = np.asarray(a)
        if name in _T:
            a = a.T
        a = np.ascontiguousarray(a)
        arrays["in_" + name] = a
        T[name] = nc.dram_tensor("in_" + name, a.shape, mb.dt.from_np(a.dtype), kind="ExternalInput").ap()
    half = np.arange(16, dtype=np.float32)
    timescale = np.float32(10000.0) ** (np.float32(2.0 / 32) * half)
    pos = np.concatenate([np.arange(77, 77 + 128), np.arange(77)]).astype(np.float32)
    rad = (pos[None, :] / timescale[:, None]).astype(np.float32)
    cos, sin = np.cos(rad), np.sin(rad)
    rope = np.stack([np.tile(np.concatenate([cos, cos]), (4, 1)), np.tile(np.concatenate([-sin, sin]), (4, 1))], 1)
    arrays["in_rope"] = np.ascontiguousarray(rope.astype(np.float32))
    T["rope"] = nc.dram_tensor("in_rope", arrays["in_rope"].shape, mb.dt.float32, kind="ExternalInput").ap()
    out = nc.dram_tensor("out_0", (B, S, D), mb.dt.float32, kind="ExternalOutput").ap()
    program(nc, T, out)
    r = run(nc, [arrays], core_ids=[0])
    return r.results[0]["out_0"]
```
